# Optimizing a Trainium2 kernel written in Bass

```python
import numpy as np
import jax
import jax.numpy as jnp

def _softmax(x, axis=-1):
    return jax.nn.softmax(x, axis=axis)

def _gelu(x):
    return jax.nn.gelu(x, approximate=True)

def _silu(x):
    return jax.nn.silu(x)

def _sigmoid(x):
    return jax.nn.sigmoid(x)

def _layernorm(x, axis=-1, eps=1e-05):
    m = jnp.mean(x, axis=axis, keepdims=True)
    v = jnp.var(x, axis=axis, keepdims=True)
    return (x - m) / jnp.sqrt(v + eps)

def _scatter_add(tgt, idx, src, axis=0):
    return tgt.at[idx].add(src)

def _segment_sum(src, seg, n):
    return jax.ops.segment_sum(src, seg, n)
kernel_name = 'mk_prb_d2_jaxref_r4_31fb0e'

def setup_inputs(seed: int=0):
    np.random.seed(seed)
    _w = jnp.asarray

    def _L0_attn_setup():
        import jax, jax.numpy as jnp
        import numpy as np
        import math
        D = 256
        CHUNK = 64
        B = 4
        S = 1024

        def _layernorm(x, g, b, eps=1e-05):
            mu = jnp.mean(x, axis=-1, keepdims=True)
            var = jnp.mean((x - mu) ** 2, axis=-1, keepdims=True)
            return (x - mu) * jax.lax.rsqrt(var + eps) * g + b
        key = jax.random.key(seed)
        ks = jax.random.split(key, 8)
        lin = lambda k: jax.random.normal(k, (D, D), jnp.float32) * 0.02
        return {'x': jax.random.normal(ks[0], (B, S, D), jnp.float32), 'Wk': lin(ks[1]), 'bk': jnp.zeros((D,), jnp.float32), 'Wv': lin(ks[2]), 'bv': jnp.zeros((D,), jnp.float32), 'Wq': lin(ks[3]), 'bq': jnp.zeros((D,), jnp.float32), 'Wkp': lin(ks[4]), 'bkp': jnp.zeros((D,), jnp.float32), 'Wqp': lin(ks[5]), 'bqp': jnp.zeros((D,), jnp.float32), 'phase_scale': jnp.ones((D,), jnp.float32) * math.pi, 'ln_g': jnp.ones((D,), jnp.float32), 'ln_b': jnp.zeros((D,), jnp.float32), 'Wo': lin(ks[6]), 'bo': jnp.zeros((D,), jnp.float32)}
    _L0_attn_in = _L0_attn_setup()

    def _L0_ffn_setup():
        import jax, jax.numpy as jnp
        import numpy as np
        B, T, C = (8, 512, 256)
        H = 1024
        E = 8
        K = 2
        LOAD_FACTOR = 1.2
        N_LAYER = 12

        def _get_expert_inputs(x, logits, expert_capacity):
            Tt = logits.shape[0]
            Cc = x.shape[1]
            top_k_logits, expert_indices = jax.lax.top_k(logits, K)
            expert_probs = jax.nn.softmax(top_k_logits, axis=-1)
            ei = jnp.swapaxes(expert_indices, 0, 1).ravel()
            one_hot = jax.nn.one_hot(ei, E, dtype=jnp.int32)
            pos = jnp.cumsum(one_hot, axis=0) * one_hot - 1
            pos = pos.reshape(-1, Tt, E)
            pos = jnp.swapaxes(pos, 0, 1)
            pos = jnp.max(pos, axis=2)
            ei = jnp.swapaxes(ei.reshape(-1, Tt), 0, 1)
            buf = jnp.zeros((E, expert_capacity, Cc), x.dtype)
            xr = jnp.repeat(x, K, axis=0)
            expert_inputs = buf.at[ei.ravel(), pos.ravel()].add(xr)
            return (expert_probs, pos, ei, expert_inputs)
        key = jax.random.key(seed)
        ks = jax.random.split(key, 9)
        std = 0.02
        proj_std = 0.02 * (2 * N_LAYER) ** (-0.5)
        return {'x': jax.random.normal(ks[0], (B, T, C), jnp.float32), 'router_w': jax.random.normal(ks[1], (C, E), jnp.float32) * std, 'router_b': jnp.zeros((E,), jnp.float32), 'w_c_fc': jax.random.normal(ks[2], (E, C, H), jnp.float32) * std, 'b_c_fc': jnp.zeros((E, 1, H), jnp.float32), 'w_gate': jax.random.normal(ks[3], (E, C, H), jnp.float32) * std, 'b_gate': jnp.zeros((E, 1, H), jnp.float32), 'w_c_proj': jax.random.normal(ks[4], (E, H, C), jnp.float32) * proj_std, 'b_c_proj': jnp.zeros((E, 1, C), jnp.float32)}
    _L0_ffn_in = _L0_ffn_setup()

    def _L1_attn_setup():
        import jax, jax.numpy as jnp
        import numpy as np
        D_MODEL = 256
        D_STATE = 64
        D_CONV = 4
        EXPAND = 2
        HEADDIM = 64
        D_INNER = EXPAND * D_MODEL
        NHEADS = D_INNER // HEADDIM
        CONV_DIM = D_INNER + 2 * D_STATE
        D_IN_PROJ = 2 * D_INNER + 2 * D_STATE + NHEADS
        BATCH, SEQLEN = (4, 512)
        DT_MIN, DT_MAX = (0.05, 1.0)
        EPS = 1e-05

        def _make_params(key, prefix):
            ks = jax.random.split(key, 5)
            p = {}
            p[prefix + 'in_w'] = jax.random.normal(ks[0], (D_IN_PROJ, D_MODEL), jnp.float32) * D_MODEL ** (-0.5)
            p[prefix + 'conv_w'] = jax.random.normal(ks[1], (CONV_DIM, D_CONV), jnp.float32) * D_CONV ** (-0.5)
            p[prefix + 'conv_b'] = jnp.zeros((CONV_DIM,), jnp.float32)
            u = jax.random.uniform(ks[2], (NHEADS,), jnp.float32)
            dt = jnp.exp(u * (np.log(DT_MAX) - np.log(DT_MIN)) + np.log(DT_MIN))
            p[prefix + 'dt_bias'] = dt + jnp.log(-jnp.expm1(-dt)) + 1.0
            p[prefix + 'A_log'] = jnp.log(jax.random.uniform(ks[3], (NHEADS,), jnp.float32, minval=1.0, maxval=16.0))
            p[prefix + 'Dp'] = jnp.ones((NHEADS,), jnp.float32)
            p[prefix + 'norm_w'] = jnp.ones((D_INNER,), jnp.float32)
            p[prefix + 'out_w'] = jax.random.normal(ks[4], (D_MODEL, D_INNER), jnp.float32) * D_INNER ** (-0.5)
            return p

        def _dconv(x, w, b):
            xt = x.transpose(0, 2, 1)
            out = jax.lax.conv_general_dilated(xt, w[:, None, :], (1,), [(D_CONV - 1, 0)], feature_group_count=CONV_DIM)
            return (out + b[:, None]).transpose(0, 2, 1)

        def _ssd(dt, A, xh, Bm, Cm):
            dA = jnp.exp(dt * A)

            def step(S, inp):
                dA_t, dt_t, x_t, B_t, C_t = inp
                S = S * dA_t[:, :, None, None] + (dt_t[:, :, None] * x_t)[..., None] * B_t[:, None, None, :]
                y = jnp.einsum('bhpn,bn->bhp', S, C_t)
                return (S, y)
            S0 = jnp.zeros((dt.shape[0], NHEADS, HEADDIM, D_STATE), dt.dtype)
            xs = (dA.swapaxes(0, 1), dt.swapaxes(0, 1), xh.swapaxes(0, 1), Bm.swapaxes(0, 1), Cm.swapaxes(0, 1))
            _, ys = jax.lax.scan(step, S0, xs)
            return ys.swapaxes(0, 1)

        def _mamba2(x, in_w, conv_w, conv_b, dt_bias, A_log, Dp, norm_w, out_w):
            Bsz, L, _ = x.shape
            zxbcdt = x @ in_w.T
            z = zxbcdt[..., :D_INNER]
            xBC = zxbcdt[..., D_INNER:D_INNER + CONV_DIM]
            dt = jax.nn.softplus(zxbcdt[..., D_INNER + CONV_DIM:] + dt_bias)
            xBC = jax.nn.silu(_dconv(xBC, conv_w, conv_b))
            xh = xBC[..., :D_INNER].reshape(Bsz, L, NHEADS, HEADDIM)
            Bm = xBC[..., D_INNER:D_INNER + D_STATE]
            Cm = xBC[..., D_INNER + D_STATE:]
            A = -jnp.exp(A_log)
            y = _ssd(dt, A, xh, Bm, Cm) + Dp[None, None, :, None] * xh
            y = y.reshape(Bsz, L, D_INNER) * jax.nn.silu(z)
            y = y * jax.lax.rsqrt(jnp.mean(y * y, -1, keepdims=True) + EPS) * norm_w
            return y @ out_w.T
        key = jax.random.key(seed)
        k1, k2, k3 = jax.random.split(key, 3)
        inp = {'x': jax.random.normal(k1, (BATCH, SEQLEN, D_MODEL), jnp.float32)}
        inp.update(_make_params(k2, 'f_'))
        inp.update(_make_params(k3, 'b_'))
        return inp
    _L1_attn_in = _L1_attn_setup()

    def _L1_ffn_setup():
        import math
        import jax, jax.numpy as jnp
        import numpy as np
        CAPACITY_FACTOR = 1.25
        key = jax.random.key(seed)
        ks = jax.random.split(key, 5)
        B, S, H, F, E = (4, 1024, 256, 256, 32)
        scale_in = 1.0 / math.sqrt(H)
        scale_mid = 1.0 / math.sqrt(F)
        return {'x': jax.random.normal(ks[0], (B, S, H), dtype=jnp.float32), 'w_router': jax.random.normal(ks[1], (H, E), dtype=jnp.float32) * scale_in, 'w_gate': jax.random.normal(ks[2], (E, H, F), dtype=jnp.float32) * scale_in, 'w_up': jax.random.normal(ks[3], (E, H, F), dtype=jnp.float32) * scale_in, 'w_down': jax.random.normal(ks[4], (E, F, H), dtype=jnp.float32) * scale_mid}
    _L1_ffn_in = _L1_ffn_setup()
    _d = {'L0_attn_x': _L0_attn_in['x'], 'L0_attn_Wk': _L0_attn_in['Wk'], 'L0_attn_bk': _L0_attn_in['bk'], 'L0_attn_Wv': _L0_attn_in['Wv'], 'L0_attn_bv': _L0_attn_in['bv'], 'L0_attn_Wq': _L0_attn_in['Wq'], 'L0_attn_bq': _L0_attn_in['bq'], 'L0_attn_Wkp': _L0_attn_in['Wkp'], 'L0_attn_bkp': _L0_attn_in['bkp'], 'L0_attn_Wqp': _L0_attn_in['Wqp'], 'L0_attn_bqp': _L0_attn_in['bqp'], 'L0_attn_phase_scale': _L0_attn_in['phase_scale'], 'L0_attn_ln_g': _L0_attn_in['ln_g'], 'L0_attn_ln_b': _L0_attn_in['ln_b'], 'L0_attn_Wo': _L0_attn_in['Wo'], 'L0_attn_bo': _L0_attn_in['bo'], 'L0_ffn_router_w': _L0_ffn_in['router_w'], 'L0_ffn_router_b': _L0_ffn_in['router_b'], 'L0_ffn_w_c_fc': _L0_ffn_in['w_c_fc'], 'L0_ffn_b_c_fc': _L0_ffn_in['b_c_fc'], 'L0_ffn_w_gate': _L0_ffn_in['w_gate'], 'L0_ffn_b_gate': _L0_ffn_in['b_gate'], 'L0_ffn_w_c_proj': _L0_ffn_in['w_c_proj'], 'L0_ffn_b_c_proj': _L0_ffn_in['b_c_proj'], 'L1_attn_f_in_w': _L1_attn_in['f_in_w'], 'L1_attn_f_conv_w': _L1_attn_in['f_conv_w'], 'L1_attn_f_conv_b': _L1_attn_in['f_conv_b'], 'L1_attn_f_dt_bias': _L1_attn_in['f_dt_bias'], 'L1_attn_f_A_log': _L1_attn_in['f_A_log'], 'L1_attn_f_Dp': _L1_attn_in['f_Dp'], 'L1_attn_f_norm_w': _L1_attn_in['f_norm_w'], 'L1_attn_f_out_w': _L1_attn_in['f_out_w'], 'L1_attn_b_in_w': _L1_attn_in['b_in_w'], 'L1_attn_b_conv_w': _L1_attn_in['b_conv_w'], 'L1_attn_b_conv_b': _L1_attn_in['b_conv_b'], 'L1_attn_b_dt_bias': _L1_attn_in['b_dt_bias'], 'L1_attn_b_A_log': _L1_attn_in['b_A_log'], 'L1_attn_b_Dp': _L1_attn_in['b_Dp'], 'L1_attn_b_norm_w': _L1_attn_in['b_norm_w'], 'L1_attn_b_out_w': _L1_attn_in['b_out_w'], 'L1_ffn_w_router': _L1_ffn_in['w_router'], 'L1_ffn_w_gate': _L1_ffn_in['w_gate'], 'L1_ffn_w_up': _L1_ffn_in['w_up'], 'L1_ffn_w_down': _L1_ffn_in['w_down']}
    _x0 = _d['L0_attn_x']
    _d['L0_attn_x'] = jax.random.normal(jax.random.fold_in(jax.random.key(seed), 1), (4, 2048, 256), dtype=_x0.dtype)
    del _x0
    return _d

def reference(L0_attn_x, L0_attn_Wk, L0_attn_bk, L0_attn_Wv, L0_attn_bv, L0_attn_Wq, L0_attn_bq, L0_attn_Wkp, L0_attn_bkp, L0_attn_Wqp, L0_attn_bqp, L0_attn_phase_scale, L0_attn_ln_g, L0_attn_ln_b, L0_attn_Wo, L0_attn_bo, L0_ffn_router_w, L0_ffn_router_b, L0_ffn_w_c_fc, L0_ffn_b_c_fc, L0_ffn_w_gate, L0_ffn_b_gate, L0_ffn_w_c_proj, L0_ffn_b_c_proj, L1_attn_f_in_w, L1_attn_f_conv_w, L1_attn_f_conv_b, L1_attn_f_dt_bias, L1_attn_f_A_log, L1_attn_f_Dp, L1_attn_f_norm_w, L1_attn_f_out_w, L1_attn_b_in_w, L1_attn_b_conv_w, L1_attn_b_conv_b, L1_attn_b_dt_bias, L1_attn_b_A_log, L1_attn_b_Dp, L1_attn_b_norm_w, L1_attn_b_out_w, L1_ffn_w_router, L1_ffn_w_gate, L1_ffn_w_up, L1_ffn_w_down):

    def _L0_attn_ref(x, Wk, bk, Wv, bv, Wq, bq, Wkp, bkp, Wqp, bqp, phase_scale, ln_g, ln_b, Wo, bo):
        import jax, jax.numpy as jnp
        import numpy as np
        import math
        D = 256
        CHUNK = 64
        B = 4
        S = 1024

        def _layernorm(x, g, b, eps=1e-05):
            mu = jnp.mean(x, axis=-1, keepdims=True)
            var = jnp.mean((x - mu) ** 2, axis=-1, keepdims=True)
            return (x - mu) * jax.lax.rsqrt(var + eps) * g + b
        batch, seq_len, dim = x.shape
        key = jnp.einsum('bsd,ed->bse', x, Wk) + bk
        value = jnp.einsum('bsd,ed->bse', x, Wv) + bv
        query = jnp.einsum('bsd,ed->bse', x, Wq) + bq
        key_phase = jnp.tanh(jnp.einsum('bsd,ed->bse', key, Wkp) + bkp) * phase_scale
        query_phase = jnp.tanh(jnp.einsum('bsd,ed->bse', query, Wqp) + bqp) * phase_scale
        bound_real = value * jnp.cos(key_phase)
        bound_imag = value * jnp.sin(key_phase)
        pad_len = -seq_len % CHUNK
        if pad_len > 0:
            pad = ((0, 0), (0, pad_len), (0, 0))
            bound_real = jnp.pad(bound_real, pad)
            bound_imag = jnp.pad(bound_imag, pad)
            query_phase = jnp.pad(query_phase, pad)
        padded_len = seq_len + pad_len
        nc = padded_len // CHUNK
        br = bound_real.reshape(batch, nc, CHUNK, dim)
        bi = bound_imag.reshape(batch, nc, CHUNK, dim)
        qp = query_phase.reshape(batch, nc, CHUNK, dim)
        mem_real = jnp.cumsum(br, axis=2)
        mem_imag = jnp.cumsum(bi, axis=2)
        retrieved = mem_real * jnp.cos(qp) + mem_imag * jnp.sin(qp)
        retrieved = retrieved.reshape(batch, padded_len, dim)[:, :seq_len]
        retrieved = retrieved / math.sqrt(dim)
        out = jnp.einsum('bsd,ed->bse', _layernorm(retrieved, ln_g, ln_b), Wo) + bo
        return x + out

    def _L0_ffn_ref(x, router_w, router_b, w_c_fc, b_c_fc, w_gate, b_gate, w_c_proj, b_c_proj):
        import jax, jax.numpy as jnp
        import numpy as np
        B, T, C = (8, 512, 256)
        H = 1024
        E = 8
        K = 2
        LOAD_FACTOR = 1.2
        N_LAYER = 12

        def _get_expert_inputs(x, logits, expert_capacity):
            Tt = logits.shape[0]
            Cc = x.shape[1]
            top_k_logits, expert_indices = jax.lax.top_k(logits, K)
            expert_probs = jax.nn.softmax(top_k_logits, axis=-1)
            ei = jnp.swapaxes(expert_indices, 0, 1).ravel()
            one_hot = jax.nn.one_hot(ei, E, dtype=jnp.int32)
            pos = jnp.cumsum(one_hot, axis=0) * one_hot - 1
            pos = pos.reshape(-1, Tt, E)
            pos = jnp.swapaxes(pos, 0, 1)
            pos = jnp.max(pos, axis=2)
            ei = jnp.swapaxes(ei.reshape(-1, Tt), 0, 1)
            buf = jnp.zeros((E, expert_capacity, Cc), x.dtype)
            xr = jnp.repeat(x, K, axis=0)
            expert_inputs = buf.at[ei.ravel(), pos.ravel()].add(xr)
            return (expert_probs, pos, ei, expert_inputs)
        Bb, Tt, Cc = x.shape
        logits = jnp.einsum('btc,ce->bte', x, router_w) + router_b
        cap = int(LOAD_FACTOR * K * Tt // E)
        probs, pos, idx, einp = jax.vmap(lambda xb, lb: _get_expert_inputs(xb, lb, cap))(x, logits)
        if Bb % E == 0:
            t = einp.reshape(E, Bb // E, E, cap, Cc)
            t = jnp.swapaxes(t, 0, 2)
        else:
            t = jnp.swapaxes(einp, 0, 1)
        einp2 = t.reshape(E, Bb * cap, Cc)
        h = jnp.einsum('eti,eih->eth', einp2, w_c_fc) + b_c_fc
        g = jnp.einsum('eti,eih->eth', einp2, w_gate) + b_gate
        o = jnp.einsum('eth,eho->eto', jax.nn.silu(h * g), w_c_proj) + b_c_proj
        if Bb % E == 0:
            o = o.reshape(E, Bb // E, E, cap, Cc)
            o = jnp.swapaxes(o, 0, 2)
            o = o.reshape(Bb, E, cap, Cc)
        else:
            o = o.reshape(E, Bb, cap, Cc)
            o = jnp.swapaxes(o, 0, 1)

        def collect(eo, i, p, pr):
            sel = eo[i, p]
            return jnp.sum(pr[..., None] * sel, axis=1)
        return jax.vmap(collect)(o, idx, pos, probs)

    def _L1_attn_ref(x, f_in_w, f_conv_w, f_conv_b, f_dt_bias, f_A_log, f_Dp, f_norm_w, f_out_w, b_in_w, b_conv_w, b_conv_b, b_dt_bias, b_A_log, b_Dp, b_norm_w, b_out_w):
        import jax, jax.numpy as jnp
        import numpy as np
        D_MODEL = 256
        D_STATE = 64
        D_CONV = 4
        EXPAND = 2
        HEADDIM = 64
        D_INNER = EXPAND * D_MODEL
        NHEADS = D_INNER // HEADDIM
        CONV_DIM = D_INNER + 2 * D_STATE
        D_IN_PROJ = 2 * D_INNER + 2 * D_STATE + NHEADS
        BATCH, SEQLEN = (4, 512)
        DT_MIN, DT_MAX = (0.05, 1.0)
        EPS = 1e-05

        def _make_params(key, prefix):
            ks = jax.random.split(key, 5)
            p = {}
            p[prefix + 'in_w'] = jax.random.normal(ks[0], (D_IN_PROJ, D_MODEL), jnp.float32) * D_MODEL ** (-0.5)
            p[prefix + 'conv_w'] = jax.random.normal(ks[1], (CONV_DIM, D_CONV), jnp.float32) * D_CONV ** (-0.5)
            p[prefix + 'conv_b'] = jnp.zeros((CONV_DIM,), jnp.float32)
            u = jax.random.uniform(ks[2], (NHEADS,), jnp.float32)
            dt = jnp.exp(u * (np.log(DT_MAX) - np.log(DT_MIN)) + np.log(DT_MIN))
            p[prefix + 'dt_bias'] = dt + jnp.log(-jnp.expm1(-dt)) + 1.0
            p[prefix + 'A_log'] = jnp.log(jax.random.uniform(ks[3], (NHEADS,), jnp.float32, minval=1.0, maxval=16.0))
            p[prefix + 'Dp'] = jnp.ones((NHEADS,), jnp.float32)
            p[prefix + 'norm_w'] = jnp.ones((D_INNER,), jnp.float32)
            p[prefix + 'out_w'] = jax.random.normal(ks[4], (D_MODEL, D_INNER), jnp.float32) * D_INNER ** (-0.5)
            return p

        def _dconv(x, w, b):
            xt = x.transpose(0, 2, 1)
            out = jax.lax.conv_general_dilated(xt, w[:, None, :], (1,), [(D_CONV - 1, 0)], feature_group_count=CONV_DIM)
            return (out + b[:, None]).transpose(0, 2, 1)

        def _ssd(dt, A, xh, Bm, Cm):
            dA = jnp.exp(dt * A)

            def step(S, inp):
                dA_t, dt_t, x_t, B_t, C_t = inp
                S = S * dA_t[:, :, None, None] + (dt_t[:, :, None] * x_t)[..., None] * B_t[:, None, None, :]
                y = jnp.einsum('bhpn,bn->bhp', S, C_t)
                return (S, y)
            S0 = jnp.zeros((dt.shape[0], NHEADS, HEADDIM, D_STATE), dt.dtype)
            xs = (dA.swapaxes(0, 1), dt.swapaxes(0, 1), xh.swapaxes(0, 1), Bm.swapaxes(0, 1), Cm.swapaxes(0, 1))
            _, ys = jax.lax.scan(step, S0, xs)
            return ys.swapaxes(0, 1)

        def _mamba2(x, in_w, conv_w, conv_b, dt_bias, A_log, Dp, norm_w, out_w):
            Bsz, L, _ = x.shape
            zxbcdt = x @ in_w.T
            z = zxbcdt[..., :D_INNER]
            xBC = zxbcdt[..., D_INNER:D_INNER + CONV_DIM]
            dt = jax.nn.softplus(zxbcdt[..., D_INNER + CONV_DIM:] + dt_bias)
            xBC = jax.nn.silu(_dconv(xBC, conv_w, conv_b))
            xh = xBC[..., :D_INNER].reshape(Bsz, L, NHEADS, HEADDIM)
            Bm = xBC[..., D_INNER:D_INNER + D_STATE]
            Cm = xBC[..., D_INNER + D_STATE:]
            A = -jnp.exp(A_log)
            y = _ssd(dt, A, xh, Bm, Cm) + Dp[None, None, :, None] * xh
            y = y.reshape(Bsz, L, D_INNER) * jax.nn.silu(z)
            y = y * jax.lax.rsqrt(jnp.mean(y * y, -1, keepdims=True) + EPS) * norm_w
            return y @ out_w.T
        out_fwd = _mamba2(x, f_in_w, f_conv_w, f_conv_b, f_dt_bias, f_A_log, f_Dp, f_norm_w, f_out_w)
        x_rev = jnp.flip(x, 1)
        out_bwd = _mamba2(x_rev, b_in_w, b_conv_w, b_conv_b, b_dt_bias, b_A_log, b_Dp, b_norm_w, b_out_w)
        return out_fwd + jnp.flip(out_bwd, 1)

    def _L1_ffn_ref(x, w_router, w_gate, w_up, w_down):
        import math
        import jax, jax.numpy as jnp
        import numpy as np
        CAPACITY_FACTOR = 1.25
        B, S, H = x.shape
        E = w_gate.shape[0]
        T = B * S
        C = int(math.ceil(CAPACITY_FACTOR * T / E))
        xt = x.reshape(T, H)
        logits = xt @ w_router
        probs = jax.nn.softmax(logits, axis=-1)
        top1 = jnp.argmax(probs, axis=-1)
        gate = jnp.take_along_axis(probs, top1[:, None], axis=1)[:, 0]
        onehot = jax.nn.one_hot(top1, E, dtype=jnp.int32)
        pos = jnp.cumsum(onehot, axis=0)[jnp.arange(T), top1] - 1
        accepted = pos < C
        slot = jnp.where(accepted, top1 * C + pos, E * C)
        buf = jnp.zeros((E * C + 1, H), dtype=x.dtype).at[slot].set(xt)
        buf = buf[:E * C].reshape(E, C, H)
        g = jnp.einsum('ech,ehf->ecf', buf, w_gate)
        u = jnp.einsum('ech,ehf->ecf', buf, w_up)
        y = jnp.einsum('ecf,efh->ech', jax.nn.silu(g) * u, w_down)
        out_tok = y.reshape(E * C, H)[jnp.clip(slot, 0, E * C - 1)]
        out_tok = jnp.where(accepted[:, None], out_tok * gate[:, None], 0.0)
        return (xt + out_tok).reshape(B, S, H)
    x = L0_attn_x
    xn = _layernorm(x, axis=-1)
    x = x + _L0_attn_ref(xn, L0_attn_Wk, L0_attn_bk, L0_attn_Wv, L0_attn_bv, L0_attn_Wq, L0_attn_bq, L0_attn_Wkp, L0_attn_bkp, L0_attn_Wqp, L0_attn_bqp, L0_attn_phase_scale, L0_attn_ln_g, L0_attn_ln_b, L0_attn_Wo, L0_attn_bo) + _L0_ffn_ref(xn, L0_ffn_router_w, L0_ffn_router_b, L0_ffn_w_c_fc, L0_ffn_b_c_fc, L0_ffn_w_gate, L0_ffn_b_gate, L0_ffn_w_c_proj, L0_ffn_b_c_proj)
    xn = _layernorm(x, axis=-1)
    x = x + _L1_attn_ref(xn, L1_attn_f_in_w, L1_attn_f_conv_w, L1_attn_f_conv_b, L1_attn_f_dt_bias, L1_attn_f_A_log, L1_attn_f_Dp, L1_attn_f_norm_w, L1_attn_f_out_w, L1_attn_b_in_w, L1_attn_b_conv_w, L1_attn_b_conv_b, L1_attn_b_dt_bias, L1_attn_b_A_log, L1_attn_b_Dp, L1_attn_b_norm_w, L1_attn_b_out_w) + _L1_ffn_ref(xn, L1_ffn_w_router, L1_ffn_w_gate, L1_ffn_w_up, L1_ffn_w_down)
    return x

_drawn_inputs = setup_inputs


def setup_inputs(seed=0):
    import zlib

    import numpy as np

    out = dict(_drawn_inputs(seed))
    spreads = {'L0_attn_bk': (0.0, 0.665),
     'L0_attn_bv': (0.0, 0.1),
     'L0_attn_bq': (0.0, 0.667),
     'L0_attn_bkp': (0.0, 0.1),
     'L0_attn_bqp': (0.0, 0.1),
     'L0_attn_phase_scale': (3.1415927410125732, 0.6),
     'L0_attn_ln_g': (1.0, 0.6),
     'L0_attn_ln_b': (0.0, 0.387),
     'L0_attn_bo': (0.0, 0.325),
     'L0_ffn_router_b': (0.0, 0.394),
     'L0_ffn_b_c_fc': (0.0, 0.8),
     'L0_ffn_b_gate': (0.0, 0.8),
     'L0_ffn_b_c_proj': (0.0, 0.433),
     'L1_attn_f_conv_b': (0.0, 1.069),
     'L1_attn_f_Dp': (1.0, 0.6),
     'L1_attn_f_norm_w': (1.0, 0.6),
     'L1_attn_b_conv_b': (0.0, 0.8),
     'L1_attn_b_Dp': (1.0, 0.6),
     'L1_attn_b_norm_w': (1.0, 0.6)}
    factors = {'L0_ffn_w_c_fc': 8.0,
     'L0_ffn_w_gate': 8.0,
     'L0_ffn_w_c_proj': 8.0,
     'L0_attn_Wk': 2.984,
     'L1_ffn_w_router': 3.518,
     'L1_ffn_w_gate': 3.743,
     'L1_ffn_w_up': 3.535,
     'L1_ffn_w_down': 3.507,
     'L1_attn_f_dt_bias': 2.827,
     'L1_attn_f_A_log': 8.0,
     'L1_attn_b_dt_bias': 3.407,
     'L1_attn_b_A_log': 8.0}
    for name, (base, spread) in spreads.items():
        noise = np.random.default_rng([zlib.crc32(name.encode()), seed]).standard_normal(out[name].shape)
        drawn = base * np.exp(spread * noise) if base else spread * noise
        out[name] = jnp.asarray(drawn.astype(out[name].dtype))
    for name, factor in factors.items():
        out[name] = (out[name] * factor).astype(out[name].dtype)
    return out
```

```python
import concourse.bass as bass
from concourse import mybir
from contextlib import ExitStack

F32 = mybir.dt.float32
F32R = mybir.dt.float32r
U32 = mybir.dt.uint32
ALU = mybir.AluOpType
ACT = mybir.ActivationFunctionType
AX = mybir.AxisListType.X


class Item:

    def __init__(self, c, r=None, unroll=2):
        self.g = c if r is None else r * unroll + c
        self.s = c % 2
        self.q = c // 2 if r is None else r * (unroll // 2) + c // 2
        self.lane = c % unroll
        self.turn = c // unroll if r is None else r + c // unroll
        self.again = r is not None or c >= 2


class Carrier:

    sem = None

    @classmethod
    def carry(cls, eng):
        eng.sem_inc(cls.sem, 1)


def pipelined(eng, stages, items, unroll=2):
    depth = len(stages)
    head = depth + 1
    rounds = (items - head) // unroll

    def step(base, r):
        for k in reversed(range(depth)):
            c = base - k
            if r is not None or 0 <= c < items:
                stages[k](Item(c, r, unroll))

    for t in range(head):
        step(t, None)
    with eng.Fori(0, rounds) as r:
        for u in range(unroll):
            step(head + u, r)
    for t in range(head + unroll * rounds, items + depth - 1):
        step(t, None)


class Steps:

    AHEAD = 4

    def __init__(self, sem, per):
        self.sem, self.per = sem, per
        self.credit = self.AHEAD * per + 1

    def open(self, eng):
        eng.sem_inc(self.sem, self.credit)

    def at(self, g, k=None):
        return g * self.per + ((self.per if k is None else k) + self.credit)


def at_row(eng, it, rows):
    return it.g * rows if isinstance(it.g, int) else eng.snap(it.g * rows)


import math

T, D, P = 8192, 256, 128
NT = T // P
KD = D // P
INV_2PI = 1.0 / (2.0 * math.pi)
ROUND = 1.5 * 2.0 ** 23
TWO_PI_HI = 6.28125
TWO_PI_LO = 2.0 * math.pi - TWO_PI_HI
PI_BELOW = 3.1415925
HALF_PI = math.pi / 2
CHUNK = 64
EPS = 1e-5

PARTS = ((0, 0), (0, 1), (1, 0))


def setup_l0(nc, env, ctx, attn_w, router_w, cols0, bo_rows, rb_rows):
    sb, sem = lambda n, s, d=F32: ctx.enter_context(nc.sbuf_tensor(n, s, d)), env.sem
    env.half_pi = sb("half_pi", [P, 1])
    env.cols = sb("cols", [P, 8, KD])
    env.bo_rows = sb("bo_rows", [P, D])
    env.rb_rows = sb("rb_rows", [P, 8])
    env.seg = sb("seg", [P, D])
    env.wraw = sb("wraw", [P, 6, KD, D])
    env.w = [sb("w_hi", [P, 6, KD, D], F32R), sb("w_lo", [P, 6, KD, D], F32R)]
    env.rwraw = sb("rwraw", [P, KD, 8])
    env.rw = [sb("rw_hi", [P, KD, 8], F32R), sb("rw_lo", [P, KD, 8], F32R)]
    loaded, pool_done, dve_done = sem("const_loaded"), sem("const_pool"), sem("const_dve")
    with nc.Block() as block:
        @block.sync
        def _(sp):
            sp.dma_start(env.wraw[:], attn_w.rearrange("w (k p) e -> p w k e", p=P)).then_inc(loaded, 16)
            sp.dma_start(env.rwraw[:], router_w.rearrange("(k p) e -> p k e", p=P)).then_inc(loaded, 16)
            sp.dma_start(env.cols[:], cols0.rearrange("p (v k) -> p v k", k=KD)).then_inc(loaded, 16)
            sp.dma_start(env.bo_rows[:], bo_rows).then_inc(loaded, 16)
            sp.dma_start(env.rb_rows[:], rb_rows).then_inc(loaded, 16)

        @block.gpsimd
        def _(pool):
            nc.gpsimd.memset(env.ident[:], 0.0).then_inc(pool_done, 1)
            pool.wait_ge(pool_done, 1)
            nc.gpsimd.affine_select(out=env.ident[:], in_=env.ident[:], compare_op=ALU.not_equal, fill=1.0,
                                    base=0, pattern=[[-1, P]], channel_multiplier=1).then_inc(pool_done, 1)

        @block.vector
        def _(dve):
            nc.vector.memset(env.neg_half[:], -0.5)
            nc.vector.memset(env.seg[:], 1.0).then_inc(dve_done, 1)
            nc.vector.memset(env.half_pi[:], HALF_PI)
            dve.wait_ge(dve_done, 1)
            nc.vector.memset(env.seg[:].rearrange("p (c t) -> p c t", t=CHUNK)[:, :, 0:1], 0.0).then_inc(dve_done, 1)
            dve.wait_ge(loaded, 80)
            nc.vector.tensor_copy(env.w[0][:], env.wraw[:]).then_inc(dve_done, 1)
            nc.vector.tensor_copy(env.rw[0][:], env.rwraw[:]).then_inc(dve_done, 1)
            nc.vector.tensor_scalar(env.cols[:, 2, :], env.cols[:, 2, :], 1.0 / math.sqrt(D), None, ALU.mult).then_inc(dve_done, 1)
            dve.wait_ge(dve_done, 5)
            nc.vector.tensor_tensor(env.w[1][:], env.wraw[:], env.w[0][:].bitcast(F32), ALU.subtract).then_inc(dve_done, 1)
            nc.vector.tensor_tensor(env.rw[1][:], env.rwraw[:], env.rw[0][:].bitcast(F32), ALU.subtract).then_inc(dve_done, 1)
            dve.wait_ge(dve_done, 7)


BK, BQ, BV, BKP, BQP, PSC, LNG, LNB = range(8)
WK, WQ, WV, WKP, WQP, WO = range(6)


def tokens_l0(nc, env, x, xn0, res0):
    G = 2 * P
    ITEMS = T // G
    with ExitStack() as ctx:
        sb = lambda n, s, d=F32: ctx.enter_context(nc.sbuf_tensor(n, s, d))
        ps = lambda n, s, d=F32: ctx.enter_context(nc.psum_tensor(n, s, d))
        sem = env.sem
        two = lambda n, s, d=F32: [sb(f"{n}{i}", s, d) for i in range(2)]
        x_in = two("x_in", [P, 2, D])
        stats = sb("stats", [P, 2, 6]); mv = sb("mv", [P, 2, 2]); var = sb("var", [P, 2]); rstd = sb("rstd", [P, 2])
        xn = two("xn", [P, 2, D])
        res = two("res", [P, 2, D]); res_t = sb("res_t", [P, 2, D])
        xt = [two("xt_hi", [P, KD, G], F32R), two("xt_lo", [P, KD, G], F32R)]
        kq = [two("kq_hi", [P, 4, G], F32R), two("kq_lo", [P, 4, G], F32R)]
        val = two("val", [P, KD, G])
        ph = sb("ph", [P, 4, G]); turns = sb("turns", [P, 4, G]); ang = sb("ang", [P, 4, G])
        sin = two("sin", [P, 4, G]); cos = two("cos", [P, 4, G])
        bound = sb("bound", [P, 4, G]); mem = sb("mem", [P, 4, G]); ret = two("ret", [P, KD, G])
        prod = sb("prod", [P, 4, G])
        stats2 = sb("stats2", [P, 2, 6]); mv2 = sb("mv2", [P, 2, 2]); var2 = sb("var2", [P, 2]); rstd2 = sb("rstd2", [P, 2])
        zt = two("zt", [P, 2, D])
        zf = sb("zf", [P, KD, G])
        z = [two("z_hi", [P, KD, G], F32R), two("z_lo", [P, KD, G], F32R)]
        res_in = two("res_in", [P, 2, D]); res_out = two("res_out", [P, 2, D])
        pT = ps("pT", [P, KD, G]); pK = ps("pK", [P, KD, G]); pQ = ps("pQ", [P, KD, G]); pC = ps("pC", [P, KD, G])
        pE = ps("pE", [P, 2, D]); pF = ps("pF", [P, KD, G]); pG = ps("pG", [P, 2, D]); pL = ps("pL", [P, 2, 8])

        x_loaded = [sem(f"x_loaded{i}") for i in range(2)]
        r_loaded = [sem(f"r_loaded{i}") for i in range(2)]
        xn_stored, res_stored, out_stored = ([sem(f"{n}{i}") for i in range(2)] for n in ("xn_stored", "res_stored", "out_stored"))
        norm = Steps(sem("norm_dve"), 8)
        norm_pool = Steps(sem("norm_pool"), 3)
        turned = Steps(sem("x_turned"), 1)
        high = Steps(sem("x_high"), 1)
        projected = Steps(sem("projected"), 4)
        proj_act = Steps(sem("proj_act"), 3)
        proj_dve = Steps(sem("proj_dve"), 3)
        phased = Steps(sem("phase_pe"), 2)
        ph_act = Steps(sem("phase_act"), 5)
        ph_dve = Steps(sem("phase_dve"), 10)
        bound_p = Steps(sem("bound_pool"), 2)
        mem_dve = Steps(sem("memory_dve"), 7)
        back = Steps(sem("ret_turned"), 1)
        ln_dve = Steps(sem("ln_dve"), 7)
        ln_pool = Steps(sem("ln_pool"), 1)
        z_turned = Steps(sem("z_turned"), 1)
        z_act = Steps(sem("z_act"), 1)
        z_dve = Steps(sem("z_dve"), 1)
        z_pool = Steps(sem("z_pool"), 1)
        out_pe = Steps(sem("out_pe"), 1)
        out_dve = Steps(sem("out_dve"), 1)

        def rows(ap, row):
            return ap[bass.ds(row, G), :].rearrange("(t p) d -> p t d", p=P)

        with nc.Block() as block:
            @block.sync
            def _(sp):
                def load(it):
                    row = at_row(sp, it, G)
                    sp.wait_ge(norm.sem, norm.at(it.g - 2, 7))
                    Carrier.carry(sp)
                    sp.wait_ge(norm_pool.sem, norm_pool.at(it.g - 2, 2))
                    Carrier.carry(sp)
                    sp.dma_start(x_in[it.s][:], rows(x, row)).then_inc(x_loaded[it.s], 16)

                def store(it):
                    row = at_row(sp, it, G)
                    sp.wait_ge(norm.sem, norm.at(it.g, 7))
                    Carrier.carry(sp)
                    sp.dma_start(rows(xn0, row), xn[it.s][:]).then_inc(xn_stored[it.s], 16)
                    sp.wait_ge(norm_pool.sem, norm_pool.at(it.g, 3))
                    Carrier.carry(sp)
                    sp.dma_start(rows(res0, row), res[it.s][:]).then_inc(res_stored[it.s], 16)

                def reload(it):
                    row = at_row(sp, it, G)
                    sp.wait_ge(out_dve.sem, out_dve.at(it.g - 2))
                    Carrier.carry(sp)
                    sp.wait_ge(res_stored[it.s], 16 * it.q + 16)
                    Carrier.carry(sp)
                    sp.dma_start(res_in[it.s][:], rows(res0, row)).then_inc(r_loaded[it.s], 16)

                def finish(it):
                    row = at_row(sp, it, G)
                    sp.wait_ge(out_dve.sem, out_dve.at(it.g))
                    Carrier.carry(sp)
                    sp.dma_start(rows(res0, row), res_out[it.s][:]).then_inc(out_stored[it.s], 16)

                nop = lambda it: None
                pipelined(sp, [load, store, nop, nop, nop, reload, finish], ITEMS)
                for s in range(2):
                    sp.wait_ge(xn_stored[s], 16 * ITEMS // 2)
                    sp.wait_ge(out_stored[s], 16 * ITEMS // 2)

            @block.vector
            def _(dve):
                v = nc.vector

                def normalise(it):
                    dve.wait_ge(x_loaded[it.s], 16 * it.q + 16)
                    dve.wait_ge(norm_pool.sem, norm_pool.at(it.g - 1, 1))
                    for t in range(2):
                        v.bn_stats(stats[:, t, :], x_in[it.s][:, t, :]).then_inc(norm.sem, 1)
                    dve.wait_ge(norm.sem, norm.at(it.g, 2))
                    Carrier.carry(dve)
                    for t in range(2):
                        v.bn_aggr(mv[:, t, :], stats[:, t, :]).then_inc(norm.sem, 1)
                    dve.wait_ge(norm.sem, norm.at(it.g, 4))
                    v.tensor_scalar(var[:], mv[:, :, 1], EPS, None, ALU.add).then_inc(norm.sem, 1)
                    dve.wait_ge(norm_pool.sem, norm_pool.at(it.g, 1))
                    if it.again:
                        dve.wait_ge(xn_stored[it.s], 16 * it.q)
                    dve.wait_ge(turned.sem, turned.at(it.g - 2))
                    dve.wait_ge(norm_pool.sem, norm_pool.at(it.g - 2))
                    for t in range(2):
                        v.tensor_scalar(xn[it.s][:, t, :], x_in[it.s][:, t, :], mv[:, t, 0:1], rstd[:, t:t + 1],
                                                  ALU.subtract, ALU.mult).then_inc(norm.sem, 1)
                    dve.wait_ge(high.sem, high.at(it.g))
                    dve.wait_ge(projected.sem, projected.at(it.g - 2))
                    v.tensor_tensor(xt[1][it.s][:], pT[:], xt[0][it.s][:].bitcast(F32), ALU.subtract).then_inc(norm.sem, 1)

                def project(it):
                    for n, (bank, bias) in enumerate(((pK, BK), (pQ, BQ))):
                        dve.wait_ge(proj_act.sem, proj_act.at(it.g, n + 1))
                        dve.wait_ge(phased.sem, phased.at(it.g - 2))
                        for c in range(KD):
                            i = v.scalar_tensor_tensor(out=kq[1][it.s][:, 2 * n + c, :], in0=bank[:, c, :],
                                                       scalar=env.cols[:, bias, c:c + 1],
                                                       in1=kq[0][it.s][:, 2 * n + c, :].bitcast(F32), op0=ALU.add, op1=ALU.subtract)
                        i.then_inc(proj_dve.sem, 1)
                    dve.wait_ge(projected.sem, projected.at(it.g, 3))
                    for t in range(2):
                        i = v.tensor_tensor(env.logits[:, bass.ds(it.g * 2 + t, 1), :] if not isinstance(it.g, int) else
                                            env.logits[:, it.g * 2 + t:it.g * 2 + t + 1, :],
                                            pL[:, t:t + 1, :], env.rb_rows[:].rearrange("p (o e) -> p o e", o=1), ALU.add)
                    i.then_inc(proj_dve.sem, 1)

                def phase(it):
                    for n in range(2):
                        dve.wait_ge(ph_act.sem, ph_act.at(it.g, n + 1))
                        for c in range(KD):
                            v.tensor_scalar(ph[:, 2 * n + c, :], ph[:, 2 * n + c, :], env.cols[:, PSC, c:c + 1], None, ALU.mult).then_inc(ph_dve.sem, 1)
                    dve.wait_ge(ph_dve.sem, ph_dve.at(it.g, 4))
                    v.tensor_scalar(turns[:], ph[:], INV_2PI, ROUND, ALU.mult, ALU.add).then_inc(ph_dve.sem, 1)
                    dve.wait_ge(ph_dve.sem, ph_dve.at(it.g, 5))
                    v.tensor_scalar(turns[:], turns[:], ROUND, None, ALU.subtract).then_inc(ph_dve.sem, 1)
                    dve.wait_ge(ph_dve.sem, ph_dve.at(it.g, 6))
                    v.scalar_tensor_tensor(out=ph[:], in0=turns[:], scalar=-TWO_PI_HI, in1=ph[:], op0=ALU.mult, op1=ALU.add).then_inc(ph_dve.sem, 1)
                    dve.wait_ge(ph_dve.sem, ph_dve.at(it.g, 7))
                    dve.wait_ge(ph_act.sem, ph_act.at(it.g - 1))
                    v.scalar_tensor_tensor(out=ph[:], in0=turns[:], scalar=-TWO_PI_LO, in1=ph[:], op0=ALU.mult, op1=ALU.add).then_inc(ph_dve.sem, 1)
                    dve.wait_ge(ph_dve.sem, ph_dve.at(it.g, 8))
                    v.tensor_scalar(ang[:], ph[:], PI_BELOW, -PI_BELOW, ALU.min, ALU.max).then_inc(ph_dve.sem, 1)
                    dve.wait_ge(ph_act.sem, ph_act.at(it.g, 3))
                    v.tensor_scalar(turns[:], turns[:], PI_BELOW, None, ALU.min).then_inc(ph_dve.sem, 1)

                def memory(it):
                    for n in range(2):
                        dve.wait_ge(bound_p.sem, bound_p.at(it.g, n + 1))
                        for c in range(KD):
                            v.tensor_tensor_scan(mem[:, 2 * n + c, :], env.seg[:], bound[:, 2 * n + c, :], 0.0, ALU.mult, ALU.add).then_inc(mem_dve.sem, 1)
                    dve.wait_ge(mem_dve.sem, mem_dve.at(it.g, 4))
                    v.tensor_tensor(prod[:, 0:2, :], mem[:, 0:2, :], cos[it.s][:, 2:4, :], ALU.mult).then_inc(mem_dve.sem, 1)
                    v.tensor_tensor(prod[:, 2:4, :], mem[:, 2:4, :], sin[it.s][:, 2:4, :], ALU.mult).then_inc(mem_dve.sem, 1)
                    dve.wait_ge(mem_dve.sem, mem_dve.at(it.g, 6))
                    dve.wait_ge(back.sem, back.at(it.g - 2))
                    v.tensor_tensor(ret[it.s][:], prod[:, 0:2, :], prod[:, 2:4, :], ALU.add).then_inc(mem_dve.sem, 1)

                def normalise_ret(it):
                    dve.wait_ge(back.sem, back.at(it.g))
                    for t in range(2):
                        v.bn_stats(stats2[:, t, :], pE[:, t, :]).then_inc(ln_dve.sem, 1)
                    dve.wait_ge(ln_dve.sem, ln_dve.at(it.g, 2))
                    Carrier.carry(dve)
                    for t in range(2):
                        v.bn_aggr(mv2[:, t, :], stats2[:, t, :]).then_inc(ln_dve.sem, 1)
                    dve.wait_ge(ln_dve.sem, ln_dve.at(it.g, 4))
                    v.tensor_scalar(var2[:], mv2[:, :, 1], EPS, None, ALU.add).then_inc(ln_dve.sem, 1)
                    dve.wait_ge(ln_pool.sem, ln_pool.at(it.g))
                    dve.wait_ge(z_turned.sem, z_turned.at(it.g - 2))
                    for t in range(2):
                        v.tensor_scalar(zt[it.s][:, t, :], pE[:, t, :], mv2[:, t, 0:1], rstd2[:, t:t + 1],
                                                    ALU.subtract, ALU.mult).then_inc(ln_dve.sem, 1)

                def z_high(it):
                    dve.wait_ge(z_act.sem, z_act.at(it.g))
                    dve.wait_ge(out_pe.sem, out_pe.at(it.g - 2))
                    v.tensor_copy(z[0][it.s][:], zf[:]).then_inc(z_dve.sem, 1)

                def add_out(it):
                    dve.wait_ge(out_pe.sem, out_pe.at(it.g))
                    dve.wait_ge(r_loaded[it.s], 16 * it.q + 16)
                    if it.again:
                        dve.wait_ge(out_stored[it.s], 16 * it.q)
                    v.tensor_tensor(res_out[it.s][:], pG[:], res_in[it.s][:], ALU.add).then_inc(out_dve.sem, 1)

                for stage in (norm, proj_dve, ph_dve, mem_dve, ln_dve, z_dve, out_dve):
                    stage.open(dve)
                pipelined(dve, [normalise, project, phase, memory, normalise_ret, z_high, add_out], ITEMS)

            @block.gpsimd
            def _(pool):
                p = nc.gpsimd

                def rstd_res(it):
                    pool.wait_ge(norm.sem, norm.at(it.g, 5))
                    p.tensor_tensor(rstd[:], var[:], env.neg_half[:, 0:2], ALU.pow).then_inc(norm_pool.sem, 1)
                    for t in range(2):
                        i = p.tensor_tensor(res_t[:, t, :], x_in[it.s][:, t, :], env.bo_rows[:], ALU.add)
                    i.then_inc(norm_pool.sem, 1)
                    pool.wait_ge(norm_pool.sem, norm_pool.at(it.g, 2))
                    pool.wait_ge(norm.sem, norm.at(it.g, 7))
                    if it.again:
                        pool.wait_ge(res_stored[it.s], 16 * it.q)
                    p.tensor_tensor(res[it.s][:], res_t[:], xn[it.s][:], ALU.add).then_inc(norm_pool.sem, 1)

                def bind(it):
                    pool.wait_ge(ph_act.sem, ph_act.at(it.g))
                    pool.wait_ge(mem_dve.sem, mem_dve.at(it.g - 1))
                    p.tensor_tensor(bound[:, 0:2, :], val[it.s][:], cos[it.s][:, 0:2, :], ALU.mult).then_inc(bound_p.sem, 1)
                    p.tensor_tensor(bound[:, 2:4, :], val[it.s][:], sin[it.s][:, 0:2, :], ALU.mult).then_inc(bound_p.sem, 1)

                def rstd_ret(it):
                    pool.wait_ge(ln_dve.sem, ln_dve.at(it.g, 5))
                    p.tensor_tensor(rstd2[:], var2[:], env.neg_half[:, 0:2], ALU.pow).then_inc(ln_pool.sem, 1)

                def z_low(it):
                    pool.wait_ge(z_dve.sem, z_dve.at(it.g))
                    p.tensor_tensor(z[1][it.s][:], zf[:], z[0][it.s][:].bitcast(F32), ALU.subtract).then_inc(z_pool.sem, 1)

                nop = lambda it: None
                for stage in (norm_pool, bound_p, ln_pool, z_pool):
                    stage.open(pool)
                pipelined(pool, [rstd_res, nop, nop, bind, rstd_ret, z_low, nop], ITEMS)

            @block.scalar
            def _(act):
                a = nc.scalar

                def x_high(it):
                    act.wait_ge(turned.sem, turned.at(it.g))
                    act.wait_ge(projected.sem, projected.at(it.g - 2))
                    a.activation(xt[0][it.s][:], pT[:], ACT.Copy).then_inc(high.sem, 1)

                def project(it):
                    for n, (bank, bias) in enumerate(((pK, BK), (pQ, BQ))):
                        act.wait_ge(projected.sem, projected.at(it.g, n + 1))
                        act.wait_ge(phased.sem, phased.at(it.g - 2))
                        for c in range(KD):
                            i = a.activation(kq[0][it.s][:, 2 * n + c, :], bank[:, c, :], ACT.Identity, bias=env.cols[:, bias, c:c + 1])
                        i.then_inc(proj_act.sem, 1)
                    act.wait_ge(projected.sem, projected.at(it.g, 4))
                    act.wait_ge(bound_p.sem, bound_p.at(it.g - 2))
                    for c in range(KD):
                        i = a.activation(val[it.s][:, c, :], pK[:, c, :], ACT.Identity, bias=env.cols[:, BV, c:c + 1],
                                         scale=1.0 / math.sqrt(D))
                    i.then_inc(proj_act.sem, 1)

                def phase(it):
                    for n, bias in enumerate((BKP, BQP)):
                        act.wait_ge(phased.sem, phased.at(it.g, n + 1))
                        act.wait_ge(ph_dve.sem, ph_dve.at(it.g - 1))
                        for c in range(KD):
                            i = a.activation(ph[:, 2 * n + c, :], pC[:, c, :], ACT.Tanh, bias=env.cols[:, bias, c:c + 1])
                        i.then_inc(ph_act.sem, 1)
                    act.wait_ge(ph_dve.sem, ph_dve.at(it.g, 9))
                    act.wait_ge(mem_dve.sem, mem_dve.at(it.g - 2))
                    act.wait_ge(bound_p.sem, bound_p.at(it.g - 2))
                    a.activation(turns[:], ang[:], ACT.Abs).then_inc(ph_act.sem, 1)
                    a.activation(sin[it.s][:], ang[:], ACT.Sin).then_inc(ph_act.sem, 1)
                    act.wait_ge(ph_dve.sem, ph_dve.at(it.g, 10))
                    a.activation(cos[it.s][:], turns[:], ACT.Sin, bias=env.half_pi[:, 0:1], scale=-1.0).then_inc(ph_act.sem, 1)

                def affine(it):
                    act.wait_ge(z_turned.sem, z_turned.at(it.g))
                    act.wait_ge(z_pool.sem, z_pool.at(it.g - 1))
                    for c in range(KD):
                        i = a.activation(zf[:, c, :], pF[:, c, :], ACT.Identity, bias=env.cols[:, LNB, c:c + 1], scale=env.cols[:, LNG, c:c + 1])
                    i.then_inc(z_act.sem, 1)

                nop = lambda it: None
                for stage in (high, proj_act, ph_act, z_act):
                    stage.open(act)
                pipelined(act, [x_high, project, phase, nop, nop, affine, nop], ITEMS)

            @block.tensor
            def _(pe):
                t_ = nc.tensor

                def product(out, weights, w_cols, acts, a_slot, a_rows):
                    n = 0
                    for k in range(KD):
                        for i, j in PARTS:
                            last = t_.matmul(out, weights[i][:, w_cols[0], k, w_cols[1]], acts[j][a_slot][:, a_rows + k, :],
                                             start=(n == 0), stop=(n == 3 * KD - 1))
                            n += 1
                    return last

                def turn_x(it):
                    pe.wait_ge(norm.sem, norm.at(it.g, 7))
                    pe.wait_ge(norm.sem, norm.at(it.g - 1))
                    for t in range(2):
                        for k in range(KD):
                            i = t_.transpose(pT[:, k, t * P:(t + 1) * P], xn[it.s][:, t, k * P:(k + 1) * P], env.ident[:])
                    i.then_inc(turned.sem, 1)

                def project(it):
                    pe.wait_ge(high.sem, high.at(it.g))
                    pe.wait_ge(norm.sem, norm.at(it.g))
                    pe.wait_ge(proj_act.sem, proj_act.at(it.g - 1))
                    for c in range(KD):
                        i = product(pK[:, c, :], env.w, (WK, slice(c * P, (c + 1) * P)), xt, it.s, 0)
                    i.then_inc(projected.sem, 1)
                    pe.wait_ge(proj_dve.sem, proj_dve.at(it.g - 1, 2))
                    for c in range(KD):
                        i = product(pQ[:, c, :], env.w, (WQ, slice(c * P, (c + 1) * P)), xt, it.s, 0)
                    i.then_inc(projected.sem, 1)
                    pe.wait_ge(proj_dve.sem, proj_dve.at(it.g - 1))
                    for t in range(2):
                        n = 0
                        for k in range(KD):
                            for a, b in PARTS:
                                i = t_.matmul(pL[:, t, :], xt[a][it.s][:, k, t * P:(t + 1) * P], env.rw[b][:, k, :],
                                              start=(n == 0), stop=(n == 3 * KD - 1))
                                n += 1
                    i.then_inc(projected.sem, 1)
                    pe.wait_ge(proj_act.sem, proj_act.at(it.g, 1))
                    pe.wait_ge(proj_dve.sem, proj_dve.at(it.g, 1))
                    for c in range(KD):
                        i = product(pK[:, c, :], env.w, (WV, slice(c * P, (c + 1) * P)), xt, it.s, 0)
                    i.then_inc(projected.sem, 1)

                def phase(it):
                    for n, w in enumerate((WKP, WQP)):
                        pe.wait_ge(proj_act.sem, proj_act.at(it.g, n + 1))
                        pe.wait_ge(proj_dve.sem, proj_dve.at(it.g, n + 1))
                        if n:
                            pe.wait_ge(ph_act.sem, ph_act.at(it.g, 1))
                        else:
                            pe.wait_ge(ph_act.sem, ph_act.at(it.g - 1, 2))
                        for c in range(KD):
                            i = product(pC[:, c, :], env.w, (w, slice(c * P, (c + 1) * P)), kq, it.s, 2 * n)
                        i.then_inc(phased.sem, 1)

                def turn_ret(it):
                    pe.wait_ge(mem_dve.sem, mem_dve.at(it.g))
                    pe.wait_ge(ln_dve.sem, ln_dve.at(it.g - 1))
                    for t in range(2):
                        for k in range(KD):
                            i = t_.transpose(pE[:, t, k * P:(k + 1) * P], ret[it.s][:, k, t * P:(t + 1) * P], env.ident[:])
                    i.then_inc(back.sem, 1)

                def turn_z(it):
                    pe.wait_ge(ln_dve.sem, ln_dve.at(it.g))
                    pe.wait_ge(z_act.sem, z_act.at(it.g - 1))
                    for t in range(2):
                        for k in range(KD):
                            i = t_.transpose(pF[:, k, t * P:(t + 1) * P], zt[it.s][:, t, k * P:(k + 1) * P], env.ident[:])
                    i.then_inc(z_turned.sem, 1)

                def project_out(it):
                    pe.wait_ge(z_dve.sem, z_dve.at(it.g))
                    pe.wait_ge(z_pool.sem, z_pool.at(it.g))
                    pe.wait_ge(out_dve.sem, out_dve.at(it.g - 1))
                    for t in range(2):
                        n = 0
                        for k in range(KD):
                            for a, b in PARTS:
                                i = t_.matmul(pG[:, t, :], z[a][it.s][:, k, t * P:(t + 1) * P], env.w[b][:, WO, k, :],
                                              start=(n == 0), stop=(n == 3 * KD - 1))
                                n += 1
                    i.then_inc(out_pe.sem, 1)

                for stage in (turned, projected, phased, back, z_turned, out_pe):
                    stage.open(pe)
                pipelined(pe, [turn_x, project, phase, lambda it: None, turn_ret, turn_z, project_out], ITEMS)


P = 128
BF16 = mybir.dt.bfloat16


def route(nc, env, name, logits, experts, choices, segments, cap, expert_rows, trash, picks):
    NT = logits.shape[1]
    per_seg = NT // segments
    W = NT * experts
    NB = (W + 511) // 512
    with ExitStack() as ctx:
        sb = lambda n, s, d=F32: ctx.enter_context(nc.sbuf_tensor(f"{name}_{n}", s, d))
        ps = lambda n, s, d=F32: ctx.enter_context(nc.psum_tensor(f"{name}_{n}", s, d))
        best = sb("best", [P, NT, 8]); which = sb("which", [P, NT, 8], U32); which_f = sb("which_f", [P, NT, 8])
        number = sb("number", [P, experts]); own = sb("own", [P, choices, NT])
        upper = sb("upper", [P, P], BF16); ones = sb("ones", [P, P], BF16)
        chosen = [sb(f"chosen{k}", [P, NT, experts], BF16) for k in range(choices)]
        before = sb("before", [P, choices, NT, experts])
        place = sb("place", [P, NT, experts])
        pos = sb("pos", [P, NT]); row = sb("row", [P, NT]); over = sb("over", [P, NT]); tmp = sb("tmp", [P, NT])
        seg_base = sb("seg_base", [P, NT])
        rel = sb("rel", [P, NT, experts]); total = sb("total", [P, NT])
        run = ps("run", [P, W]); tot = ps("tot", [P, W])
        made = env.sem(f"{name}_consts"); steps = env.sem(f"{name}_dve"); counted = env.sem(f"{name}_counted")
        weighed = env.sem(f"{name}_exp")
        bc = lambda ap, shape: ap.to_broadcast(shape)
        count = {}

        with nc.Block() as block:
            @block.gpsimd
            def _(pool):
                p = nc.gpsimd
                p.iota(number[:], [[1, experts]], base=0, channel_multiplier=0,
                       allow_small_or_imprecise_dtypes=True).then_inc(made, 1)
                for k in range(choices):
                    p.iota(own[:, k, :], [[P, NT]], base=trash + k * NT * P, channel_multiplier=1,
                           allow_small_or_imprecise_dtypes=True).then_inc(made, 1)
                p.memset(upper[:], 1.0).then_inc(made, 1)
                p.memset(ones[:], 1.0).then_inc(made, 1)
                for b in range(segments):
                    p.memset(seg_base[:, b * per_seg:(b + 1) * per_seg], float(b * cap)).then_inc(made, 1)
                pool.wait_ge(made, 3 + choices + segments)
                p.affine_select(out=upper[:], in_=upper[:], compare_op=ALU.is_ge, fill=0.0, base=0,
                                pattern=[[1, P]], channel_multiplier=-1).then_inc(made, 1)

            @block.vector
            def _(dve):
                v = nc.vector
                n = [0]

                def done(i):
                    n[0] += 1
                    i.then_inc(steps, 1)

                def settle():
                    dve.wait_ge(steps, n[0])

                for t in range(NT):
                    done(v.max(best[:, t, :], logits[:, t, :]))
                settle()
                for t in range(NT):
                    done(v.max_index(which[:, t, :], best[:, t, :], logits[:, t, :]))
                settle()
                done(v.tensor_copy(which_f[:], which[:]))
                if choices == 2:
                    done(v.tensor_tensor(tmp[:], best[:, :, 1], best[:, :, 0], ALU.subtract))
                    settle()
                else:
                    done(v.tensor_tensor(rel[:], logits[:], bc(best[:, :, 0:1], [P, NT, experts]), ALU.subtract))
                    settle()
                count["weigh"] = n[0]
                dve.wait_ge(made, 4 + choices + segments)
                for k in range(choices):
                    done(v.tensor_tensor(chosen[k][:], bc(which_f[:, :, k:k + 1], [P, NT, experts]),
                                         bc(number[:].unsqueeze(1), [P, NT, experts]), ALU.is_equal))
                    count[k] = n[0]
                for k in range(choices):
                    dve.wait_ge(counted, k + 1)
                    b4 = before[:, k].rearrange("p (b t) e -> p b t e", b=segments)
                    t4 = tot[:].rearrange("p (b t e) -> p b t e", b=segments, e=experts)
                    if k == 0:
                        done(v.memset(b4[:, :, 0, :], 0.0))
                    settle()
                    for t in range(per_seg):
                        last = t == per_seg - 1
                        if last and k + 1 == choices:
                            break
                        to = before[:, k + 1].rearrange("p (b t) e -> p b t e", b=segments)[:, :, 0, :] if last else b4[:, :, t + 1, :]
                        done(v.tensor_tensor(to, b4[:, :, t, :], t4[:, :, t, :], ALU.add))
                        settle()
                    flat = before[:, k].rearrange("p t e -> p (t e)")
                    done(v.tensor_tensor(place[:].rearrange("p t e -> p (t e)"), run[:], flat, ALU.add))
                    settle()
                    done(v.tensor_tensor(place[:], place[:], chosen[k][:], ALU.mult))
                    settle()
                    done(v.tensor_reduce(pos[:], place[:], axis=AX, op=ALU.add))
                    count["run%d" % k] = n[0]
                    settle()
                    done(v.tensor_scalar(over[:], pos[:], cap + 0.5, None, ALU.is_gt))
                    done(v.tensor_scalar(pos[:], pos[:], -1.0, cap - 1.0, ALU.add, ALU.min))
                    done(v.tensor_scalar(row[:], which_f[:, :, k], float(expert_rows), None, ALU.mult))
                    settle()
                    done(v.tensor_tensor(row[:], row[:], seg_base[:], ALU.add))
                    settle()
                    done(v.tensor_tensor(row[:], row[:], pos[:], ALU.add))
                    settle()
                    done(v.tensor_copy(picks[k].read[:], row[:]))
                    done(v.tensor_tensor(tmp[:] if choices == 1 else total[:], own[:, k, :], row[:], ALU.subtract))
                    settle()
                    t_ = tmp if choices == 1 else total
                    done(v.tensor_tensor(t_[:], t_[:], over[:], ALU.mult))
                    settle()
                    done(v.tensor_tensor(row[:], row[:], t_[:], ALU.add))
                    settle()
                    done(v.tensor_copy(picks[k].write[:], row[:]))
                    settle()
                dve.wait_ge(weighed, 1)
                if choices == 2:
                    done(v.tensor_scalar(total[:], tmp[:], 1.0, None, ALU.add))
                    settle()
                    done(v.reciprocal(picks[0].weight[:], total[:]))
                    settle()
                    done(v.tensor_tensor(picks[1].weight[:], picks[0].weight[:], tmp[:], ALU.mult))
                else:
                    done(v.tensor_reduce(total[:], rel[:], axis=AX, op=ALU.add))
                    done(v.tensor_scalar(over[:], over[:], -1.0, 1.0, ALU.mult, ALU.add))
                    settle()
                    done(v.reciprocal(total[:], total[:]))
                    settle()
                    done(v.tensor_tensor(picks[0].weight[:], total[:], over[:], ALU.mult))
                settle()

            @block.scalar
            def _(act):
                act.wait_ge(steps, count["weigh"])
                if choices == 2:
                    nc.scalar.activation(tmp[:], tmp[:], ACT.Exp).then_inc(weighed, 1)
                else:
                    nc.scalar.activation(rel[:], rel[:], ACT.Exp).then_inc(weighed, 1)

            @block.tensor
            def _(pe):
                pe.wait_ge(made, 4 + choices + segments)
                for k in range(choices):
                    pe.wait_ge(steps, count[k])
                    if k:
                        pe.wait_ge(steps, count["run%d" % (k - 1)])
                    flat = chosen[k][:].rearrange("p t e -> p (t e)")
                    for b in range(NB):
                        c = slice(b * 512, min(W, (b + 1) * 512))
                        nc.tensor.matmul(run[:, c], upper[:], flat[:, c], start=True, stop=True)
                        i = nc.tensor.matmul(tot[:, c], ones[:], flat[:, c], start=True, stop=True)
                    i.then_inc(counted, 1)


class Pick:

    def __init__(self, keep, name, NT):
        self.write = keep(f"{name}_write", [P, NT], U32)
        self.read = keep(f"{name}_read", [P, NT], U32)
        self.weight = keep(f"{name}_weight", [P, NT])


def scatter(nc, env, name, src, buf, picks, NT):
    SL = 4
    K = len(picks)
    with ExitStack() as ctx:
        rows = [ctx.enter_context(nc.sbuf_tensor(f"{name}_rows{i}", [P, src.shape[1]], F32)) for i in range(SL)]
        at = [[ctx.enter_context(nc.sbuf_tensor(f"{name}_at{i}_{k}", [P, 1], U32)) for k in range(K)] for i in range(SL)]
        loaded = [env.sem(f"{name}_loaded{i}") for i in range(SL)]
        sent = [env.sem(f"{name}_sent{i}") for i in range(SL)]
        indexed = env.sem(f"{name}_indexed")
        with nc.Block() as block:
            @block.sync
            def _(sp):
                for i in range(SL):
                    sp.dma_start(rows[i][:], src[i * P:(i + 1) * P, :]).then_inc(loaded[i], 16)
                with sp.Fori(1, NT // SL) as r:
                    for i in range(SL):
                        row = sp.snap((r * SL + i) * P)
                        sp.wait_ge(sent[i], r * (16 * K))
                        Carrier.carry(sp)
                        sp.dma_start(rows[i][:], src[bass.ds(row, P), :]).then_inc(loaded[i], 16)

            @block.gpsimd
            def _(pool):
                def send(r, i):
                    for k in range(K):
                        if not isinstance(r, int):
                            pool.wait_ge(sent[i], r * (16 * K))
                            Carrier.carry(pool)
                        nc.gpsimd.tensor_copy(at[i][k][:], picks[k].write[:, bass.ds(r * SL + i, 1)]).then_inc(indexed, 1)
                    pool.wait_ge(loaded[i], r * 16 + 16)
                    Carrier.carry(pool)
                    pool.wait_ge(indexed, (r * SL + i + 1) * K)
                    Carrier.carry(pool)
                    for k in range(K):
                        pool.indirect_dma_start(buf[:, :], bass.IndirectOffsetOnAxis(ap=at[i][k][:, 0:1], axis=0),
                                                rows[i][:], None).then_inc(sent[i], 16)

                for i in range(SL):
                    send(0, i)
                with pool.Fori(1, NT // SL) as r:
                    for i in range(SL):
                        send(r, i)
                for i in range(SL):
                    pool.wait_ge(sent[i], 16 * K * (NT // SL))


P, D, KD = 128, 256, 2
PARTS = ((0, 0), (0, 1), (1, 0))
E0, H0 = 8, 1024
HC = H0 // P
GR = 512
SUB = GR // P
PER = 5
ROWS0 = PER * GR
CAP0 = 614


def experts_l0(nc, env, buf, out_buf, w_fc, w_gate, w_proj, bias_cols, bias_rows):
    with ExitStack() as ctx:
        sb = lambda n, s, d=F32: ctx.enter_context(nc.sbuf_tensor("m0_" + n, s, d))
        ps = lambda n, s, d=F32: ctx.enter_context(nc.psum_tensor("m0_" + n, s, d))
        sem = lambda n: env.sem("m0_" + n)
        two = lambda n, s, d=F32: [sb(f"{n}{i}", s, d) for i in range(2)]
        cols = sb("cols", [P, 2, E0, HC]); rows_b = sb("rows", [P, E0, D])
        gate_bias = two("gate_bias", [P, HC]); bias_set = sem("bias_set")
        raw = sb("raw", [P, KD * H0])
        wt = [two("w_hi", [P, 3, KD * H0], F32R), two("w_lo", [P, 3, KD * H0], F32R)]
        x_in = two("x_in", [P, SUB, D])
        xt = [two("xt_hi", [P, KD, GR], F32R), two("xt_lo", [P, KD, GR], F32R)]
        gate = two("gate", [P, GR]); prod = two("prod", [P, GR]); act_f = two("act", [P, GR])
        ht = [sb("ht_hi", [P, HC, GR], F32R), sb("ht_lo", [P, HC, GR], F32R)]
        out = two("out", [P, SUB, D])
        pA = [ps(f"pA{i}", [P, GR]) for i in range(2)]
        pH = [ps(f"pH{i}", [P, GR]) for i in range(2)]; pG = [ps(f"pG{i}", [P, GR]) for i in range(2)]
        pO = [ps(f"pO{i}", [P, 2, D]) for i in range(2)]
        fc = lambda part, u, k, hc: wt[part][u][:, 0, :].rearrange("p (k h) -> p k h", k=KD)[:, k, hc * P:(hc + 1) * P]
        gt = lambda part, u, k, hc: wt[part][u][:, 1, :].rearrange("p (k h) -> p k h", k=KD)[:, k, hc * P:(hc + 1) * P]
        pj = lambda part, u, hc: wt[part][u][:, 2, :].rearrange("p (c d) -> p c d", c=HC)[:, hc, :]

        consts = sem("consts"); w_loaded = sem("w_loaded")
        w_high, w_low = sem("w_high"), sem("w_low")
        x_loaded = [sem(f"x_loaded{i}") for i in range(2)]; out_stored = [sem(f"out_stored{i}") for i in range(2)]
        turned = Steps(sem("turned"), 2); x_high = Steps(sem("x_high"), 2); x_low = Steps(sem("x_low"), 2)
        up = Steps(sem("up"), 2 * HC)
        gated = Steps(sem("gated"), HC); glu = Steps(sem("glu"), HC); silu = Steps(sem("silu"), HC)
        h_high = Steps(sem("h_high"), HC); h_low = Steps(sem("h_low"), HC)
        down = Steps(sem("down"), 2); added = Steps(sem("added"), 2); freed = Steps(sem("freed"), 1)

        def experts(eng, body, first=None):
            if first:
                first()
            with eng.Fori(0, E0 // 2) as r:
                for u in range(2):
                    body(r, u)

        def item(r, u, j):
            return Item(u * PER + j, r, 2 * PER)

        with nc.Block() as block:
            @block.sync
            def _(sp):
                sp.dma_start(cols[:], bias_cols.rearrange("p (w e c) -> p w e c", w=2, e=E0)).then_inc(consts, 16)
                sp.dma_start(rows_b[:], bias_rows.rearrange("p (e d) -> p e d", e=E0)).then_inc(consts, 16)

                def load_weight(e, n):
                    src = (w_fc, w_gate, w_proj)[n][bass.ds(e, 1)].rearrange("o (k p) h -> p (o k) h", p=P)
                    sp.dma_start(raw[:].rearrange("p (k h) -> p k h", h=(H0, H0, D)[n]), src).then_inc(w_loaded, 16)

                def load_x(it):
                    row = sp.snap(it.g * GR)
                    sp.wait_ge(turned.sem, turned.at(it.g - 2))
                    Carrier.carry(sp)
                    sp.dma_start(x_in[it.s][:], buf[bass.ds(row, GR), :].rearrange("(t p) d -> p t d", p=P)).then_inc(x_loaded[it.s], 16)

                def free(it):
                    sp.wait_ge(out_stored[it.s], it.q * 16 + 16)
                    sp.sem_inc(freed.sem, 1)

                def store(it):
                    row = sp.snap(it.g * GR)
                    sp.wait_ge(added.sem, added.at(it.g))
                    Carrier.carry(sp)
                    sp.dma_start(out_buf[bass.ds(row, GR), :].rearrange("(t p) d -> p t d", p=P), out[it.s][:]).then_inc(out_stored[it.s], 16)

                def body(r, u):
                    nxt = sp.snap(r * 2 + 1) if u == 0 else sp.snap((r * 2 + 2) % E0)
                    for j in range(PER):
                        load_x(item(r, u, j))
                        if j:
                            store(item(r, u, j - 1))
                        if j > 1:
                            free(item(r, u, j - 2))
                        if 1 <= j <= 3:
                            sp.wait_ge(w_low, r * 6 + (u * 3 + 2 + j))
                            Carrier.carry(sp)
                            load_weight(nxt, j - 1)
                    store(item(r, u, PER - 1))
                    free(item(r, u, PER - 2))
                    free(item(r, u, PER - 1))

                for n in range(3):
                    if n:
                        sp.wait_ge(w_low, n)
                    load_weight(0, n)
                freed.open(sp)
                experts(sp, body)
                for s in range(2):
                    sp.wait_ge(out_stored[s], 16 * E0 * PER // 2)

            @block.vector
            def _(dve):
                v = nc.vector

                def split_high(u, n, loaded, used):
                    dve.wait_ge(w_loaded, loaded)
                    dve.wait_ge(down.sem, down.at(used))
                    v.tensor_copy(wt[0][u][:, n, :], raw[:]).then_inc(w_high, 1)

                def low_x(it):
                    for k in range(KD):
                        dve.wait_ge(x_high.sem, x_high.at(it.g, k + 1))
                        if k == 0:
                            dve.wait_ge(up.sem, up.at(it.g - 2))
                        v.tensor_tensor(xt[1][it.s][:, k, :], pA[k][:], xt[0][it.s][:, k, :].bitcast(F32), ALU.subtract).then_inc(x_low.sem, 1)

                def hidden(it, e):

                    def high(hc):
                        dve.wait_ge(silu.sem, silu.at(it.g, hc + 1))
                        if hc == 0:
                            dve.wait_ge(down.sem, down.at(it.g - 1))
                        v.tensor_copy(ht[0][:, hc, :], act_f[hc % 2][:]).then_inc(h_high.sem, 1)

                    for hc in range(HC):
                        dve.wait_ge(up.sem, up.at(it.g, 2 * hc + 1))
                        dve.wait_ge(gated.sem, gated.at(it.g, hc + 1))
                        dve.wait_ge(silu.sem, silu.at(it.g, hc - 1))
                        v.scalar_tensor_tensor(out=prod[hc % 2][:], in0=pH[hc % 2][:], scalar=cols[:, 0, bass.ds(e, 1), hc:hc + 1].rearrange("p o c -> p (o c)"),
                                                        in1=gate[hc % 2][:], op0=ALU.add, op1=ALU.mult).then_inc(glu.sem, 1)
                        if hc:
                            high(hc - 1)
                    high(HC - 1)

                def add_bias(it, e):
                    for half in range(2):
                        dve.wait_ge(down.sem, down.at(it.g, half + 1))
                        if half == 0:
                            dve.wait_ge(freed.sem, freed.at(it.g - 2))
                        for t in range(2):
                            i = v.tensor_tensor(out[it.s][:, half * 2 + t, :].unsqueeze(1), pO[half][:, t:t + 1, :], rows_b[:, bass.ds(e, 1), :], ALU.add)
                        i.then_inc(added.sem, 1)

                def body(r, u):
                    e = dve.snap(r * 2 + u)
                    for j in range(PER):
                        if j:
                            add_bias(item(r, u, j - 1), e)
                        if j == 0:
                            low_x(item(r, u, 0))
                        hidden(item(r, u, j), e)
                        if j + 1 < PER:
                            low_x(item(r, u, j + 1))
                        if 1 <= j <= 3:
                            split_high(1 - u, j - 1, r * 96 + (u * 48 + 48 + 16 * j), r * (2 * PER) + (u * PER - 1))
                    add_bias(item(r, u, PER - 1), e)

                for stage in (x_low, glu, h_high, added):
                    stage.open(dve)
                dve.wait_ge(consts, 32)
                for n in range(3):
                    split_high(0, n, 16 * n + 16, -1)
                experts(dve, body)

            @block.gpsimd
            def _(pool):
                p = nc.gpsimd

                def split_low(u, n, high):
                    pool.wait_ge(w_high, high)
                    p.tensor_tensor(wt[1][u][:, n, :], raw[:], wt[0][u][:, n, :].bitcast(F32), ALU.subtract).then_inc(w_low, 1)

                def hidden(it):
                    for hc in range(HC):
                        pool.wait_ge(h_high.sem, h_high.at(it.g, hc + 1))
                        p.tensor_tensor(ht[1][:, hc, :], act_f[hc % 2][:], ht[0][:, hc, :].bitcast(F32), ALU.subtract).then_inc(h_low.sem, 1)

                def body(r, u):
                    for j in range(PER):
                        hidden(item(r, u, j))
                        if 1 <= j <= 3:
                            split_low(1 - u, j - 1, r * 6 + (u * 3 + 3 + j))

                for n in range(3):
                    split_low(0, n, n + 1)
                for stage in (h_low,):
                    stage.open(pool)
                experts(pool, body)

            @block.scalar
            def _(act):
                a = nc.scalar

                def high_x(it):
                    for k in range(KD):
                        act.wait_ge(turned.sem, turned.at(it.g, k + 1))
                        if k == 0:
                            act.wait_ge(up.sem, up.at(it.g - 2))
                        a.activation(xt[0][it.s][:, k, :], pA[k][:], ACT.Copy).then_inc(x_high.sem, 1)

                def hidden(it, u):

                    def activate(hc):
                        act.wait_ge(glu.sem, glu.at(it.g, hc + 1))
                        act.wait_ge(h_high.sem, h_high.at(it.g, hc - 1))
                        act.wait_ge(h_low.sem, h_low.at(it.g, hc - 1))
                        a.activation(act_f[hc % 2][:], prod[hc % 2][:], ACT.Silu).then_inc(silu.sem, 1)

                    for hc in range(HC):
                        act.wait_ge(up.sem, up.at(it.g, 2 * hc + 2))
                        act.wait_ge(glu.sem, glu.at(it.g, hc - 1))
                        a.activation(gate[hc % 2][:], pG[hc % 2][:], ACT.Identity, bias=gate_bias[u][:, hc:hc + 1]).then_inc(gated.sem, 1)
                        if hc:
                            activate(hc - 1)
                    activate(HC - 1)

                def body(r, u):
                    e = act.snap(r * 2 + u)
                    a.activation(gate_bias[u][:].unsqueeze(1), cols[:, 1, bass.ds(e, 1), :], ACT.Copy).then_inc(bias_set, 1)
                    high_x(item(r, u, 0))
                    act.wait_ge(bias_set, r * 2 + u + 1)
                    for j in range(PER):
                        hidden(item(r, u, j), u)
                        if j + 1 < PER:
                            high_x(item(r, u, j + 1))

                act.wait_ge(consts, 32)
                for stage in (x_high, gated, silu):
                    stage.open(act)
                experts(act, body)

            @block.tensor
            def _(pe):
                t_ = nc.tensor

                def turn_x(it):
                    pe.wait_ge(x_loaded[it.s], it.q * 16 + 16)
                    for k in range(KD):
                        pe.wait_ge(x_low.sem, x_low.at(it.g - 1, k + 1))
                        for t in range(SUB):
                            i = t_.transpose(pA[k][:, t * P:(t + 1) * P], x_in[it.s][:, t, k * P:(k + 1) * P], env.ident[:])
                        i.then_inc(turned.sem, 1)

                def up_products(it, u):
                    pe.wait_ge(x_low.sem, x_low.at(it.g))
                    for hc in range(HC):
                        pe.wait_ge(glu.sem, glu.at(it.g, hc - 1))
                        for bank, w in ((pH, fc), (pG, gt)):
                            n = 0
                            for k in range(KD):
                                for i, j in PARTS:
                                    last = t_.matmul(bank[hc % 2][:], w(i, u, k, hc), xt[j][it.s][:, k, :], start=(n == 0), stop=(n == 5))
                                    n += 1
                            last.then_inc(up.sem, 1)

                def down_products(it, u):
                    for half in range(2):
                        pe.wait_ge(added.sem, added.at(it.g - 1, half + 1))
                        for t in range(2):
                            n = 0
                            sub = half * 2 + t
                            for hc in range(HC):
                                if sub == 0:
                                    pe.wait_ge(h_low.sem, h_low.at(it.g, hc + 1))
                                for i, j in PARTS:
                                    last = t_.matmul(pO[half][:, t, :], ht[i][:, hc, sub * P:(sub + 1) * P], pj(j, u, hc),
                                                     start=(n == 0), stop=(n == 3 * HC - 1))
                                    n += 1
                        last.then_inc(down.sem, 1)

                def body(r, u):
                    turn_x(item(r, u, 0))
                    for j in range(PER):
                        if j:
                            down_products(item(r, u, j - 1), u)
                        if j == 0:
                            pe.wait_ge(w_low, r * 6 + u * 3 + 3)
                        up_products(item(r, u, j), u)
                        if j + 1 < PER:
                            turn_x(item(r, u, j + 1))
                    down_products(item(r, u, PER - 1), u)

                for stage in (turned, up, down):
                    stage.open(pe)
                experts(pe, body)


P, D, KD = 128, 256, 2
PARTS = ((0, 0), (0, 1), (1, 0))
EPS = 1e-5


def combine_l0(nc, env, out0, picks, res0, res1, xn1, xt1, head_w, logits1, dt_raw, NT):
    NO = head_w.shape[1]
    NE = logits1.shape[2]
    with ExitStack() as ctx:
        sb = lambda n, s, d=F32: ctx.enter_context(nc.sbuf_tensor("c0_" + n, s, d))
        ps = lambda n, s, d=F32: ctx.enter_context(nc.psum_tensor("c0_" + n, s, d))
        sem = lambda n: env.sem("c0_" + n)
        two = lambda n, s, d=F32: [sb(f"{n}{i}", s, d) for i in range(2)]
        w_raw = sb("w_raw", [P, KD, NO]); w = [sb("w_hi", [P, KD, NO], F32R), sb("w_lo", [P, KD, NO], F32R)]
        res_in = two("res_in", [P, D])
        at = [two(f"at{k}_", [P, 1], U32) for k in range(2)]
        got = [two(f"got{k}_", [P, D]) for k in range(2)]
        x1 = two("x1", [P, D]); part = sb("part", [P, D])
        stats = sb("stats", [P, 6]); mv = sb("mv", [P, 2]); var = sb("var", [P, 1]); rstd = sb("rstd", [P, 1])
        xn = two("xn", [P, D]); res = two("res", [P, D])
        xt = two("xt", [P, 2, KD, P], F32R)
        pT = [ps(f"pT{i}", [P, KD, P]) for i in range(2)]; pH = ps("pH", [P, NO])
        w_loaded = sem("w_loaded"); w_split = sem("w_split")
        loaded = [sem(f"loaded{i}") for i in range(2)]; gathered = [sem(f"gathered{i}") for i in range(2)]
        xn_stored, res_stored, xt_stored = ([sem(f"{n}{i}") for i in range(2)] for n in ("xn_stored", "res_stored", "xt_stored"))
        indexed = Steps(sem("indexed"), 2)
        norm = Steps(sem("norm"), 6)
        pool_s = Steps(sem("pool"), 2)
        turned = Steps(sem("turned"), 1); high = Steps(sem("high"), 1); low = Steps(sem("low"), 1)
        heads = Steps(sem("heads"), 1); kept = Steps(sem("kept"), 1)
        nop = lambda it: None
        with nc.Block() as block:
            @block.sync
            def _(sp):
                sp.dma_start(w_raw[:], head_w.rearrange("(k p) e -> p k e", p=P)).then_inc(w_loaded, 16)

                def load(it):
                    row = at_row(sp, it, P)
                    sp.wait_ge(norm.sem, norm.at(it.g - 2, 1))
                    Carrier.carry(sp)
                    sp.dma_start(res_in[it.s][:], res0[bass.ds(row, P), :]).then_inc(loaded[it.s], 16)

                def store(it):
                    row = at_row(sp, it, P)
                    sp.wait_ge(norm.sem, norm.at(it.g))
                    Carrier.carry(sp)
                    sp.dma_start(xn1[bass.ds(row, P), :], xn[it.s][:]).then_inc(xn_stored[it.s], 16)
                    sp.wait_ge(pool_s.sem, pool_s.at(it.g))
                    Carrier.carry(sp)
                    sp.dma_start(res1[bass.ds(row, P), :], res[it.s][:]).then_inc(res_stored[it.s], 16)

                def store_turned(it):
                    row = at_row(sp, it, P)
                    sp.wait_ge(high.sem, high.at(it.g))
                    Carrier.carry(sp)
                    sp.wait_ge(low.sem, low.at(it.g))
                    Carrier.carry(sp)
                    sp.dma_start(xt1[bass.ds(row, P)], xt[it.s][:].bitcast(F32)).then_inc(xt_stored[it.s], 16)

                pipelined(sp, [load, store, store_turned, nop], NT)
                for s in range(2):
                    for q in (xn_stored, res_stored, xt_stored):
                        sp.wait_ge(q[s], 16 * NT // 2)

            @block.gpsimd
            def _(pool):
                p = nc.gpsimd

                def gather(it):
                    for k in range(2):
                        if it.again:
                            pool.wait_ge(gathered[it.s], it.q * 32)
                            Carrier.carry(pool)
                        p.tensor_copy(at[k][it.s][:], picks[k].read[:, bass.ds(it.g, 1)]).then_inc(indexed.sem, 1)
                    pool.wait_ge(indexed.sem, indexed.at(it.g))
                    Carrier.carry(pool)
                    pool.wait_ge(norm.sem, norm.at(it.g - 2, 2))
                    Carrier.carry(pool)
                    for k in range(2):
                        pool.indirect_dma_start(got[k][it.s][:], None, out0[:, :],
                                                bass.IndirectOffsetOnAxis(ap=at[k][it.s][:, 0:1], axis=0)).then_inc(gathered[it.s], 16)

                def normalise(it):
                    pool.wait_ge(norm.sem, norm.at(it.g, 5))
                    p.tensor_tensor(rstd[:], var[:], env.neg_half[:, 0:1], ALU.pow).then_inc(pool_s.sem, 1)
                    pool.wait_ge(norm.sem, norm.at(it.g))
                    if it.again:
                        pool.wait_ge(res_stored[it.s], it.q * 16)
                    p.tensor_tensor(res[it.s][:], x1[it.s][:], xn[it.s][:], ALU.add).then_inc(pool_s.sem, 1)

                for stage in (indexed, pool_s):
                    stage.open(pool)
                pipelined(pool, [gather, normalise, nop, nop], NT)

            @block.vector
            def _(dve):
                v = nc.vector
                dve.wait_ge(w_loaded, 16)
                v.tensor_copy(w[0][:], w_raw[:]).then_inc(w_split, 1)
                dve.wait_ge(w_split, 1)
                v.tensor_tensor(w[1][:], w_raw[:], w[0][:].bitcast(F32), ALU.subtract).then_inc(w_split, 1)

                def normalise(it):
                    dve.wait_ge(loaded[it.s], it.q * 16 + 16)
                    dve.wait_ge(gathered[it.s], it.q * 32 + 32)
                    weight = lambda k: picks[k].weight[:, bass.ds(it.g, 1)]
                    v.scalar_tensor_tensor(out=part[:], in0=got[0][it.s][:], scalar=weight(0), in1=res_in[it.s][:],
                                                     op0=ALU.mult, op1=ALU.add).then_inc(norm.sem, 1)
                    dve.wait_ge(norm.sem, norm.at(it.g, 1))
                    dve.wait_ge(pool_s.sem, pool_s.at(it.g - 2))
                    v.scalar_tensor_tensor(out=x1[it.s][:], in0=got[1][it.s][:], scalar=weight(1), in1=part[:],
                                                     op0=ALU.mult, op1=ALU.add).then_inc(norm.sem, 1)
                    dve.wait_ge(norm.sem, norm.at(it.g, 2))
                    v.bn_stats(stats[:], x1[it.s][:]).then_inc(norm.sem, 1)
                    dve.wait_ge(norm.sem, norm.at(it.g, 3))
                    Carrier.carry(dve)
                    v.bn_aggr(mv[:], stats[:]).then_inc(norm.sem, 1)
                    dve.wait_ge(norm.sem, norm.at(it.g, 4))
                    v.tensor_scalar(var[:], mv[:, 1:2], EPS, None, ALU.add).then_inc(norm.sem, 1)
                    dve.wait_ge(pool_s.sem, pool_s.at(it.g, 1))
                    dve.wait_ge(turned.sem, turned.at(it.g - 2))
                    if it.again:
                        dve.wait_ge(xn_stored[it.s], it.q * 16)
                    v.tensor_scalar(xn[it.s][:], x1[it.s][:], mv[:, 0:1], rstd[:], ALU.subtract, ALU.mult).then_inc(norm.sem, 1)

                def low_part(it):
                    dve.wait_ge(high.sem, high.at(it.g))
                    if it.again:
                        dve.wait_ge(xt_stored[it.s], it.q * 16)
                    v.tensor_tensor(xt[it.s][:, 1], pT[it.s][:], xt[it.s][:, 0].bitcast(F32), ALU.subtract).then_inc(low.sem, 1)

                def keep(it):
                    dve.wait_ge(heads.sem, heads.at(it.g))
                    v.tensor_copy(logits1[:, bass.ds(it.g, 1), :], pH[:, 0:NE].unsqueeze(1))
                    v.tensor_copy(dt_raw[:, bass.ds(it.g, 1), :], pH[:, NE:NO].unsqueeze(1)).then_inc(kept.sem, 1)

                for stage in (norm, low, kept):
                    stage.open(dve)
                pipelined(dve, [nop, normalise, low_part, keep], NT)

            @block.scalar
            def _(act):
                def high_part(it):
                    act.wait_ge(turned.sem, turned.at(it.g))
                    act.wait_ge(heads.sem, heads.at(it.g - 2))
                    if it.again:
                        act.wait_ge(xt_stored[it.s], it.q * 16)
                    nc.scalar.activation(xt[it.s][:, 0], pT[it.s][:], ACT.Copy).then_inc(high.sem, 1)

                for stage in (high,):
                    stage.open(act)
                pipelined(act, [nop, nop, high_part, nop], NT)

            @block.tensor
            def _(pe):
                t_ = nc.tensor
                pe.wait_ge(w_split, 2)

                def turn(it):
                    pe.wait_ge(norm.sem, norm.at(it.g))
                    pe.wait_ge(low.sem, low.at(it.g - 2))
                    for k in range(KD):
                        i = t_.transpose(pT[it.s][:, k, :], xn[it.s][:, k * P:(k + 1) * P], env.ident[:])
                    i.then_inc(turned.sem, 1)

                def project(it):
                    pe.wait_ge(low.sem, low.at(it.g))
                    pe.wait_ge(kept.sem, kept.at(it.g - 1))
                    n = 0
                    for k in range(KD):
                        for a, b in PARTS:
                            i = t_.matmul(pH[:], xt[it.s][:, a, k, :], w[b][:, k, :], start=(n == 0), stop=(n == 5))
                            n += 1
                    i.then_inc(heads.sem, 1)

                for stage in (turned, heads):
                    stage.open(pe)
                pipelined(pe, [nop, nop, turn, project], NT)


def combine_l1(nc, env, out1, pick, res, final, NT):
    with ExitStack() as ctx:
        sb = lambda n, s, d=F32: ctx.enter_context(nc.sbuf_tensor("c1_" + n, s, d))
        sem = lambda n: env.sem("c1_" + n)
        two = lambda n, s, d=F32: [sb(f"{n}{i}", s, d) for i in range(2)]
        res_in = two("res_in", [P, D]); at = two("at", [P, 1], U32); got = two("got", [P, D]); out = two("out", [P, D])
        loaded = [sem(f"loaded{i}") for i in range(2)]; gathered = [sem(f"gathered{i}") for i in range(2)]
        stored = [sem(f"stored{i}") for i in range(2)]
        indexed = Steps(sem("indexed"), 1); summed = Steps(sem("summed"), 1)
        nop = lambda it: None
        with nc.Block() as block:
            @block.sync
            def _(sp):
                def load(it):
                    row = at_row(sp, it, P)
                    sp.wait_ge(summed.sem, summed.at(it.g - 2))
                    Carrier.carry(sp)
                    sp.dma_start(res_in[it.s][:], res[bass.ds(row, P), :]).then_inc(loaded[it.s], 16)

                def store(it):
                    row = at_row(sp, it, P)
                    sp.wait_ge(summed.sem, summed.at(it.g))
                    Carrier.carry(sp)
                    sp.dma_start(final[bass.ds(row, P), :], out[it.s][:]).then_inc(stored[it.s], 16)

                pipelined(sp, [load, store], NT)
                for s in range(2):
                    sp.wait_ge(stored[s], 16 * NT // 2)

            @block.gpsimd
            def _(pool):
                def gather(it):
                    if it.again:
                        pool.wait_ge(gathered[it.s], it.q * 16)
                        Carrier.carry(pool)
                    nc.gpsimd.tensor_copy(at[it.s][:], pick.read[:, bass.ds(it.g, 1)]).then_inc(indexed.sem, 1)
                    pool.wait_ge(indexed.sem, indexed.at(it.g))
                    Carrier.carry(pool)
                    pool.wait_ge(summed.sem, summed.at(it.g - 2))
                    Carrier.carry(pool)
                    pool.indirect_dma_start(got[it.s][:], None, out1[:, :],
                                            bass.IndirectOffsetOnAxis(ap=at[it.s][:, 0:1], axis=0)).then_inc(gathered[it.s], 16)

                for stage in (indexed,):
                    stage.open(pool)
                pipelined(pool, [gather, nop], NT)

            @block.vector
            def _(dve):
                def add(it):
                    dve.wait_ge(loaded[it.s], it.q * 16 + 16)
                    dve.wait_ge(gathered[it.s], it.q * 16 + 16)
                    if it.again:
                        dve.wait_ge(stored[it.s], it.q * 16)
                    nc.vector.scalar_tensor_tensor(out=out[it.s][:], in0=got[it.s][:], scalar=pick.weight[:, bass.ds(it.g, 1)],
                                                               in1=res_in[it.s][:], op0=ALU.mult, op1=ALU.add).then_inc(summed.sem, 1)

                for stage in (summed,):
                    stage.open(dve)
                pipelined(dve, [nop, add], NT)


P, D, KD = 128, 256, 2
PARTS = ((0, 0), (0, 1), (1, 0))
E1, CAP1 = 32, 320
SUBS = [(n * P, min(P, CAP1 - n * P)) for n in range((CAP1 + P - 1) // P)]


def experts_l1(nc, env, buf, out_buf, weights):
    with ExitStack() as ctx:
        sb = lambda n, s, d=F32: ctx.enter_context(nc.sbuf_tensor("m1_" + n, s, d))
        ps = lambda n, s, d=F32: ctx.enter_context(nc.psum_tensor("m1_" + n, s, d))
        sem = lambda n: env.sem("m1_" + n)
        two = lambda n, s, d=F32: [sb(f"{n}{i}", s, d) for i in range(2)]
        NS = len(SUBS)
        raw = two("raw", [P, 3, KD, D])
        w = [two("w_hi", [P, 3, KD, D], F32R), two("w_lo", [P, 3, KD, D], F32R)]
        x_in = two("x_in", [P, NS, D])
        xt = [two("xt_hi", [P, KD, CAP1], F32R), two("xt_lo", [P, KD, CAP1], F32R)]
        gate = two("gate", [P, KD, CAP1]); h = two("h", [P, KD, CAP1])
        ht = [two("ht_hi", [P, KD, CAP1], F32R), two("ht_lo", [P, KD, CAP1], F32R)]
        out = two("out", [P, NS, D])
        pA = [ps(f"pA{k}", [P, CAP1]) for k in range(KD)]
        pG = [ps(f"pG{k}", [P, CAP1]) for k in range(KD)]; pU = [ps(f"pU{k}", [P, CAP1]) for k in range(KD)]
        pO = [ps("pO0", [P, 2, D]), ps("pO1", [P, 1, D])]
        w_loaded = [sem(f"w_loaded{i}") for i in range(2)]; x_loaded = [sem(f"x_loaded{i}") for i in range(2)]
        stored = [sem(f"stored{i}") for i in range(2)]
        w_high = Steps(sem("w_high"), 1); w_low = Steps(sem("w_low"), 1)
        turned = Steps(sem("turned"), 2); x_high = Steps(sem("x_high"), 2); x_low = Steps(sem("x_low"), 2)
        up = Steps(sem("up"), 2); silu = Steps(sem("silu"), 2); mul = Steps(sem("mul"), 2)
        h_high = Steps(sem("h_high"), 2); h_low = Steps(sem("h_low"), 2)
        down = Steps(sem("down"), 2); kept = Steps(sem("kept"), 2)
        nop = lambda it: None
        with nc.Block() as block:
            @block.sync
            def _(sp):
                def load(it):
                    e = it.g if isinstance(it.g, int) else sp.snap(it.g)
                    row = at_row(sp, it, CAP1)
                    sp.wait_ge(w_low.sem, w_low.at(it.g - 2))
                    Carrier.carry(sp)
                    sp.dma_start(raw[it.s][:], weights[bass.ds(e, 1)].rearrange("o w (k p) f -> p (o w) k f", p=P)).then_inc(w_loaded[it.s], 16)
                    sp.wait_ge(turned.sem, turned.at(it.g - 2))
                    Carrier.carry(sp)
                    for n, (at, m) in enumerate(SUBS):
                        sp.dma_start(x_in[it.s][0:m, n, :], buf[bass.ds(row + at, m), :]).then_inc(x_loaded[it.s], 16)

                def store(it):
                    row = at_row(sp, it, CAP1)
                    sp.wait_ge(kept.sem, kept.at(it.g))
                    Carrier.carry(sp)
                    for n, (at, m) in enumerate(SUBS):
                        sp.dma_start(out_buf[bass.ds(row + at, m), :], out[it.s][0:m, n, :]).then_inc(stored[it.s], 16)

                pipelined(sp, [load, nop, nop, store], E1)
                for s in range(2):
                    sp.wait_ge(stored[s], 16 * NS * E1 // 2)

            @block.vector
            def _(dve):
                v = nc.vector

                def split(it):
                    dve.wait_ge(w_loaded[it.s], it.q * 16 + 16)
                    dve.wait_ge(down.sem, down.at(it.g - 2))
                    v.tensor_copy(w[0][it.s][:], raw[it.s][:]).then_inc(w_high.sem, 1)
                    for k in range(KD):
                        dve.wait_ge(x_high.sem, x_high.at(it.g, k + 1))
                        dve.wait_ge(up.sem, up.at(it.g - 2))
                        v.tensor_tensor(xt[1][it.s][:, k, :], pA[k][:], xt[0][it.s][:, k, :].bitcast(F32), ALU.subtract).then_inc(x_low.sem, 1)

                def hidden(it):
                    dve.wait_ge(h_low.sem, h_low.at(it.g - 2))
                    for k in range(KD):
                        dve.wait_ge(silu.sem, silu.at(it.g, k + 1))
                        v.tensor_tensor(h[it.s][:, k, :], pU[k][:], gate[it.s][:, k, :], ALU.mult).then_inc(mul.sem, 1)
                    dve.wait_ge(down.sem, down.at(it.g - 2))
                    for k in range(KD):
                        dve.wait_ge(mul.sem, mul.at(it.g, k + 1))
                        v.tensor_copy(ht[0][it.s][:, k, :], h[it.s][:, k, :]).then_inc(h_high.sem, 1)

                for stage in (w_high, x_low, mul, h_high):
                    stage.open(dve)
                pipelined(dve, [nop, split, hidden, nop], E1)

            @block.gpsimd
            def _(pool):
                p = nc.gpsimd

                def split(it):
                    pool.wait_ge(w_high.sem, w_high.at(it.g))
                    p.tensor_tensor(w[1][it.s][:], raw[it.s][:], w[0][it.s][:].bitcast(F32), ALU.subtract).then_inc(w_low.sem, 1)

                def hidden(it):
                    for k in range(KD):
                        pool.wait_ge(h_high.sem, h_high.at(it.g, k + 1))
                        p.tensor_tensor(ht[1][it.s][:, k, :], h[it.s][:, k, :], ht[0][it.s][:, k, :].bitcast(F32), ALU.subtract).then_inc(h_low.sem, 1)

                for stage in (w_low, h_low):
                    stage.open(pool)
                pipelined(pool, [nop, split, hidden, nop], E1)

            @block.scalar
            def _(act):
                a = nc.scalar

                def high_part(it):
                    for k in range(KD):
                        act.wait_ge(turned.sem, turned.at(it.g, k + 1))
                        act.wait_ge(up.sem, up.at(it.g - 2))
                        a.activation(xt[0][it.s][:, k, :], pA[k][:], ACT.Copy).then_inc(x_high.sem, 1)

                def gates(it):
                    act.wait_ge(mul.sem, mul.at(it.g - 2))
                    for k in range(KD):
                        act.wait_ge(up.sem, up.at(it.g, k + 1))
                        a.activation(gate[it.s][:, k, :], pG[k][:], ACT.Silu).then_inc(silu.sem, 1)

                def keep(it):
                    if it.again:
                        act.wait_ge(stored[it.s], it.q * (16 * NS))
                    act.wait_ge(down.sem, down.at(it.g, 1))
                    a.activation(out[it.s][:, 0:2, :], pO[0][:], ACT.Copy).then_inc(kept.sem, 1)
                    act.wait_ge(down.sem, down.at(it.g, 2))
                    m = SUBS[-1][1]
                    a.activation(out[it.s][0:m, 2, :], pO[1][0:m, 0, :], ACT.Copy).then_inc(kept.sem, 1)

                for stage in (x_high, silu, kept):
                    stage.open(act)
                pipelined(act, [nop, high_part, gates, keep], E1)

            @block.tensor
            def _(pe):
                t_ = nc.tensor

                def turn(it):
                    pe.wait_ge(x_loaded[it.s], (it.q + 1) * (16 * NS))
                    for k in range(KD):
                        pe.wait_ge(x_low.sem, x_low.at(it.g - 1, k + 1))
                        for n, (at, m) in enumerate(SUBS):
                            i = t_.transpose(pA[k][:, at:at + m], x_in[it.s][0:m, n, k * P:(k + 1) * P], env.ident[0:m, 0:m])
                        i.then_inc(turned.sem, 1)

                def up_products(it):
                    pe.wait_ge(w_low.sem, w_low.at(it.g))
                    pe.wait_ge(x_low.sem, x_low.at(it.g))
                    for f in range(KD):
                        pe.wait_ge(mul.sem, mul.at(it.g - 1, f + 1))
                        for n_w, bank in ((0, pG), (1, pU)):
                            n = 0
                            for k in range(KD):
                                for i, j in PARTS:
                                    last = t_.matmul(bank[f][:], w[i][it.s][:, n_w, k, f * P:(f + 1) * P], xt[j][it.s][:, k, :],
                                                     start=(n == 0), stop=(n == 5))
                                    n += 1
                        last.then_inc(up.sem, 1)

                def down_products(it):
                    pe.wait_ge(h_low.sem, h_low.at(it.g))
                    for s_, (at, m) in enumerate(SUBS):
                        if s_ == 0:
                            pe.wait_ge(kept.sem, kept.at(it.g - 1, 1))
                        if s_ == 2:
                            pe.wait_ge(kept.sem, kept.at(it.g - 1, 2))
                        n = 0
                        for k in range(KD):
                            for i, j in PARTS:
                                last = t_.matmul(pO[s_ // 2][0:m, s_ % 2, :], ht[i][it.s][:, k, at:at + m], w[j][it.s][:, 2, k, :],
                                                 start=(n == 0), stop=(n == 5))
                                n += 1
                        if s_:
                            last.then_inc(down.sem, 1)

                for stage in (turned, up, down):
                    stage.open(pe)
                pipelined(pe, [nop, turn, up_products, down_products], E1)


P, D, KD = 128, 256, 2
PARTS = ((0, 0), (0, 1), (1, 0))
EPS = 1e-5
DI, NS, NH, HD = 512, 64, 8, 64
CC = DI // P
CX = CC + 1
TAPS = 4
HALO = TAPS - 1
BATCH, SEQ = 4, 2048
TB = SEQ // P
NT = BATCH * TB
W = P + HALO


def mixer(nc, env, tag, backward, in_w, conv_cols, out_w, norm_cols, head_rows, dt_raw, dt_col, xt1, res_in_d, res_out_d):
    with ExitStack() as ctx:
        sb = lambda n, s, d=F32: ctx.enter_context(nc.sbuf_tensor(f"{tag}_{n}", s, d))
        ps = lambda n, s, d=F32: ctx.enter_context(nc.psum_tensor(f"{tag}_{n}", s, d))
        sem = lambda n: env.sem(f"{tag}_{n}")
        two = lambda n, s, d=F32: [sb(f"{n}{i}", s, d) for i in range(2)]
        NO = DI + CX * P
        w_raw = sb("w_raw", [P, KD, NO]); w = [sb("w_hi", [P, KD, NO], F32R), sb("w_lo", [P, KD, NO], F32R)]
        conv = sb("conv", [P, CX, TAPS + 1]); norm_c = sb("norm_c", [P, CC])
        ow_raw = sb("ow_raw", [P, CC, D]); ow = sb("ow", [P, CC, D])
        rows = sb("rows", [P, 3, NH])
        dt = sb("dt", [P, NT, NH]); da = sb("da", [P, NT, NH])
        grow = sb("grow", [P, NT, NH]); fade = sb("fade", [P, NT, NH]); whole = sb("whole", [P, NT, NH])
        t1 = sb("t1", [P, NT, NH]); t2 = sb("t2", [P, NT, NH])
        upto = sb("upto", [P, P]); past = sb("past", [P, P]); ones = sb("ones", [P, P])
        state = sb("state", [NS, BATCH, DI]); faded = [sb(f"faded{i}", [NS, DI]) for i in range(2)]
        u = sb("u", [P, BATCH, CX, W])

        xt = two("xt", [P, 2, KD, P], F32R)
        gate = [sb(f"gate{i}", [P, DI]) for i in range(4)]
        cv = two("cv", [P, CX, P]); xc = two("xc", [P, CC, P]); bt = two("bt", [NS, P]); ct = two("ct", [NS, P])
        seg = two("seg", [P, NH, P])
        decay = sb("decay", [P, NH, P]); gm = sb("gm", [P, P]); mix = two("mix", [P, NH, P])
        b_tok = two("b_tok", [P, NS]); x_tok = two("x_tok", [P, DI]); xdt = two("xdt", [P, DI])
        xw = two("xw", [P, DI]); skip = two("skip", [P, DI])
        y1 = sb("y1", [P, DI]); y2 = sb("y2", [P, DI]); y3 = sb("y3", [P, DI]); yz = two("yz", [P, DI])
        sq = sb("sq", [P, DI]); ss = two("ss", [P, 1]); ms = two("ms", [P, 1]); rstd = two("rstd", [P, 1])
        yt = two("yt", [P, CC, P])
        res = two("res", [P, D]); out = two("out", [P, D])

        bank = [ps(f"bank{i}", [P, 512]) for i in range(8)]
        pB0 = bank[0][:].rearrange("p (c t) -> p c t", c=CC); pB1 = bank[1][:, 0:P]
        pYT = bank[0][:].rearrange("p (c t) -> p c t", c=CC); pS = bank[1][0:NS, :]
        pZ = bank[2][:]; pI = bank[2][:]
        pX = bank[3][:]
        pBT = bank[4][:, 0:NS]; pG = bank[4][:, P:2 * P]; pO = bank[4][:, 2 * P:2 * P + D]
        pD = [bank[5][:].rearrange("p (h t) -> p h t", h=4), bank[6][:].rearrange("p (h t) -> p h t", h=4)]
        pY = bank[7][:]

        loaded, made, prep, prep_pe, prep_act = sem("loaded"), sem("made"), sem("prep"), sem("prep_pe"), sem("prep_act")
        x_loaded = [sem(f"x_loaded{i}") for i in range(2)]; r_loaded = [sem(f"r_loaded{i}") for i in range(2)]
        stored = [sem(f"stored{i}") for i in range(2)]
        proj = Steps(sem("proj"), 2)
        u_kept = Steps(sem("u_kept"), 1)
        halo = Steps(sem("halo"), 1)
        conved = Steps(sem("conved"), 4)
        silu_z = Steps(sem("silu_z"), 1)
        silu = Steps(sem("silu"), 3)
        seg_p = Steps(sem("seg"), 1)
        turn = Steps(sem("turn"), 3)
        tok = Steps(sem("tok"), 4)
        tok_act = Steps(sem("tok_act"), 2)
        tok_pool = Steps(sem("tok_pool"), 2)
        scan = Steps(sem("scan"), 3)
        st_pool = Steps(sem("st_pool"), 1)
        y_dve = Steps(sem("y_dve"), 5)
        y_act = Steps(sem("y_act"), 1)
        ms_dve = Steps(sem("ms_dve"), 1); ms_pool = Steps(sem("ms_pool"), 1)
        yturn = Steps(sem("yturn"), 1); y_kept = Steps(sem("y_kept"), 1)
        outp = Steps(sem("outp"), 1); summed = Steps(sem("summed"), 1)
        nop = lambda it: None
        main = slice(0, P) if backward else slice(HALO, W)

        def tile(it):
            return it.turn * (-1 if backward else 1) + (it.lane * TB + (TB - 1 if backward else 0))

        def bc(ap, n):
            return ap.unsqueeze(2).to_broadcast([ap.shape[0], ap.shape[1], n])

        def heads(ap):
            return ap.rearrange("p (h d) -> p h d", h=NH)

        with nc.Block() as block:
            @block.sync
            def _(sp):
                sp.dma_start(w_raw[:], in_w.rearrange("(k p) e -> p k e", p=P)).then_inc(loaded, 16)
                sp.dma_start(conv[:], conv_cols.rearrange("p (c w) -> p c w", c=CX)).then_inc(loaded, 16)
                sp.dma_start(ow_raw[:], out_w.rearrange("(k p) e -> p k e", p=P)).then_inc(loaded, 16)
                sp.dma_start(norm_c[:], norm_cols).then_inc(loaded, 16)
                sp.dma_start(rows[:], head_rows.rearrange("p (v h) -> p v h", h=NH)).then_inc(loaded, 16)

            @block.gpsimd
            def _(pool):
                p = nc.gpsimd
                p.memset(upto[:], 1.0).then_inc(made, 1)
                p.memset(past[:], 1.0).then_inc(made, 1)
                p.memset(ones[:], 1.0).then_inc(made, 1)
                p.memset(state[:], 0.0).then_inc(made, 1)
                p.memset(u[:], 0.0).then_inc(made, 1)
                pool.wait_ge(made, 5)
                d = -1 if backward else 1
                p.affine_select(out=upto[:], in_=upto[:], compare_op=ALU.is_ge, fill=0.0, base=0,
                                pattern=[[d, P]], channel_multiplier=-d).then_inc(made, 1)
                p.affine_select(out=past[:], in_=past[:], compare_op=ALU.is_gt, fill=0.0, base=0,
                                pattern=[[-d, P]], channel_multiplier=d).then_inc(made, 1)

            @block.vector
            def _(dve):
                v = nc.vector
                n = [0]

                def done(i):
                    n[0] += 1
                    i.then_inc(prep, 1)
                    dve.wait_ge(prep, n[0])

                dve.wait_ge(loaded, 80)
                done(v.tensor_copy(w[0][:], w_raw[:]))
                done(v.tensor_tensor(w[1][:], w_raw[:], w[0][:].bitcast(F32), ALU.subtract))
                for c in range(CC):
                    done(v.tensor_scalar(ow[:, c, :], ow_raw[:, c, :], norm_c[:, c:c + 1], None, ALU.mult))
                row = lambda k: rows[:, k, :].unsqueeze(1).to_broadcast([P, NT, NH])
                done(v.tensor_tensor(t1[:], dt_raw[:, :, dt_col:dt_col + NH], row(0), ALU.add))
                assert n[0] == 7
                dve.wait_ge(prep_act, 2)
                done(v.tensor_scalar(grow[:], t2[:], 1.0, None, ALU.add))
                assert n[0] == 8
                done(v.tensor_scalar(dt[:], grow[:], -1.0, None, ALU.add))
                done(v.tensor_tensor(dt[:], dt[:], t2[:], ALU.subtract))
                done(v.reciprocal(fade[:], grow[:]))
                done(v.tensor_tensor(dt[:], dt[:], fade[:], ALU.mult))
                dve.wait_ge(prep_act, 3)
                done(v.tensor_tensor(dt[:], whole[:], dt[:], ALU.subtract))
                done(v.tensor_scalar(t1[:], t1[:], 0.0, None, ALU.max))
                done(v.tensor_tensor(dt[:], dt[:], t1[:], ALU.add))
                done(v.tensor_tensor(da[:], dt[:], row(1), ALU.mult))
                done(v.tensor_scalar(da[:], da[:], -1.0, None, ALU.mult))
                assert n[0] == 17

            @block.scalar
            def _(act):
                a = nc.scalar
                act.wait_ge(prep, 7)
                a.activation(t2[:], t1[:], ACT.Abs).then_inc(prep_act, 1)
                act.wait_ge(prep_act, 1)
                a.activation(t2[:], t2[:], ACT.Exp, scale=-1.0)
                a.activation(rows[:, 1, :], rows[:, 1, :], ACT.Exp).then_inc(prep_act, 1)
                act.wait_ge(prep, 8)
                a.activation(whole[:], grow[:], ACT.Ln).then_inc(prep_act, 1)
                act.wait_ge(prep_pe, 1)
                for n, to in enumerate((grow, fade, whole)):
                    a.activation(to[:].rearrange("p t h -> p (t h)"), bank[n][:], ACT.Exp).then_inc(prep_act, 1)

            @block.tensor
            def _(pe):
                pe.wait_ge(made, 7)
                pe.wait_ge(prep, 17)
                for n, m in enumerate((upto, past, ones)):
                    i = nc.tensor.matmul(bank[n][:], m[:], da[:].rearrange("p t h -> p (t h)"), start=True, stop=True)
                i.then_inc(prep_pe, 1)

        with nc.Block() as block:
            @block.sync
            def _(sp):
                def load(it):
                    row = tile(it) * P if isinstance(it.g, int) else sp.snap(tile(it) * P)
                    sp.wait_ge(proj.sem, proj.at(it.g - 2))
                    Carrier.carry(sp)
                    sp.dma_start(xt[it.s][:].bitcast(F32), xt1[bass.ds(row, P)]).then_inc(x_loaded[it.s], 16)

                def reload(it):
                    row = tile(it) * P if isinstance(it.g, int) else sp.snap(tile(it) * P)
                    sp.wait_ge(summed.sem, summed.at(it.g - 2))
                    Carrier.carry(sp)
                    sp.dma_start(res[it.s][:], res_in_d[bass.ds(row, P), :]).then_inc(r_loaded[it.s], 16)

                def store(it):
                    row = tile(it) * P if isinstance(it.g, int) else sp.snap(tile(it) * P)
                    sp.wait_ge(summed.sem, summed.at(it.g))
                    Carrier.carry(sp)
                    sp.dma_start(res_out_d[bass.ds(row, P), :], out[it.s][:]).then_inc(stored[it.s], 16)

                pipelined(sp, [load, nop, nop, nop, nop, reload, store], NT, 4)
                for s in range(2):
                    sp.wait_ge(stored[s], 16 * NT // 2)

            @block.gpsimd
            def _(pool):
                p = nc.gpsimd

                def segments(it):
                    T = tile(it)
                    pool.wait_ge(turn.sem, turn.at(it.g - 2))
                    Carrier.carry(pool)
                    p.tensor_tensor(seg[it.s][:], da[:, bass.ds(T, 1), :].rearrange("p o h -> p (o h)").unsqueeze(2).to_broadcast([P, NH, P]),
                                               upto[:].unsqueeze(1).to_broadcast([P, NH, P]), ALU.mult).then_inc(seg_p.sem, 1)

                def tokens(it):
                    T = tile(it)
                    pool.wait_ge(tok.sem, tok.at(it.g, 1))
                    Carrier.carry(pool)
                    pool.wait_ge(scan.sem, scan.at(it.g - 2))
                    Carrier.carry(pool)
                    p.tensor_tensor(heads(xw[it.s][:]), heads(xdt[it.s][:]),
                                                  fade[:, bass.ds(T, 1), :].rearrange("p o h -> p (o h)").unsqueeze(2).to_broadcast([P, NH, HD]), ALU.mult).then_inc(tok_pool.sem, 1)
                    pool.wait_ge(tok_act.sem, tok_act.at(it.g, 1))
                    Carrier.carry(pool)
                    pool.wait_ge(y_dve.sem, y_dve.at(it.g - 2))
                    Carrier.carry(pool)
                    p.tensor_tensor(heads(skip[it.s][:]), heads(x_tok[it.s][:]), bc(rows[:, 2, :], HD), ALU.mult).then_inc(tok_pool.sem, 1)

                def fade_state(it):
                    T = tile(it)
                    pool.wait_ge(y_dve.sem, y_dve.at(it.g - 2))
                    Carrier.carry(pool)
                    pool.wait_ge(y_dve.sem, y_dve.at(it.g - BATCH, 3))
                    Carrier.carry(pool)
                    p.tensor_tensor(heads(faded[it.s][:]), heads(state[:, it.lane, :]),
                                                 whole[0:NS, bass.ds(T, 1), :].rearrange("p o h -> p (o h)").unsqueeze(2).to_broadcast([NS, NH, HD]), ALU.mult).then_inc(st_pool.sem, 1)

                def root(it):
                    pool.wait_ge(ms_dve.sem, ms_dve.at(it.g))
                    pool.wait_ge(summed.sem, summed.at(it.g - 2))
                    p.tensor_tensor(rstd[it.s][:], ms[it.s][:], env.neg_half[:, 0:1], ALU.pow).then_inc(ms_pool.sem, 1)

                for stage in (seg_p, tok_pool, st_pool, ms_pool):
                    stage.open(pool)
                pipelined(pool, [nop, nop, segments, tokens, fade_state, root, nop], NT, 4)

            @block.vector
            def _(dve):
                v = nc.vector

                def convolve(it):
                    T_u = u[:, it.lane]
                    dve.wait_ge(u_kept.sem, u_kept.at(it.g))
                    dve.wait_ge(silu.sem, silu.at(it.g - 2))
                    for k in range(TAPS):
                        off = HALO - k if backward else k
                        for c in range(CX):
                            src = T_u[:, c, off:off + P]
                            if k == 0:
                                i = v.tensor_scalar(cv[it.s][:, c, :], src, conv[:, c, 0:1], conv[:, c, TAPS:TAPS + 1], ALU.mult, ALU.add)
                            else:
                                i = v.scalar_tensor_tensor(out=cv[it.s][:, c, :], in0=src, scalar=conv[:, c, k:k + 1],
                                                           in1=cv[it.s][:, c, :], op0=ALU.mult, op1=ALU.add)
                        i.then_inc(conved.sem, 1)
                        dve.wait_ge(conved.sem, conved.at(it.g, k + 1))

                def tokens(it):
                    T = tile(it)
                    dve.wait_ge(tok_act.sem, tok_act.at(it.g, 1))
                    dve.wait_ge(tok_pool.sem, tok_pool.at(it.g - 2))
                    dve.wait_ge(scan.sem, scan.at(it.g - 2))
                    v.tensor_tensor(heads(xdt[it.s][:]), heads(x_tok[it.s][:]), dt[:, bass.ds(T, 1), :].rearrange("p o h -> p (o h)").unsqueeze(2).to_broadcast([P, NH, HD]), ALU.mult).then_inc(tok.sem, 1)
                    dve.wait_ge(turn.sem, turn.at(it.g, 3))
                    v.tensor_copy(b_tok[it.s][:], pBT).then_inc(tok.sem, 1)
                    v.tensor_tensor(gm[:], pG, upto[:], ALU.mult).then_inc(tok.sem, 1)
                    dve.wait_ge(tok.sem, tok.at(it.g, 3))
                    dve.wait_ge(tok_act.sem, tok_act.at(it.g, 2))
                    v.tensor_tensor(mix[it.s][:], decay[:], gm[:].unsqueeze(1).to_broadcast([P, NH, P]), ALU.mult).then_inc(tok.sem, 1)

                def outputs(it):
                    T = tile(it)
                    dve.wait_ge(scan.sem, scan.at(it.g, 1))
                    v.tensor_tensor(heads(y1[:]), heads(pI), grow[:, bass.ds(T, 1), :].rearrange("p o h -> p (o h)").unsqueeze(2).to_broadcast([P, NH, HD]), ALU.mult).then_inc(y_dve.sem, 1)
                    dve.wait_ge(y_dve.sem, y_dve.at(it.g, 1))
                    dve.wait_ge(scan.sem, scan.at(it.g, 2))
                    v.tensor_tensor(y2[:], pY, y1[:], ALU.add).then_inc(y_dve.sem, 1)
                    dve.wait_ge(scan.sem, scan.at(it.g, 3))
                    dve.wait_ge(st_pool.sem, st_pool.at(it.g))
                    v.tensor_tensor(state[:, it.lane, :], pS, faded[it.s][:], ALU.add).then_inc(y_dve.sem, 1)
                    dve.wait_ge(y_dve.sem, y_dve.at(it.g, 3))
                    dve.wait_ge(tok_pool.sem, tok_pool.at(it.g))
                    v.tensor_tensor(y3[:], y2[:], skip[it.s][:], ALU.add).then_inc(y_dve.sem, 1)
                    dve.wait_ge(y_dve.sem, y_dve.at(it.g, 4))
                    dve.wait_ge(yturn.sem, yturn.at(it.g - 2))
                    dve.wait_ge(y_act.sem, y_act.at(it.g - 2))
                    v.tensor_tensor(yz[it.s][:], y3[:], gate[it.lane][:], ALU.mult).then_inc(y_dve.sem, 1)

                def mean_square(it):
                    dve.wait_ge(y_act.sem, y_act.at(it.g))
                    dve.wait_ge(ms_pool.sem, ms_pool.at(it.g - 2))
                    v.tensor_scalar(ms[it.s][:], ss[it.s][:], 1.0 / DI, EPS, ALU.mult, ALU.add).then_inc(ms_dve.sem, 1)

                def add_out(it):
                    dve.wait_ge(outp.sem, outp.at(it.g))
                    dve.wait_ge(ms_pool.sem, ms_pool.at(it.g))
                    dve.wait_ge(r_loaded[it.s], it.q * 16 + 16)
                    if it.again:
                        dve.wait_ge(stored[it.s], it.q * 16)
                    v.scalar_tensor_tensor(out=out[it.s][:], in0=pO, scalar=rstd[it.s][:], in1=res[it.s][:], op0=ALU.mult, op1=ALU.add).then_inc(summed.sem, 1)

                for stage in (conved, tok, y_dve, ms_dve, summed):
                    stage.open(dve)
                pipelined(dve, [nop, nop, convolve, tokens, outputs, mean_square, add_out], NT, 4)

            @block.scalar
            def _(act):
                a = nc.scalar

                def keep(it):
                    T_u = u[:, it.lane]
                    act.wait_ge(conved.sem, conved.at(it.g - BATCH))
                    frm, to = (slice(0, HALO), slice(P, W)) if backward else (slice(P, W), slice(0, HALO))
                    a.activation(T_u[:, :, to], T_u[:, :, frm], ACT.Copy).then_inc(halo.sem, 1)
                    act.wait_ge(halo.sem, halo.at(it.g, 1))
                    act.wait_ge(proj.sem, proj.at(it.g, 1))
                    a.activation(T_u[:, 0:CC, main], pB0, ACT.Copy)
                    a.activation(T_u[:, CC, main], pB1, ACT.Copy).then_inc(u_kept.sem, 1)

                def project(it):
                    keep(it)
                    act.wait_ge(proj.sem, proj.at(it.g, 2))
                    act.wait_ge(y_dve.sem, y_dve.at(it.g - 4))
                    a.activation(gate[it.lane][:], pZ, ACT.Silu).then_inc(silu_z.sem, 1)

                def activate(it):
                    act.wait_ge(conved.sem, conved.at(it.g))
                    act.wait_ge(turn.sem, turn.at(it.g - 2))
                    act.wait_ge(scan.sem, scan.at(it.g - 2))
                    a.activation(xc[it.s][:], cv[it.s][:, 0:CC, :], ACT.Silu).then_inc(silu.sem, 1)
                    a.activation(bt[it.s][:], cv[it.s][0:NS, CC, :], ACT.Silu).then_inc(silu.sem, 1)
                    a.activation(ct[it.s][:], cv[it.s][NS:P, CC, :], ACT.Silu).then_inc(silu.sem, 1)

                def tokens(it):
                    act.wait_ge(turn.sem, turn.at(it.g, 2))
                    act.wait_ge(tok_pool.sem, tok_pool.at(it.g - 2))
                    act.wait_ge(tok.sem, tok.at(it.g - 2))
                    a.activation(x_tok[it.s][:], pX, ACT.Copy).then_inc(tok_act.sem, 1)
                    act.wait_ge(turn.sem, turn.at(it.g, 1))
                    act.wait_ge(tok.sem, tok.at(it.g - 1))
                    for half in range(2):
                        i = a.activation(decay[:, half * 4:half * 4 + 4, :], pD[half], ACT.Exp)
                    i.then_inc(tok_act.sem, 1)

                def square(it):
                    act.wait_ge(y_dve.sem, y_dve.at(it.g))
                    act.wait_ge(ms_dve.sem, ms_dve.at(it.g - 2))
                    a.activation(sq[:], yz[it.s][:], ACT.Square, accum_out=ss[it.s][:]).then_inc(y_act.sem, 1)

                def keep_turned(it):
                    act.wait_ge(yturn.sem, yturn.at(it.g))
                    act.wait_ge(outp.sem, outp.at(it.g - 2))
                    a.activation(yt[it.s][:], pYT, ACT.Copy).then_inc(y_kept.sem, 1)

                for stage in (u_kept, halo, silu_z, silu, tok_act, y_act, y_kept):
                    stage.open(act)
                pipelined(act, [nop, project, activate, tokens, square, keep_turned, nop], NT, 4)

            @block.tensor
            def _(pe):
                t_ = nc.tensor

                def cap(g):
                    return min(g, NT - 1) if isinstance(g, int) else g

                def project(it):
                    pe.wait_ge(x_loaded[it.s], it.q * 16 + 16)
                    pe.wait_ge(y_kept.sem, y_kept.at(it.g - 4))
                    pe.wait_ge(y_dve.sem, y_dve.at(it.g - 3, 3))
                    pe.wait_ge(u_kept.sem, u_kept.at(it.g - 1))
                    for c in range(CX):
                        n = 0
                        for k in range(KD):
                            for i, j in PARTS:
                                last = t_.matmul(pB0[:, c, :] if c < CC else pB1, w[i][:, k, DI + c * P:DI + (c + 1) * P],
                                                 xt[it.s][:, j, k, :], start=(n == 0), stop=(n == 5))
                                n += 1
                    last.then_inc(proj.sem, 1)
                    pe.wait_ge(silu_z.sem, silu_z.at(it.g - 1))
                    n = 0
                    for k in range(KD):
                        for i, j in PARTS:
                            last = t_.matmul(pZ, xt[it.s][:, i, k, :], w[j][:, k, 0:DI], start=(n == 0), stop=(n == 5))
                            n += 1
                    last.then_inc(proj.sem, 1)

                def tokens(it):
                    pe.wait_ge(seg_p.sem, seg_p.at(it.g))
                    pe.wait_ge(tok_act.sem, tok_act.at(it.g - 1))
                    for half in range(2):
                        i = t_.matmul(pD[half], past[:], seg[it.s][:, half * 4:half * 4 + 4, :], start=True, stop=True)
                    i.then_inc(turn.sem, 1)
                    pe.wait_ge(silu.sem, silu.at(it.g))
                    pe.wait_ge(tok_act.sem, tok_act.at(it.g - 1))
                    for c in range(CC):
                        i = t_.transpose(pX[:, c * P:(c + 1) * P], xc[it.s][:, c, :], env.ident[:])
                    i.then_inc(turn.sem, 1)
                    pe.wait_ge(summed.sem, summed.at(it.g - 3))
                    pe.wait_ge(tok.sem, tok.at(it.g - 1, 3))
                    t_.matmul(pG, bt[it.s][:], ct[it.s][:], start=True, stop=True)
                    t_.transpose(pBT, bt[it.s][:], env.ident[0:NS, 0:NS]).then_inc(turn.sem, 1)

                def scans(it):
                    pe.wait_ge(y_dve.sem, y_dve.at(it.g - BATCH, 3))
                    pe.wait_ge(silu_z.sem, silu_z.at(cap(it.g + 2)))
                    t_.matmul(pI, ct[it.s][:], state[:, it.lane, :], start=True, stop=True).then_inc(scan.sem, 1)
                    pe.wait_ge(tok.sem, tok.at(it.g))
                    pe.wait_ge(y_dve.sem, y_dve.at(it.g - 1, 2))
                    for h in range(NH):
                        i = t_.matmul(pY[:, h * HD:(h + 1) * HD], mix[it.s][:, h, :], xdt[it.s][:, h * HD:(h + 1) * HD], start=True, stop=True)
                    i.then_inc(scan.sem, 1)
                    pe.wait_ge(tok_pool.sem, tok_pool.at(it.g, 1))
                    pe.wait_ge(u_kept.sem, u_kept.at(cap(it.g + 2)))
                    t_.matmul(pS, b_tok[it.s][:], xw[it.s][:], start=True, stop=True).then_inc(scan.sem, 1)

                def turn_y(it):
                    pe.wait_ge(y_dve.sem, y_dve.at(it.g))
                    pe.wait_ge(u_kept.sem, u_kept.at(cap(it.g + 3)))
                    for c in range(CC):
                        i = t_.transpose(pYT[:, c, :], yz[it.s][:, c * P:(c + 1) * P], env.ident[:])
                    i.then_inc(yturn.sem, 1)

                def project_out(it):
                    pe.wait_ge(y_kept.sem, y_kept.at(it.g))
                    pe.wait_ge(summed.sem, summed.at(it.g - 1))
                    pe.wait_ge(tok.sem, tok.at(cap(it.g + 2), 3))
                    for c in range(CC):
                        i = t_.matmul(pO, yt[it.s][:, c, :], ow[:, c, :], start=(c == 0), stop=(c == CC - 1))
                    i.then_inc(outp.sem, 1)

                for stage in (proj, turn, scan, yturn, outp):
                    stage.open(pe)
                pipelined(pe, [nop, project, nop, tokens, scans, turn_y, project_out], NT, 4)


ZERO_ROWS = 8


def program(nc, x, attn_w, router_w, cols0, bo_rows, rb_rows, w_fc, w_gate, w_proj, e_cols, e_rows, head_w,
            f_in, f_conv, f_out, f_norm, f_heads, b_in, b_conv, b_out, b_norm, b_heads, w_experts, final):
    NT = T // P
    rows_l0, rows_l1 = E0 * ROWS0, E1 * CAP1

    def dram(name, shape):
        return nc.dram_tensor("dram_" + name, shape, F32, kind="Internal").ap()

    xn0, res0, res1, res2, xn1 = (dram(n, [T, D]) for n in ("xn0", "res0", "res1", "res2", "xn1"))
    res3 = dram("res3", [T, D])
    xt1 = dram("xt1", [T, 2, KD, P])
    buf0, buf1 = dram("buf0", [rows_l0 + 2 * T, D]), dram("buf1", [rows_l1 + T, D])
    out0, out1 = dram("out0", [rows_l0, D]), dram("out1", [rows_l1, D])

    env = Env(nc)
    with ExitStack() as outer:
        keep = lambda n, s, d=F32: outer.enter_context(nc.sbuf_tensor(n, s, d))
        Carrier.sem = nc.alloc_semaphore("carrier")
        zeroed = nc.alloc_semaphore("zeroed")
        env.ident, env.neg_half = keep("ident", [P, P]), keep("neg_half", [P, 4])
        env.logits = keep("logits0", [P, NT, 8])
        logits1, dt_raw = keep("logits1", [P, NT, E1]), keep("dt_raw", [P, NT, 2 * NH])
        picks0 = [Pick(keep, f"pick0_{k}", NT) for k in range(2)]
        picks1 = [Pick(keep, "pick1", NT)]
        with nc.sbuf_tensor("zeros", [P, ZERO_ROWS * D], F32) as zeros:
            with env.phase(), ExitStack() as ctx:
                setup_l0(nc, env, ctx, attn_w, router_w, cols0, bo_rows, rb_rows)
                zero_buffers(nc, env, zeros, zeroed, ((buf0, rows_l0), (buf1, rows_l1)))
                tokens_l0(nc, env, x, xn0, res0)
            with env.phase():
                route(nc, env, "r0", env.logits, E0, 2, BATCH, CAP0, ROWS0, rows_l0, picks0)
            with nc.Block() as block:
                @block.gpsimd
                def _(pool):
                    pool.wait_ge(zeroed, 16 * (rows_l0 + rows_l1) // (P * ZERO_ROWS))
        with env.phase():
            scatter(nc, env, "s0", xn0, buf0, picks0, NT)
        with env.phase():
            experts_l0(nc, env, buf0, out0, w_fc, w_gate, w_proj, e_cols, e_rows)
        with env.phase():
            combine_l0(nc, env, out0, picks0, res0, res1, xn1, xt1, head_w, logits1, dt_raw, NT)
        with env.phase():
            route(nc, env, "r1", logits1, E1, 1, 1, CAP1, CAP1, rows_l1, picks1)
        with env.phase():
            scatter(nc, env, "s1", xn1, buf1, picks1, NT)
        with env.phase():
            experts_l1(nc, env, buf1, out1, w_experts)
        with env.phase():
            mixer(nc, env, "mf", False, f_in, f_conv, f_out, f_norm, f_heads, dt_raw, 0, xt1, res1, res2)
        with env.phase():
            mixer(nc, env, "mb", True, b_in, b_conv, b_out, b_norm, b_heads, dt_raw, NH, xt1, res2, res3)
        with env.phase():
            combine_l1(nc, env, out1, picks1[0], res3, final, NT)


class Env:

    def __init__(self, nc):
        self.nc = nc

    def phase(self):
        return self.nc.cleanup_on_exit()

    def sem(self, name):
        return self.nc.alloc_semaphore(name)


def zero_buffers(nc, env, zeros, zeroed, buffers):
    filled = env.sem("zeros_filled")
    with nc.Block() as block:
        @block.gpsimd
        def _(pool):
            nc.gpsimd.memset(zeros[:], 0.0).then_inc(filled, 1)

        @block.sync
        def _(sp):
            sp.wait_ge(filled, 1)
            for buf, rows in buffers:
                blocks = buf[0:rows, :].rearrange("(n p r) d -> n p (r d)", p=P, r=ZERO_ROWS)
                with sp.Fori(0, rows // (P * ZERO_ROWS)) as i:
                    sp.dma_start(blocks[bass.ds(i, 1)].rearrange("o p c -> p (o c)"), zeros[:]).then_inc(zeroed, 16)



def _laid_out(i):
    import numpy as np

    p0, p1 = "L0_attn_", "L0_ffn_"

    def columns(a):
        return a.reshape(-1, P).T

    out = {
        "x": i[p0 + "x"].reshape(T, D),
        "attn_w": np.stack([i[p0 + n].T for n in ("Wk", "Wq", "Wv", "Wkp", "Wqp", "Wo")]),
        "router_w": i[p1 + "router_w"],
        "cols0": np.concatenate([columns(i[p0 + n]) for n in ("bk", "bq", "bv", "bkp", "bqp", "phase_scale", "ln_g", "ln_b")], 1),
        "bo_rows": np.tile(i[p0 + "bo"], (P, 1)),
        "rb_rows": np.tile(i[p1 + "router_b"], (P, 1)),
        "w_fc": i[p1 + "w_c_fc"], "w_gate": i[p1 + "w_gate"], "w_proj": i[p1 + "w_c_proj"],
        "e_cols": np.concatenate([columns(i[p1 + "b_c_fc"]), columns(i[p1 + "b_gate"])], 1),
        "e_rows": np.tile(i[p1 + "b_c_proj"].reshape(1, -1), (P, 1)),
        "head_w": np.concatenate([i["L1_ffn_w_router"]] + [i[f"L1_attn_{d}_in_w"][-NH:].T for d in "fb"], 1),
    }
    for d in "fb":
        q = f"L1_attn_{d}_"
        conv = np.concatenate([i[q + "conv_w"], i[q + "conv_b"][:, None]], 1)
        out[d + "_in"] = i[q + "in_w"][:-NH].T
        out[d + "_conv"] = conv.reshape(CX, P, TAPS + 1).transpose(1, 0, 2).reshape(P, -1)
        out[d + "_out"] = i[q + "out_w"].T
        out[d + "_norm"] = columns(i[q + "norm_w"])
        out[d + "_heads"] = np.tile(np.concatenate([i[q + n] for n in ("dt_bias", "A_log", "Dp")]), (P, 1))
    out["w_experts"] = np.stack([i["L1_ffn_" + n] for n in ("w_gate", "w_up", "w_down")], 1)
    return {n: np.ascontiguousarray(a) for n, a in out.items()}


def kernel(**inputs):
    import numpy as _np
    import concourse.bacc as _bacc
    from concourse.bass_utils import run_bass_kernel_spmd as _run

    nc = _bacc.Bacc("TRN2", target_bir_lowering=False, num_devices=1)
    laid = _laid_out({n: _np.asarray(a) for n, a in inputs.items()})
    arrays, args = {}, []
    for name, a in laid.items():
        arrays[f"in_{name}"] = a
        args.append(nc.dram_tensor(f"in_{name}", a.shape, mybir.dt.from_np(a.dtype), kind="ExternalInput").ap())
    args.append(nc.dram_tensor("final", (T, D), F32, kind="ExternalOutput").ap())
    program(nc, *args)
    r = _run(nc, [arrays], core_ids=[0])
    return r.results[0]["final"].reshape(BATCH, SEQ, D)
```

```python
import concourse.bass as bass
from concourse import mybir
from contextlib import ExitStack

F32 = mybir.dt.float32
F32R = mybir.dt.float32r
U32 = mybir.dt.uint32
ALU = mybir.AluOpType
ACT = mybir.ActivationFunctionType
AX = mybir.AxisListType.X


class Item:

    def __init__(self, c, r=None, unroll=2):
        self.g = c if r is None else r * unroll + c
        self.s = c % 2
        self.q = c // 2 if r is None else r * (unroll // 2) + c // 2
        self.lane = c % unroll
        self.turn = c // unroll if r is None else r + c // unroll
        self.again = r is not None or c >= 2
        self.again_lane = r is not None or c >= unroll


class Carrier:

    sem = None

    @classmethod
    def carry(cls, eng):
        eng.sem_inc(cls.sem, 1)


def pipelined(eng, depth, items, unroll, *stages):
    head = depth + 1
    rounds = (items - head) // unroll

    def step(base, r):
        for lag, stage in stages:
            c = base - lag
            if r is not None or 0 <= c < items:
                stage(Item(c, r, unroll))

    for t in range(head):
        step(t, None)
    with eng.Fori(0, rounds) as r:
        for u in range(unroll):
            step(head + u, r)
    for t in range(head + unroll * rounds, items + depth - 1):
        step(t, None)


class Steps:

    AHEAD = 4

    def __init__(self, sem, per):
        self.sem, self.per = sem, per
        self.credit = self.AHEAD * per + 1

    def open(self, eng):
        eng.sem_inc(self.sem, self.credit)

    def at(self, g, k=None):
        return g * self.per + ((self.per if k is None else k) + self.credit)


def at_row(eng, it, rows):
    return it.g * rows if isinstance(it.g, int) else eng.snap(it.g * rows)


import math

T, D, P = 8192, 256, 128
NT = T // P
KD = D // P
INV_2PI = 1.0 / (2.0 * math.pi)
ROUND = 1.5 * 2.0 ** 23
TWO_PI_HI = 6.28125
TWO_PI_LO = 2.0 * math.pi - TWO_PI_HI
PI_BELOW = 3.1415925
HALF_PI = math.pi / 2
CHUNK = 64
EPS = 1e-5
ZERO_ROWS = 5


PARTS = ((0, 0), (0, 1), (1, 0))


def setup_l0(nc, env, ctx, attn_w, router_w, cols0, bo_rows, rb_rows):
    sb, sem = lambda n, s, d=F32: ctx.enter_context(nc.sbuf_tensor(n, s, d)), env.sem
    env.half_pi = sb("half_pi", [P, 1])
    env.cols = sb("cols", [P, 8, KD])
    env.scale4 = sb("scale4", [P, 4])
    env.bo_rows = sb("bo_rows", [P, D])
    env.rb_rows = sb("rb_rows", [P, 8])
    env.seg = sb("seg", [P, D])
    env.wraw = sb("wraw", [P, 6, KD, D])
    env.w = [sb("w_hi", [P, 6, KD, D], F32R), sb("w_lo", [P, 6, KD, D], F32R)]
    env.rwraw = sb("rwraw", [P, KD, 8])
    env.rw = [sb("rw_hi", [P, KD, 8], F32R), sb("rw_lo", [P, KD, 8], F32R)]
    loaded, pool_done, dve_done = sem("const_loaded"), sem("const_pool"), sem("const_dve")
    with nc.Block() as block:
        @block.sync
        def _(sp):
            sp.dma_start(env.wraw[:], attn_w.rearrange("w (k p) e -> p w k e", p=P)).then_inc(loaded, 16)
            sp.dma_start(env.rwraw[:], router_w.rearrange("(k p) e -> p k e", p=P)).then_inc(loaded, 16)
            sp.dma_start(env.cols[:], cols0.rearrange("p (v k) -> p v k", k=KD)).then_inc(loaded, 16)
            sp.dma_start(env.bo_rows[:], bo_rows).then_inc(loaded, 16)
            sp.dma_start(env.rb_rows[:], rb_rows).then_inc(loaded, 16)

        @block.gpsimd
        def _(pool):
            nc.gpsimd.memset(env.ident[:], 0.0).then_inc(pool_done, 1)
            pool.wait_ge(pool_done, 1)
            nc.gpsimd.affine_select(out=env.ident[:], in_=env.ident[:], compare_op=ALU.not_equal, fill=1.0,
                                    base=0, pattern=[[-1, P]], channel_multiplier=1).then_inc(pool_done, 1)

        @block.vector
        def _(dve):
            nc.vector.memset(env.neg_half[:], -0.5)
            nc.vector.memset(env.seg[:], 1.0).then_inc(dve_done, 1)
            nc.vector.memset(env.half_pi[:], HALF_PI)
            dve.wait_ge(dve_done, 1)
            nc.vector.memset(env.seg[:].rearrange("p (c t) -> p c t", t=CHUNK)[:, :, 0:1], 0.0).then_inc(dve_done, 1)
            dve.wait_ge(loaded, 80)
            nc.vector.tensor_copy(env.w[0][:], env.wraw[:]).then_inc(dve_done, 1)
            nc.vector.tensor_copy(env.rw[0][:], env.rwraw[:]).then_inc(dve_done, 1)
            for n in range(2):
                nc.vector.tensor_copy(env.scale4[:, n * KD:(n + 1) * KD], env.cols[:, 5, :])
            nc.vector.tensor_scalar(env.cols[:, 2, :], env.cols[:, 2, :], 1.0 / math.sqrt(D), None, ALU.mult).then_inc(dve_done, 1)
            dve.wait_ge(dve_done, 5)
            nc.vector.tensor_tensor(env.w[1][:], env.wraw[:], env.w[0][:].bitcast(F32), ALU.subtract).then_inc(dve_done, 1)
            nc.vector.tensor_tensor(env.rw[1][:], env.rwraw[:], env.rw[0][:].bitcast(F32), ALU.subtract).then_inc(dve_done, 1)
            dve.wait_ge(dve_done, 7)


BK, BQ, BV, BKP, BQP, PSC, LNG, LNB = range(8)
WK, WQ, WV, WKP, WQP, WO = range(6)


def tokens_l0(nc, env, x, xn0, res0, buffers):
    G = 2 * P
    ITEMS = T // G
    with ExitStack() as ctx:
        sb = lambda n, s, d=F32: ctx.enter_context(nc.sbuf_tensor(n, s, d))
        ps = lambda n, s, d=F32: ctx.enter_context(nc.psum_tensor(n, s, d))
        sem = env.sem
        two = lambda n, s, d=F32: [sb(f"{n}{i}", s, d) for i in range(2)]
        x_in = two("x_in", [P, 2, D])
        stats = sb("stats", [P, 2, 6]); mv = sb("mv", [P, 2, 2]); var = sb("var", [P, 2]); rstd = sb("rstd", [P, 2])
        xn = two("xn", [P, 2, D])
        res = two("res", [P, 2, D]); res_t = sb("res_t", [P, 2, D])
        xt = [two("xt_hi", [P, KD, G], F32R), two("xt_lo", [P, KD, G], F32R)]
        kq = [two("kq_hi", [P, 4, G], F32R), two("kq_lo", [P, 4, G], F32R)]
        val = [sb(f"val{i}", [P, KD, G]) for i in range(4)]
        ph = two("ph", [P, 4, G]); turns = sb("turns", [P, 4, G]); ang = sb("ang", [P, 4, G])
        sin = two("sin", [P, 4, G]); cos = two("cos", [P, 4, G])
        apart = sb("apart", [P, 4, G])
        bound = sb("bound", [P, 4, G]); mem = sb("mem", [P, 4, G]); ret = two("ret", [P, KD, G])
        prod = sb("prod", [P, 4, G])
        stats2 = sb("stats2", [P, 2, 6]); mv2 = sb("mv2", [P, 2, 2]); var2 = sb("var2", [P, 2]); rstd2 = sb("rstd2", [P, 2])
        zt = two("zt", [P, 2, D])
        zf = sb("zf", [P, KD, G])
        z = [two("z_hi", [P, KD, G], F32R), two("z_lo", [P, KD, G], F32R)]
        res_in = two("res_in", [P, 2, D]); res_out = two("res_out", [P, 2, D])
        pT = ps("pT", [P, KD, G]); pK = ps("pK", [P, KD, G]); pQ = ps("pQ", [P, KD, G]); pC = ps("pC", [P, KD, G])
        pE = ps("pE", [P, 2, D]); pF = ps("pF", [P, KD, G]); pG = ps("pG", [P, 2, D]); pL = ps("pL", [P, 2, 8])

        shares = [n // ITEMS for _, n in buffers]
        zeros = sb("zeros", [P, ZERO_ROWS * D]); zeroed, zeros_set = sem("zeroed"), sem("zeros_set")
        x_loaded = [sem(f"x_loaded{i}") for i in range(2)]
        r_loaded = [sem(f"r_loaded{i}") for i in range(2)]
        xn_stored, res_stored, out_stored = ([sem(f"{n}{i}") for i in range(2)] for n in ("xn_stored", "res_stored", "out_stored"))
        norm = Steps(sem("norm_dve"), 7)
        low = Steps(sem("x_low"), 1)
        norm_pool = Steps(sem("norm_pool"), 3)
        turned = Steps(sem("x_turned"), 1)
        high = Steps(sem("x_high"), 1)
        projected = Steps(sem("projected"), 4)
        proj_act = Steps(sem("proj_act"), 3)
        proj_dve = Steps(sem("proj_dve"), 3)
        phased = Steps(sem("phase_pe"), 2)
        tanhs = Steps(sem("tanhs"), 2)
        scaled = Steps(sem("scaled"), 1)
        ph_dve = Steps(sem("phase_dve"), 5)
        sines = Steps(sem("sines"), 3)
        bound_p = Steps(sem("bound_pool"), 2)
        mem_dve = Steps(sem("memory_dve"), 7)
        back = Steps(sem("ret_turned"), 1)
        ln_dve = Steps(sem("ln_dve"), 7)
        ln_pool = Steps(sem("ln_pool"), 1)
        z_turned = Steps(sem("z_turned"), 1)
        z_act = Steps(sem("z_act"), 1)
        z_dve = Steps(sem("z_dve"), 1)
        z_pool = Steps(sem("z_pool"), 1)
        out_pe = Steps(sem("out_pe"), 1)
        out_dve = Steps(sem("out_dve"), 1)

        def rows(ap, row):
            return ap[bass.ds(row, G), :].rearrange("(t p) d -> p t d", p=P)

        with nc.Block() as block:
            @block.sync
            def _(sp):
                def load(it):
                    row = at_row(sp, it, G)
                    sp.wait_ge(norm.sem, norm.at(it.g - 2, 7))
                    Carrier.carry(sp)
                    sp.wait_ge(norm_pool.sem, norm_pool.at(it.g - 2, 2))
                    Carrier.carry(sp)
                    sp.dma_start(x_in[it.s][:], rows(x, row)).then_inc(x_loaded[it.s], 16)

                def store(it):
                    row = at_row(sp, it, G)
                    sp.wait_ge(norm.sem, norm.at(it.g, 7))
                    Carrier.carry(sp)
                    sp.dma_start(rows(xn0, row), xn[it.s][:]).then_inc(xn_stored[it.s], 16)
                    sp.wait_ge(norm_pool.sem, norm_pool.at(it.g, 3))
                    Carrier.carry(sp)
                    sp.dma_start(rows(res0, row), res[it.s][:]).then_inc(res_stored[it.s], 16)

                def reload(it):
                    row = at_row(sp, it, G)
                    sp.wait_ge(out_dve.sem, out_dve.at(it.g - 2))
                    Carrier.carry(sp)
                    sp.wait_ge(res_stored[it.s], 16 * it.q + 16)
                    Carrier.carry(sp)
                    sp.dma_start(res_in[it.s][:], rows(res0, row)).then_inc(r_loaded[it.s], 16)

                def zero(it):
                    for (buf, _), share in zip(buffers, shares):
                        row = it.g * share if isinstance(it.g, int) else sp.snap(it.g * share)
                        part = share // ZERO_ROWS
                        sp.dma_start(buf[bass.ds(row, share), :].rearrange("(p r) d -> p (r d)", r=ZERO_ROWS), zeros[0:part, :]).then_inc(zeroed, 16)

                def finish(it):
                    row = at_row(sp, it, G)
                    sp.wait_ge(out_dve.sem, out_dve.at(it.g))
                    Carrier.carry(sp)
                    sp.dma_start(rows(res0, row), res_out[it.s][:]).then_inc(out_stored[it.s], 16)

                sp.wait_ge(zeros_set, 1)
                pipelined(sp, 8, ITEMS, 4, (6, reload), (0, load), (1, store), (7, finish), (0, zero))
                sp.wait_ge(zeroed, 16 * len(buffers) * ITEMS)
                for s in range(2):
                    sp.wait_ge(xn_stored[s], 16 * ITEMS // 2)
                    sp.wait_ge(out_stored[s], 16 * ITEMS // 2)

            @block.vector
            def _(dve):
                v = nc.vector
                v.memset(zeros[:], 0.0).then_inc(zeros_set, 1)

                def normalise(it):
                    dve.wait_ge(x_loaded[it.s], 16 * it.q + 16)
                    dve.wait_ge(norm_pool.sem, norm_pool.at(it.g - 1, 1))
                    for t in range(2):
                        v.bn_stats(stats[:, t, :], x_in[it.s][:, t, :]).then_inc(norm.sem, 1)
                    dve.wait_ge(norm.sem, norm.at(it.g, 2))
                    Carrier.carry(dve)
                    for t in range(2):
                        v.bn_aggr(mv[:, t, :], stats[:, t, :]).then_inc(norm.sem, 1)
                    dve.wait_ge(norm.sem, norm.at(it.g, 4))
                    v.tensor_scalar(var[:], mv[:, :, 1], EPS, None, ALU.add).then_inc(norm.sem, 1)

                def center(it):
                    dve.wait_ge(norm_pool.sem, norm_pool.at(it.g, 1))
                    if it.again:
                        dve.wait_ge(xn_stored[it.s], 16 * it.q)
                    dve.wait_ge(turned.sem, turned.at(it.g - 2))
                    dve.wait_ge(norm_pool.sem, norm_pool.at(it.g - 2))
                    for t in range(2):
                        v.tensor_scalar(xn[it.s][:, t, :], x_in[it.s][:, t, :], mv[:, t, 0:1], rstd[:, t:t + 1],
                                                  ALU.subtract, ALU.mult).then_inc(norm.sem, 1)

                def x_low(it):
                    dve.wait_ge(high.sem, high.at(it.g))
                    dve.wait_ge(projected.sem, projected.at(it.g - 2))
                    v.tensor_tensor(xt[1][it.s][:], pT[:], xt[0][it.s][:].bitcast(F32), ALU.subtract).then_inc(low.sem, 1)

                def project(it):
                    for n, (bank, bias) in enumerate(((pK, BK), (pQ, BQ))):
                        dve.wait_ge(proj_act.sem, proj_act.at(it.g, n + 1))
                        dve.wait_ge(phased.sem, phased.at(it.g - 2))
                        for c in range(KD):
                            i = v.scalar_tensor_tensor(out=kq[1][it.s][:, 2 * n + c, :], in0=bank[:, c, :],
                                                       scalar=env.cols[:, bias, c:c + 1],
                                                       in1=kq[0][it.s][:, 2 * n + c, :].bitcast(F32), op0=ALU.add, op1=ALU.subtract)
                        i.then_inc(proj_dve.sem, 1)
                    dve.wait_ge(projected.sem, projected.at(it.g, 3))
                    for t in range(2):
                        i = v.tensor_tensor(env.logits[:, bass.ds(it.g * 2 + t, 1), :] if not isinstance(it.g, int) else
                                            env.logits[:, it.g * 2 + t:it.g * 2 + t + 1, :],
                                            pL[:, t:t + 1, :], env.rb_rows[:].rearrange("p (o e) -> p o e", o=1), ALU.add)
                    i.then_inc(proj_dve.sem, 1)

                def phase(it):
                    dve.wait_ge(scaled.sem, scaled.at(it.g))
                    v.tensor_scalar(turns[:], ph[it.s][:], INV_2PI, ROUND, ALU.mult, ALU.add).then_inc(ph_dve.sem, 1)
                    dve.wait_ge(ph_dve.sem, ph_dve.at(it.g, 1))
                    v.tensor_scalar(turns[:], turns[:], ROUND, None, ALU.subtract).then_inc(ph_dve.sem, 1)
                    dve.wait_ge(ph_dve.sem, ph_dve.at(it.g, 2))
                    v.scalar_tensor_tensor(out=ph[it.s][:], in0=turns[:], scalar=-TWO_PI_HI, in1=ph[it.s][:], op0=ALU.mult, op1=ALU.add).then_inc(ph_dve.sem, 1)
                    dve.wait_ge(ph_dve.sem, ph_dve.at(it.g, 3))
                    v.scalar_tensor_tensor(out=ph[it.s][:], in0=turns[:], scalar=-TWO_PI_LO, in1=ph[it.s][:], op0=ALU.mult, op1=ALU.add).then_inc(ph_dve.sem, 1)
                    dve.wait_ge(ph_dve.sem, ph_dve.at(it.g, 4))
                    dve.wait_ge(sines.sem, sines.at(it.g - 1))
                    v.tensor_scalar(ang[:], ph[it.s][:], PI_BELOW, -PI_BELOW, ALU.min, ALU.max).then_inc(ph_dve.sem, 1)

                def memory(it):
                    for n in range(2):
                        dve.wait_ge(bound_p.sem, bound_p.at(it.g, n + 1))
                        for c in range(KD):
                            v.tensor_tensor_scan(mem[:, 2 * n + c, :], env.seg[:], bound[:, 2 * n + c, :], 0.0, ALU.mult, ALU.add).then_inc(mem_dve.sem, 1)
                    dve.wait_ge(mem_dve.sem, mem_dve.at(it.g, 4))
                    v.tensor_tensor(prod[:, 0:2, :], mem[:, 0:2, :], cos[it.s][:, 2:4, :], ALU.mult).then_inc(mem_dve.sem, 1)
                    v.tensor_tensor(prod[:, 2:4, :], mem[:, 2:4, :], sin[it.s][:, 2:4, :], ALU.mult).then_inc(mem_dve.sem, 1)
                    dve.wait_ge(mem_dve.sem, mem_dve.at(it.g, 6))
                    dve.wait_ge(back.sem, back.at(it.g - 2))
                    v.tensor_tensor(ret[it.s][:], prod[:, 0:2, :], prod[:, 2:4, :], ALU.add).then_inc(mem_dve.sem, 1)

                def normalise_ret(it):
                    dve.wait_ge(back.sem, back.at(it.g))
                    for t in range(2):
                        v.bn_stats(stats2[:, t, :], pE[:, t, :]).then_inc(ln_dve.sem, 1)
                    dve.wait_ge(ln_dve.sem, ln_dve.at(it.g, 2))
                    Carrier.carry(dve)
                    for t in range(2):
                        v.bn_aggr(mv2[:, t, :], stats2[:, t, :]).then_inc(ln_dve.sem, 1)
                    dve.wait_ge(ln_dve.sem, ln_dve.at(it.g, 4))
                    v.tensor_scalar(var2[:], mv2[:, :, 1], EPS, None, ALU.add).then_inc(ln_dve.sem, 1)

                def center_ret(it):
                    dve.wait_ge(ln_pool.sem, ln_pool.at(it.g))
                    dve.wait_ge(z_turned.sem, z_turned.at(it.g - 2))
                    for t in range(2):
                        v.tensor_scalar(zt[it.s][:, t, :], pE[:, t, :], mv2[:, t, 0:1], rstd2[:, t:t + 1],
                                                    ALU.subtract, ALU.mult).then_inc(ln_dve.sem, 1)

                def z_high(it):
                    dve.wait_ge(z_act.sem, z_act.at(it.g))
                    dve.wait_ge(out_pe.sem, out_pe.at(it.g - 2))
                    v.tensor_copy(z[0][it.s][:], zf[:]).then_inc(z_dve.sem, 1)

                def add_out(it):
                    dve.wait_ge(out_pe.sem, out_pe.at(it.g))
                    dve.wait_ge(r_loaded[it.s], 16 * it.q + 16)
                    if it.again:
                        dve.wait_ge(out_stored[it.s], 16 * it.q)
                    v.tensor_tensor(res_out[it.s][:], pG[:], res_in[it.s][:], ALU.add).then_inc(out_dve.sem, 1)

                for stage in (norm, low, proj_dve, ph_dve, mem_dve, ln_dve, z_dve, out_dve):
                    stage.open(dve)
                pipelined(dve, 8, ITEMS, 4, (1, x_low), (5, normalise_ret), (7, add_out), (5, center_ret), (0, normalise),
                          (3, phase), (0, center), (1, project), (6, z_high), (4, memory))

            @block.gpsimd
            def _(pool):
                p = nc.gpsimd

                def rstd_x(it):
                    pool.wait_ge(norm.sem, norm.at(it.g, 5))
                    p.tensor_tensor(rstd[:], var[:], env.neg_half[:, 0:2], ALU.pow).then_inc(norm_pool.sem, 1)

                def residual(it):
                    pool.wait_ge(norm_pool.sem, norm_pool.at(it.g - 1))
                    for t in range(2):
                        i = p.tensor_tensor(res_t[:, t, :], x_in[it.s][:, t, :], env.bo_rows[:], ALU.add)
                    i.then_inc(norm_pool.sem, 1)
                    pool.wait_ge(norm_pool.sem, norm_pool.at(it.g, 2))
                    pool.wait_ge(norm.sem, norm.at(it.g, 7))
                    if it.again:
                        pool.wait_ge(res_stored[it.s], 16 * it.q)
                    p.tensor_tensor(res[it.s][:], res_t[:], xn[it.s][:], ALU.add).then_inc(norm_pool.sem, 1)

                def scale(it):
                    pool.wait_ge(tanhs.sem, tanhs.at(it.g))
                    p.tensor_tensor(ph[it.s][:], ph[it.s][:], env.scale4[:].unsqueeze(2).to_broadcast([P, 4, G]), ALU.mult).then_inc(scaled.sem, 1)

                def bind(it):
                    pool.wait_ge(sines.sem, sines.at(it.g))
                    pool.wait_ge(mem_dve.sem, mem_dve.at(it.g - 1))
                    p.tensor_tensor(bound[:, 0:2, :], val[it.lane][:], cos[it.s][:, 0:2, :], ALU.mult).then_inc(bound_p.sem, 1)
                    p.tensor_tensor(bound[:, 2:4, :], val[it.lane][:], sin[it.s][:, 0:2, :], ALU.mult).then_inc(bound_p.sem, 1)

                def rstd_ret(it):
                    pool.wait_ge(ln_dve.sem, ln_dve.at(it.g, 5))
                    p.tensor_tensor(rstd2[:], var2[:], env.neg_half[:, 0:2], ALU.pow).then_inc(ln_pool.sem, 1)

                def z_low(it):
                    pool.wait_ge(z_dve.sem, z_dve.at(it.g))
                    p.tensor_tensor(z[1][it.s][:], zf[:], z[0][it.s][:].bitcast(F32), ALU.subtract).then_inc(z_pool.sem, 1)

                for stage in (norm_pool, scaled, bound_p, ln_pool, z_pool):
                    stage.open(pool)
                pipelined(pool, 8, ITEMS, 4, (3, scale), (5, rstd_ret), (4, bind), (0, rstd_x), (6, z_low), (0, residual))

            @block.scalar
            def _(act):
                a = nc.scalar

                def x_high(it):
                    act.wait_ge(turned.sem, turned.at(it.g))
                    act.wait_ge(projected.sem, projected.at(it.g - 2))
                    a.activation(xt[0][it.s][:], pT[:], ACT.Copy).then_inc(high.sem, 1)

                def project(it):
                    for n, (bank, bias) in enumerate(((pK, BK), (pQ, BQ))):
                        act.wait_ge(projected.sem, projected.at(it.g, n + 1))
                        act.wait_ge(phased.sem, phased.at(it.g - 2))
                        for c in range(KD):
                            i = a.activation(kq[0][it.s][:, 2 * n + c, :], bank[:, c, :], ACT.Identity, bias=env.cols[:, bias, c:c + 1])
                        i.then_inc(proj_act.sem, 1)

                def value(it):
                    act.wait_ge(projected.sem, projected.at(it.g, 4))
                    act.wait_ge(bound_p.sem, bound_p.at(it.g - 4))
                    for c in range(KD):
                        i = a.activation(val[it.lane][:, c, :], pK[:, c, :], ACT.Identity, bias=env.cols[:, BV, c:c + 1],
                                         scale=1.0 / math.sqrt(D))
                    i.then_inc(proj_act.sem, 1)

                def tanh(it):
                    for n, bias in enumerate((BKP, BQP)):
                        act.wait_ge(phased.sem, phased.at(it.g, n + 1))
                        act.wait_ge(ph_dve.sem, ph_dve.at(it.g - 2))
                        for c in range(KD):
                            i = a.activation(ph[it.s][:, 2 * n + c, :], pC[:, c, :], ACT.Tanh, bias=env.cols[:, bias, c:c + 1])
                        i.then_inc(tanhs.sem, 1)

                def sine(it):
                    act.wait_ge(ph_dve.sem, ph_dve.at(it.g))
                    act.wait_ge(mem_dve.sem, mem_dve.at(it.g - 2))
                    act.wait_ge(bound_p.sem, bound_p.at(it.g - 2))
                    a.activation(apart[:], ang[:], ACT.Abs).then_inc(sines.sem, 1)
                    a.activation(sin[it.s][:], ang[:], ACT.Sin).then_inc(sines.sem, 1)
                    act.wait_ge(sines.sem, sines.at(it.g, 1))
                    a.activation(cos[it.s][:], apart[:], ACT.Sin, bias=env.half_pi[:, 0:1], scale=-1.0).then_inc(sines.sem, 1)

                def affine(it):
                    act.wait_ge(z_turned.sem, z_turned.at(it.g))
                    act.wait_ge(z_pool.sem, z_pool.at(it.g - 1))
                    for c in range(KD):
                        i = a.activation(zf[:, c, :], pF[:, c, :], ACT.Identity, bias=env.cols[:, LNB, c:c + 1], scale=env.cols[:, LNG, c:c + 1])
                    i.then_inc(z_act.sem, 1)

                for stage in (high, proj_act, tanhs, sines, z_act):
                    stage.open(act)
                pipelined(act, 8, ITEMS, 4, (2, value), (1, x_high), (2, tanh), (6, affine), (1, project), (3, sine))

            @block.tensor
            def _(pe):
                t_ = nc.tensor

                def product(out, weights, w_cols, acts, a_slot, a_rows):
                    n = 0
                    for k in range(KD):
                        for i, j in PARTS:
                            last = t_.matmul(out, weights[i][:, w_cols[0], k, w_cols[1]], acts[j][a_slot][:, a_rows + k, :],
                                             start=(n == 0), stop=(n == 3 * KD - 1))
                            n += 1
                    return last

                def turn_x(it):
                    pe.wait_ge(norm.sem, norm.at(it.g, 7))
                    pe.wait_ge(low.sem, low.at(it.g - 1))
                    for t in range(2):
                        for k in range(KD):
                            i = t_.transpose(pT[:, k, t * P:(t + 1) * P], xn[it.s][:, t, k * P:(k + 1) * P], env.ident[:])
                    i.then_inc(turned.sem, 1)

                def project(it):
                    pe.wait_ge(high.sem, high.at(it.g))
                    pe.wait_ge(low.sem, low.at(it.g))
                    pe.wait_ge(proj_act.sem, proj_act.at(it.g - 1))
                    for c in range(KD):
                        i = product(pK[:, c, :], env.w, (WK, slice(c * P, (c + 1) * P)), xt, it.s, 0)
                    i.then_inc(projected.sem, 1)
                    pe.wait_ge(proj_dve.sem, proj_dve.at(it.g - 1, 2))
                    for c in range(KD):
                        i = product(pQ[:, c, :], env.w, (WQ, slice(c * P, (c + 1) * P)), xt, it.s, 0)
                    i.then_inc(projected.sem, 1)
                    pe.wait_ge(proj_dve.sem, proj_dve.at(it.g - 1))
                    for t in range(2):
                        n = 0
                        for k in range(KD):
                            for a, b in PARTS:
                                i = t_.matmul(pL[:, t, :], xt[a][it.s][:, k, t * P:(t + 1) * P], env.rw[b][:, k, :],
                                              start=(n == 0), stop=(n == 3 * KD - 1))
                                n += 1
                    i.then_inc(projected.sem, 1)

                def values(it):
                    pe.wait_ge(proj_act.sem, proj_act.at(it.g, 1))
                    pe.wait_ge(proj_dve.sem, proj_dve.at(it.g, 1))
                    for c in range(KD):
                        i = product(pK[:, c, :], env.w, (WV, slice(c * P, (c + 1) * P)), xt, it.s, 0)
                    i.then_inc(projected.sem, 1)

                def phase(it, n):
                    pe.wait_ge(proj_act.sem, proj_act.at(it.g, n + 1))
                    pe.wait_ge(proj_dve.sem, proj_dve.at(it.g, n + 1))
                    pe.wait_ge(tanhs.sem, tanhs.at(it.g, n))
                    for c in range(KD):
                        i = product(pC[:, c, :], env.w, ((WKP, WQP)[n], slice(c * P, (c + 1) * P)), kq, it.s, 2 * n)
                    i.then_inc(phased.sem, 1)

                def phase_keys(it):
                    phase(it, 0)

                def phase_queries(it):
                    phase(it, 1)

                def turn_ret(it):
                    pe.wait_ge(mem_dve.sem, mem_dve.at(it.g))
                    pe.wait_ge(ln_dve.sem, ln_dve.at(it.g - 1))
                    for t in range(2):
                        for k in range(KD):
                            i = t_.transpose(pE[:, t, k * P:(k + 1) * P], ret[it.s][:, k, t * P:(t + 1) * P], env.ident[:])
                    i.then_inc(back.sem, 1)

                def turn_z(it):
                    pe.wait_ge(ln_dve.sem, ln_dve.at(it.g))
                    pe.wait_ge(z_act.sem, z_act.at(it.g - 1))
                    for t in range(2):
                        for k in range(KD):
                            i = t_.transpose(pF[:, k, t * P:(t + 1) * P], zt[it.s][:, t, k * P:(k + 1) * P], env.ident[:])
                    i.then_inc(z_turned.sem, 1)

                def project_out(it):
                    pe.wait_ge(z_dve.sem, z_dve.at(it.g))
                    pe.wait_ge(z_pool.sem, z_pool.at(it.g))
                    pe.wait_ge(out_dve.sem, out_dve.at(it.g - 1))
                    for t in range(2):
                        n = 0
                        for k in range(KD):
                            for a, b in PARTS:
                                i = t_.matmul(pG[:, t, :], z[a][it.s][:, k, t * P:(t + 1) * P], env.w[b][:, WO, k, :],
                                              start=(n == 0), stop=(n == 3 * KD - 1))
                                n += 1
                    i.then_inc(out_pe.sem, 1)

                for stage in (turned, projected, phased, back, z_turned, out_pe):
                    stage.open(pe)
                pipelined(pe, 8, ITEMS, 4, (7, project_out), (2, phase_keys), (5, turn_ret), (6, turn_z), (2, phase_queries),
                          (1, project), (1, values), (0, turn_x))


P = 128
BF16 = mybir.dt.bfloat16


def route(nc, env, name, logits, experts, choices, segments, cap, expert_rows, trash, picks):
    NT = logits.shape[1]
    per_seg = NT // segments
    W = NT * experts
    NB = (W + 511) // 512
    with ExitStack() as ctx:
        sb = lambda n, s, d=F32: ctx.enter_context(nc.sbuf_tensor(f"{name}_{n}", s, d))
        ps = lambda n, s, d=F32: ctx.enter_context(nc.psum_tensor(f"{name}_{n}", s, d))
        best = sb("best", [P, NT, 8]); which = sb("which", [P, NT, 8], U32); which_f = sb("which_f", [P, NT, 8])
        number = sb("number", [P, experts]); own = sb("own", [P, choices, NT])
        upper = sb("upper", [P, P], BF16); ones = sb("ones", [P, P], BF16)
        chosen = [sb(f"chosen{k}", [P, NT, experts], BF16) for k in range(choices)]
        upto_t = sb("upto_t", [P, choices, experts, NT])
        reset = sb("reset", [P, experts, NT])
        before = sb("before", [P, NT, experts])
        place = sb("place", [P, NT, experts])
        pos = sb("pos", [P, NT]); row = sb("row", [P, NT]); over = sb("over", [P, NT]); tmp = sb("tmp", [P, NT])
        seg_base = sb("seg_base", [P, NT])
        rel = sb("rel", [P, NT, experts]); total = sb("total", [P, NT])
        run = ps("run", [P, W]); tot = ps("tot", [P, W])
        made = env.sem(f"{name}_consts"); steps = env.sem(f"{name}_dve"); counted = env.sem(f"{name}_counted")
        weighed = env.sem(f"{name}_exp")
        bc = lambda ap, shape: ap.to_broadcast(shape)
        count = {}

        with nc.Block() as block:
            @block.gpsimd
            def _(pool):
                p = nc.gpsimd
                p.iota(number[:], [[1, experts]], base=0, channel_multiplier=0,
                       allow_small_or_imprecise_dtypes=True).then_inc(made, 1)
                for k in range(choices):
                    p.iota(own[:, k, :], [[P, NT]], base=trash + k * NT * P, channel_multiplier=1,
                           allow_small_or_imprecise_dtypes=True).then_inc(made, 1)
                p.memset(upper[:], 1.0).then_inc(made, 1)
                p.memset(ones[:], 1.0).then_inc(made, 1)
                for b in range(segments):
                    p.memset(seg_base[:, b * per_seg:(b + 1) * per_seg], float(b * cap)).then_inc(made, 1)
                pool.wait_ge(made, 3 + choices + segments)
                p.affine_select(out=upper[:], in_=upper[:], compare_op=ALU.is_ge, fill=0.0, base=0,
                                pattern=[[1, P]], channel_multiplier=-1).then_inc(made, 1)

            @block.vector
            def _(dve):
                v = nc.vector
                n = [0]

                def done(i):
                    n[0] += 1
                    i.then_inc(steps, 1)

                def settle():
                    dve.wait_ge(steps, n[0])

                done(v.memset(reset[:], 1.0))
                settle()
                done(v.memset(reset[:].rearrange("p e (b t) -> p e b t", b=segments)[:, :, :, 0:1], 0.0))
                for t in range(NT):
                    done(v.max(best[:, t, :], logits[:, t, :]))
                settle()
                for t in range(NT):
                    done(v.max_index(which[:, t, :], best[:, t, :], logits[:, t, :]))
                settle()
                done(v.tensor_copy(which_f[:], which[:]))
                if choices == 2:
                    done(v.tensor_tensor(tmp[:], best[:, :, 1], best[:, :, 0], ALU.subtract))
                    settle()
                else:
                    done(v.tensor_tensor(rel[:], logits[:], bc(best[:, :, 0:1], [P, NT, experts]), ALU.subtract))
                    settle()
                count["weigh"] = n[0]
                dve.wait_ge(made, 4 + choices + segments)
                for k in range(choices):
                    done(v.tensor_tensor(chosen[k][:], bc(which_f[:, :, k:k + 1], [P, NT, experts]),
                                         bc(number[:].unsqueeze(1), [P, NT, experts]), ALU.is_equal))
                    count[k] = n[0]
                for k in range(choices):
                    dve.wait_ge(counted, k + 1)
                    per_tile = tot[:].rearrange("p (t e) -> p e t", e=experts)
                    for e in range(experts):
                        done(v.tensor_tensor_scan(upto_t[:, k, e, :], reset[:, e, :], per_tile[:, e, :], 0.0, ALU.mult, ALU.add))
                    settle()
                    done(v.tensor_tensor(before[:].rearrange("p t e -> p e t"), upto_t[:, k], per_tile, ALU.subtract))
                    settle()
                    if k:
                        ends = upto_t[:, 0].rearrange("p e (b t) -> p e b t", b=segments)[:, :, :, per_seg - 1:per_seg]
                        b4 = before[:].rearrange("p (b t) e -> p e b t", b=segments)
                        for b in range(segments):
                            done(v.tensor_tensor(b4[:, :, b, :], b4[:, :, b, :], ends[:, :, b, :].to_broadcast([P, experts, per_seg]), ALU.add))
                        settle()
                    flat = before[:].rearrange("p t e -> p (t e)")
                    done(v.tensor_tensor(place[:].rearrange("p t e -> p (t e)"), run[:], flat, ALU.add))
                    settle()
                    done(v.tensor_tensor(place[:], place[:], chosen[k][:], ALU.mult))
                    settle()
                    done(v.tensor_reduce(pos[:], place[:], axis=AX, op=ALU.add))
                    count["run%d" % k] = n[0]
                    settle()
                    done(v.tensor_scalar(over[:], pos[:], cap + 0.5, None, ALU.is_gt))
                    done(v.tensor_scalar(pos[:], pos[:], -1.0, cap - 1.0, ALU.add, ALU.min))
                    done(v.tensor_scalar(row[:], which_f[:, :, k], float(expert_rows), None, ALU.mult))
                    settle()
                    done(v.tensor_tensor(row[:], row[:], seg_base[:], ALU.add))
                    settle()
                    done(v.tensor_tensor(row[:], row[:], pos[:], ALU.add))
                    settle()
                    done(v.tensor_copy(picks[k].read[:], row[:]))
                    done(v.tensor_tensor(tmp[:] if choices == 1 else total[:], own[:, k, :], row[:], ALU.subtract))
                    settle()
                    t_ = tmp if choices == 1 else total
                    done(v.tensor_tensor(t_[:], t_[:], over[:], ALU.mult))
                    settle()
                    done(v.tensor_tensor(row[:], row[:], t_[:], ALU.add))
                    settle()
                    done(v.tensor_copy(picks[k].write[:], row[:]))
                    settle()
                dve.wait_ge(weighed, 1)
                if choices == 2:
                    done(v.tensor_scalar(total[:], tmp[:], 1.0, None, ALU.add))
                    settle()
                    done(v.reciprocal(picks[0].weight[:], total[:]))
                    settle()
                    done(v.tensor_tensor(picks[1].weight[:], picks[0].weight[:], tmp[:], ALU.mult))
                else:
                    done(v.tensor_reduce(total[:], rel[:], axis=AX, op=ALU.add))
                    done(v.tensor_scalar(over[:], over[:], -1.0, 1.0, ALU.mult, ALU.add))
                    settle()
                    done(v.reciprocal(total[:], total[:]))
                    settle()
                    done(v.tensor_tensor(picks[0].weight[:], total[:], over[:], ALU.mult))
                settle()

            @block.scalar
            def _(act):
                act.wait_ge(steps, count["weigh"])
                if choices == 2:
                    nc.scalar.activation(tmp[:], tmp[:], ACT.Exp).then_inc(weighed, 1)
                else:
                    nc.scalar.activation(rel[:], rel[:], ACT.Exp).then_inc(weighed, 1)

            @block.tensor
            def _(pe):
                pe.wait_ge(made, 4 + choices + segments)
                for k in range(choices):
                    pe.wait_ge(steps, count[k])
                    if k:
                        pe.wait_ge(steps, count["run%d" % (k - 1)])
                    flat = chosen[k][:].rearrange("p t e -> p (t e)")
                    for b in range(NB):
                        c = slice(b * 512, min(W, (b + 1) * 512))
                        nc.tensor.matmul(run[:, c], upper[:], flat[:, c], start=True, stop=True)
                        i = nc.tensor.matmul(tot[:, c], ones[:], flat[:, c], start=True, stop=True)
                    i.then_inc(counted, 1)


class Pick:

    def __init__(self, keep, name, NT):
        self.write = keep(f"{name}_write", [P, NT], U32)
        self.read = keep(f"{name}_read", [P, NT], U32)
        self.weight = keep(f"{name}_weight", [P, NT])


def scatter(nc, env, name, src, buf, picks, NT):
    SL = 4
    K = len(picks)
    with ExitStack() as ctx:
        rows = [ctx.enter_context(nc.sbuf_tensor(f"{name}_rows{i}", [P, src.shape[1]], F32)) for i in range(SL)]
        at = [[ctx.enter_context(nc.sbuf_tensor(f"{name}_at{i}_{k}", [P, 1], U32)) for k in range(K)] for i in range(SL)]
        loaded = [env.sem(f"{name}_loaded{i}") for i in range(SL)]
        sent = [env.sem(f"{name}_sent{i}") for i in range(SL)]
        indexed = env.sem(f"{name}_indexed")
        with nc.Block() as block:
            @block.sync
            def _(sp):
                for i in range(SL):
                    sp.dma_start(rows[i][:], src[i * P:(i + 1) * P, :]).then_inc(loaded[i], 16)
                with sp.Fori(1, NT // SL) as r:
                    for i in range(SL):
                        row = sp.snap((r * SL + i) * P)
                        sp.wait_ge(sent[i], r * (16 * K))
                        Carrier.carry(sp)
                        sp.dma_start(rows[i][:], src[bass.ds(row, P), :]).then_inc(loaded[i], 16)

            @block.gpsimd
            def _(pool):
                def send(r, i):
                    for k in range(K):
                        if not isinstance(r, int):
                            pool.wait_ge(sent[i], r * (16 * K))
                            Carrier.carry(pool)
                        nc.gpsimd.tensor_copy(at[i][k][:], picks[k].write[:, bass.ds(r * SL + i, 1)]).then_inc(indexed, 1)
                    pool.wait_ge(loaded[i], r * 16 + 16)
                    Carrier.carry(pool)
                    pool.wait_ge(indexed, (r * SL + i + 1) * K)
                    Carrier.carry(pool)
                    for k in range(K):
                        pool.indirect_dma_start(buf[:, :], bass.IndirectOffsetOnAxis(ap=at[i][k][:, 0:1], axis=0),
                                                rows[i][:], None).then_inc(sent[i], 16)

                for i in range(SL):
                    send(0, i)
                with pool.Fori(1, NT // SL) as r:
                    for i in range(SL):
                        send(r, i)
                for i in range(SL):
                    pool.wait_ge(sent[i], 16 * K * (NT // SL))


P, D, KD = 128, 256, 2
PARTS = ((0, 0), (0, 1), (1, 0))
E0, H0 = 8, 1024
HC = H0 // P
GR = 512
SUB = GR // P
PER = 5
ROWS0 = PER * GR
CAP0 = 614


def experts_l0(nc, env, buf, out_buf, w_fc, w_gate, w_proj, bias_cols, bias_rows):
    with ExitStack() as ctx:
        sb = lambda n, s, d=F32: ctx.enter_context(nc.sbuf_tensor("m0_" + n, s, d))
        ps = lambda n, s, d=F32: ctx.enter_context(nc.psum_tensor("m0_" + n, s, d))
        sem = lambda n: env.sem("m0_" + n)
        two = lambda n, s, d=F32: [sb(f"{n}{i}", s, d) for i in range(2)]
        cols = sb("cols", [P, 2, E0, HC]); rows_b = sb("rows", [P, E0, D])
        gate_bias = two("gate_bias", [P, HC]); bias_set = sem("bias_set")
        raw = sb("raw", [P, KD * H0])
        wt = [two("w_hi", [P, 3, KD * H0], F32R), two("w_lo", [P, 3, KD * H0], F32R)]
        x_in = two("x_in", [P, SUB, D])
        xt = [two("xt_hi", [P, KD, GR], F32R), two("xt_lo", [P, KD, GR], F32R)]
        gate = two("gate", [P, GR]); prod = two("prod", [P, GR]); act_f = two("act", [P, GR])
        ht = [sb("ht_hi", [P, HC, GR], F32R), sb("ht_lo", [P, HC, GR], F32R)]
        out = two("out", [P, SUB, D])
        pA = [ps(f"pA{i}", [P, GR]) for i in range(2)]
        pH = [ps(f"pH{i}", [P, GR]) for i in range(2)]; pG = [ps(f"pG{i}", [P, GR]) for i in range(2)]
        pO = [ps(f"pO{i}", [P, 2, D]) for i in range(2)]
        fc = lambda part, u, k, hc: wt[part][u][:, 0, :].rearrange("p (k h) -> p k h", k=KD)[:, k, hc * P:(hc + 1) * P]
        gt = lambda part, u, k, hc: wt[part][u][:, 1, :].rearrange("p (k h) -> p k h", k=KD)[:, k, hc * P:(hc + 1) * P]
        pj = lambda part, u, hc: wt[part][u][:, 2, :].rearrange("p (c d) -> p c d", c=HC)[:, hc, :]

        consts = sem("consts"); w_loaded = sem("w_loaded")
        w_high, w_low = sem("w_high"), sem("w_low")
        x_loaded = [sem(f"x_loaded{i}") for i in range(2)]; out_stored = [sem(f"out_stored{i}") for i in range(2)]
        turned = Steps(sem("turned"), 2); x_high = Steps(sem("x_high"), 2); x_low = Steps(sem("x_low"), 2)
        up = Steps(sem("up"), 2 * HC)
        gated = Steps(sem("gated"), HC); glu = Steps(sem("glu"), HC); silu = Steps(sem("silu"), HC)
        h_high = Steps(sem("h_high"), HC); h_low = Steps(sem("h_low"), HC)
        down = Steps(sem("down"), 2); added = Steps(sem("added"), 2); freed = Steps(sem("freed"), 1)

        def experts(eng, body, first=None):
            if first:
                first()
            with eng.Fori(0, E0 // 2) as r:
                for u in range(2):
                    body(r, u)

        def item(r, u, j):
            return Item(u * PER + j, r, 2 * PER)

        with nc.Block() as block:
            @block.sync
            def _(sp):
                sp.dma_start(cols[:], bias_cols.rearrange("p (w e c) -> p w e c", w=2, e=E0)).then_inc(consts, 16)
                sp.dma_start(rows_b[:], bias_rows.rearrange("p (e d) -> p e d", e=E0)).then_inc(consts, 16)

                def load_weight(e, n):
                    src = (w_fc, w_gate, w_proj)[n][bass.ds(e, 1)].rearrange("o (k p) h -> p (o k) h", p=P)
                    sp.dma_start(raw[:].rearrange("p (k h) -> p k h", h=(H0, H0, D)[n]), src).then_inc(w_loaded, 16)

                def load_x(it):
                    row = sp.snap(it.g * GR)
                    sp.wait_ge(turned.sem, turned.at(it.g - 2))
                    Carrier.carry(sp)
                    sp.dma_start(x_in[it.s][:], buf[bass.ds(row, GR), :].rearrange("(t p) d -> p t d", p=P)).then_inc(x_loaded[it.s], 16)

                def free(it):
                    sp.wait_ge(out_stored[it.s], it.q * 16 + 16)
                    sp.sem_inc(freed.sem, 1)

                def store(it):
                    row = sp.snap(it.g * GR)
                    sp.wait_ge(added.sem, added.at(it.g))
                    Carrier.carry(sp)
                    sp.dma_start(out_buf[bass.ds(row, GR), :].rearrange("(t p) d -> p t d", p=P), out[it.s][:]).then_inc(out_stored[it.s], 16)

                def body(r, u):
                    nxt = sp.snap(r * 2 + 1) if u == 0 else sp.snap((r * 2 + 2) % E0)
                    for j in range(PER):
                        load_x(item(r, u, j))
                        if j:
                            store(item(r, u, j - 1))
                        if j > 1:
                            free(item(r, u, j - 2))
                        if 1 <= j <= 3:
                            sp.wait_ge(w_low, r * 6 + (u * 3 + 2 + j))
                            Carrier.carry(sp)
                            load_weight(nxt, j - 1)
                    store(item(r, u, PER - 1))
                    free(item(r, u, PER - 2))
                    free(item(r, u, PER - 1))

                for n in range(3):
                    if n:
                        sp.wait_ge(w_low, n)
                    load_weight(0, n)
                freed.open(sp)
                experts(sp, body)
                for s in range(2):
                    sp.wait_ge(out_stored[s], 16 * E0 * PER // 2)

            @block.vector
            def _(dve):
                v = nc.vector

                def split_high(u, n, loaded, used):
                    dve.wait_ge(w_loaded, loaded)
                    dve.wait_ge(down.sem, down.at(used))
                    v.tensor_copy(wt[0][u][:, n, :], raw[:]).then_inc(w_high, 1)

                def low_x(it):
                    for k in range(KD):
                        dve.wait_ge(x_high.sem, x_high.at(it.g, k + 1))
                        if k == 0:
                            dve.wait_ge(up.sem, up.at(it.g - 2))
                        v.tensor_tensor(xt[1][it.s][:, k, :], pA[k][:], xt[0][it.s][:, k, :].bitcast(F32), ALU.subtract).then_inc(x_low.sem, 1)

                def hidden(it, e):

                    def high(hc):
                        dve.wait_ge(silu.sem, silu.at(it.g, hc + 1))
                        if hc == 0:
                            dve.wait_ge(down.sem, down.at(it.g - 1))
                        v.tensor_copy(ht[0][:, hc, :], act_f[hc % 2][:]).then_inc(h_high.sem, 1)

                    for hc in range(HC):
                        dve.wait_ge(up.sem, up.at(it.g, 2 * hc + 1))
                        dve.wait_ge(gated.sem, gated.at(it.g, hc + 1))
                        dve.wait_ge(silu.sem, silu.at(it.g, hc - 1))
                        v.scalar_tensor_tensor(out=prod[hc % 2][:], in0=pH[hc % 2][:], scalar=cols[:, 0, bass.ds(e, 1), hc:hc + 1].rearrange("p o c -> p (o c)"),
                                                        in1=gate[hc % 2][:], op0=ALU.add, op1=ALU.mult).then_inc(glu.sem, 1)
                        if hc:
                            high(hc - 1)
                    high(HC - 1)

                def add_bias(it, e):
                    for half in range(2):
                        dve.wait_ge(down.sem, down.at(it.g, half + 1))
                        if half == 0:
                            dve.wait_ge(freed.sem, freed.at(it.g - 2))
                        for t in range(2):
                            i = v.tensor_tensor(out[it.s][:, half * 2 + t, :].unsqueeze(1), pO[half][:, t:t + 1, :], rows_b[:, bass.ds(e, 1), :], ALU.add)
                        i.then_inc(added.sem, 1)

                def body(r, u):
                    e = dve.snap(r * 2 + u)
                    for j in range(PER):
                        if j:
                            add_bias(item(r, u, j - 1), e)
                        if j == 0:
                            low_x(item(r, u, 0))
                        hidden(item(r, u, j), e)
                        if j + 1 < PER:
                            low_x(item(r, u, j + 1))
                        if 1 <= j <= 3:
                            split_high(1 - u, j - 1, r * 96 + (u * 48 + 48 + 16 * j), r * (2 * PER) + (u * PER - 1))
                    add_bias(item(r, u, PER - 1), e)

                for stage in (x_low, glu, h_high, added):
                    stage.open(dve)
                dve.wait_ge(consts, 32)
                for n in range(3):
                    split_high(0, n, 16 * n + 16, -1)
                experts(dve, body)

            @block.gpsimd
            def _(pool):
                p = nc.gpsimd

                def split_low(u, n, high):
                    pool.wait_ge(w_high, high)
                    p.tensor_tensor(wt[1][u][:, n, :], raw[:], wt[0][u][:, n, :].bitcast(F32), ALU.subtract).then_inc(w_low, 1)

                def hidden(it):
                    for hc in range(HC):
                        pool.wait_ge(h_high.sem, h_high.at(it.g, hc + 1))
                        p.tensor_tensor(ht[1][:, hc, :], act_f[hc % 2][:], ht[0][:, hc, :].bitcast(F32), ALU.subtract).then_inc(h_low.sem, 1)

                def body(r, u):
                    for j in range(PER):
                        hidden(item(r, u, j))
                        if 1 <= j <= 3:
                            split_low(1 - u, j - 1, r * 6 + (u * 3 + 3 + j))

                for n in range(3):
                    split_low(0, n, n + 1)
                for stage in (h_low,):
                    stage.open(pool)
                experts(pool, body)

            @block.scalar
            def _(act):
                a = nc.scalar

                def high_x(it):
                    for k in range(KD):
                        act.wait_ge(turned.sem, turned.at(it.g, k + 1))
                        if k == 0:
                            act.wait_ge(up.sem, up.at(it.g - 2))
                        a.activation(xt[0][it.s][:, k, :], pA[k][:], ACT.Copy).then_inc(x_high.sem, 1)

                def hidden(it, u):

                    def activate(hc):
                        act.wait_ge(glu.sem, glu.at(it.g, hc + 1))
                        act.wait_ge(h_high.sem, h_high.at(it.g, hc - 1))
                        act.wait_ge(h_low.sem, h_low.at(it.g, hc - 1))
                        a.activation(act_f[hc % 2][:], prod[hc % 2][:], ACT.Silu).then_inc(silu.sem, 1)

                    for hc in range(HC):
                        act.wait_ge(up.sem, up.at(it.g, 2 * hc + 2))
                        act.wait_ge(glu.sem, glu.at(it.g, hc - 1))
                        a.activation(gate[hc % 2][:], pG[hc % 2][:], ACT.Identity, bias=gate_bias[u][:, hc:hc + 1]).then_inc(gated.sem, 1)
                        if hc:
                            activate(hc - 1)
                    activate(HC - 1)

                def body(r, u):
                    e = act.snap(r * 2 + u)
                    a.activation(gate_bias[u][:].unsqueeze(1), cols[:, 1, bass.ds(e, 1), :], ACT.Copy).then_inc(bias_set, 1)
                    high_x(item(r, u, 0))
                    act.wait_ge(bias_set, r * 2 + u + 1)
                    for j in range(PER):
                        hidden(item(r, u, j), u)
                        if j + 1 < PER:
                            high_x(item(r, u, j + 1))

                act.wait_ge(consts, 32)
                for stage in (x_high, gated, silu):
                    stage.open(act)
                experts(act, body)

            @block.tensor
            def _(pe):
                t_ = nc.tensor

                def turn_x(it):
                    pe.wait_ge(x_loaded[it.s], it.q * 16 + 16)
                    for k in range(KD):
                        pe.wait_ge(x_low.sem, x_low.at(it.g - 1, k + 1))
                        for t in range(SUB):
                            i = t_.transpose(pA[k][:, t * P:(t + 1) * P], x_in[it.s][:, t, k * P:(k + 1) * P], env.ident[:])
                        i.then_inc(turned.sem, 1)

                def up_products(it, u):
                    pe.wait_ge(x_low.sem, x_low.at(it.g))
                    for hc in range(HC):
                        pe.wait_ge(glu.sem, glu.at(it.g, hc - 1))
                        for bank, w in ((pH, fc), (pG, gt)):
                            n = 0
                            for k in range(KD):
                                for i, j in PARTS:
                                    last = t_.matmul(bank[hc % 2][:], w(i, u, k, hc), xt[j][it.s][:, k, :], start=(n == 0), stop=(n == 5))
                                    n += 1
                            last.then_inc(up.sem, 1)

                def down_products(it, u):
                    for half in range(2):
                        pe.wait_ge(added.sem, added.at(it.g - 1, half + 1))
                        for t in range(2):
                            n = 0
                            sub = half * 2 + t
                            for hc in range(HC):
                                if sub == 0:
                                    pe.wait_ge(h_low.sem, h_low.at(it.g, hc + 1))
                                for i, j in PARTS:
                                    last = t_.matmul(pO[half][:, t, :], ht[i][:, hc, sub * P:(sub + 1) * P], pj(j, u, hc),
                                                     start=(n == 0), stop=(n == 3 * HC - 1))
                                    n += 1
                        last.then_inc(down.sem, 1)

                def body(r, u):
                    turn_x(item(r, u, 0))
                    for j in range(PER):
                        if j:
                            down_products(item(r, u, j - 1), u)
                        if j == 0:
                            pe.wait_ge(w_low, r * 6 + u * 3 + 3)
                        up_products(item(r, u, j), u)
                        if j + 1 < PER:
                            turn_x(item(r, u, j + 1))
                    down_products(item(r, u, PER - 1), u)

                for stage in (turned, up, down):
                    stage.open(pe)
                experts(pe, body)


P, D, KD = 128, 256, 2
PARTS = ((0, 0), (0, 1), (1, 0))
EPS = 1e-5


def combine_l0(nc, env, out0, picks, res0, res1, xn1, xt1, head_w, logits1, dt_raw, NT):
    NO = head_w.shape[1]
    NE = logits1.shape[2]
    SL = 4
    with ExitStack() as ctx:
        sb = lambda n, s, d=F32: ctx.enter_context(nc.sbuf_tensor("c0_" + n, s, d))
        ps = lambda n, s, d=F32: ctx.enter_context(nc.psum_tensor("c0_" + n, s, d))
        sem = lambda n: env.sem("c0_" + n)
        slots = lambda n, s, d=F32: [sb(f"{n}{i}", s, d) for i in range(SL)]
        sems = lambda n: [sem(f"{n}{i}") for i in range(SL)]
        w_raw = sb("w_raw", [P, KD, NO]); w = [sb("w_hi", [P, KD, NO], F32R), sb("w_lo", [P, KD, NO], F32R)]
        res_in = slots("res_in", [P, D])
        at = [slots(f"at{k}_", [P, 1], U32) for k in range(2)]
        got = [slots(f"got{k}_", [P, D]) for k in range(2)]
        x1 = slots("x1", [P, D]); part = slots("part", [P, D])
        stats = slots("stats", [P, 6]); mv = slots("mv", [P, 2]); var = slots("var", [P, 1]); rstd = slots("rstd", [P, 1])
        xn = slots("xn", [P, D]); res = slots("res", [P, D])
        xt = slots("xt", [P, 2, KD, P], F32R)
        pT = [ps(f"pT{i}", [P, KD, P]) for i in range(SL)]; pH = [ps(f"pH{i}", [P, NO]) for i in range(2)]
        w_loaded = sem("w_loaded"); w_split = sem("w_split")
        loaded, gathered = sems("loaded"), sems("gathered")
        xn_stored, res_stored, xt_stored = sems("xn_stored"), sems("res_stored"), sems("xt_stored")
        indexed = Steps(sem("indexed"), 2)
        first, summed = Steps(sem("first"), 1), Steps(sem("summed"), 1)
        norm = Steps(sem("norm"), 3)
        center_s = Steps(sem("center"), 1)
        root, both = Steps(sem("root"), 1), Steps(sem("both"), 1)
        turned = Steps(sem("turned"), 1); high = Steps(sem("high"), 1); low = Steps(sem("low"), 1)
        heads = Steps(sem("heads"), 1); kept = Steps(sem("kept"), 1)
        with nc.Block() as block:
            @block.sync
            def _(sp):
                sp.dma_start(w_raw[:], head_w.rearrange("(k p) e -> p k e", p=P)).then_inc(w_loaded, 16)

                def load(it):
                    row = at_row(sp, it, P)
                    sp.wait_ge(first.sem, first.at(it.g - SL))
                    Carrier.carry(sp)
                    sp.dma_start(res_in[it.lane][:], res0[bass.ds(row, P), :]).then_inc(loaded[it.lane], 16)

                def store(it):
                    row = at_row(sp, it, P)
                    sp.wait_ge(center_s.sem, center_s.at(it.g))
                    Carrier.carry(sp)
                    sp.dma_start(xn1[bass.ds(row, P), :], xn[it.lane][:]).then_inc(xn_stored[it.lane], 16)

                def store_sum(it):
                    row = at_row(sp, it, P)
                    sp.wait_ge(both.sem, both.at(it.g))
                    Carrier.carry(sp)
                    sp.dma_start(res1[bass.ds(row, P), :], res[it.lane][:]).then_inc(res_stored[it.lane], 16)

                def store_turned(it):
                    row = at_row(sp, it, P)
                    sp.wait_ge(high.sem, high.at(it.g))
                    Carrier.carry(sp)
                    sp.wait_ge(low.sem, low.at(it.g))
                    Carrier.carry(sp)
                    sp.dma_start(xt1[bass.ds(row, P)], xt[it.lane][:].bitcast(F32)).then_inc(xt_stored[it.lane], 16)

                pipelined(sp, 8, NT, SL, (0, load), (5, store), (5, store_sum), (6, store_turned))
                for s in range(SL):
                    for q in (xn_stored, res_stored, xt_stored):
                        sp.wait_ge(q[s], 16 * NT // SL)

            @block.gpsimd
            def _(pool):
                p = nc.gpsimd

                def index(it):
                    if it.again_lane:
                        pool.wait_ge(gathered[it.lane], it.turn * 32)
                        Carrier.carry(pool)
                    for k in range(2):
                        p.tensor_copy(at[k][it.lane][:], picks[k].read[:, bass.ds(it.g, 1)]).then_inc(indexed.sem, 1)

                def gather(it):
                    pool.wait_ge(indexed.sem, indexed.at(it.g))
                    Carrier.carry(pool)
                    pool.wait_ge(summed.sem, summed.at(it.g - SL))
                    Carrier.carry(pool)
                    for k in range(2):
                        pool.indirect_dma_start(got[k][it.lane][:], None, out0[:, :],
                                                bass.IndirectOffsetOnAxis(ap=at[k][it.lane][:, 0:1], axis=0)).then_inc(gathered[it.lane], 16)

                def rstd_x(it):
                    pool.wait_ge(norm.sem, norm.at(it.g))
                    pool.wait_ge(center_s.sem, center_s.at(it.g - SL))
                    p.tensor_tensor(rstd[it.lane][:], var[it.lane][:], env.neg_half[:, 0:1], ALU.pow).then_inc(root.sem, 1)

                def add_both(it):
                    pool.wait_ge(center_s.sem, center_s.at(it.g))
                    if it.again_lane:
                        pool.wait_ge(res_stored[it.lane], it.turn * 16)
                    p.tensor_tensor(res[it.lane][:], x1[it.lane][:], xn[it.lane][:], ALU.add).then_inc(both.sem, 1)

                for stage in (indexed, root, both):
                    stage.open(pool)
                pipelined(pool, 8, NT, SL, (3, rstd_x), (0, index), (5, add_both), (1, gather))

            @block.vector
            def _(dve):
                v = nc.vector
                dve.wait_ge(w_loaded, 16)
                v.tensor_copy(w[0][:], w_raw[:]).then_inc(w_split, 1)
                dve.wait_ge(w_split, 1)
                v.tensor_tensor(w[1][:], w_raw[:], w[0][:].bitcast(F32), ALU.subtract).then_inc(w_split, 1)

                def weight(it, k):
                    return picks[k].weight[:, bass.ds(it.g, 1)]

                def add_first(it):
                    dve.wait_ge(loaded[it.lane], it.turn * 16 + 16)
                    dve.wait_ge(gathered[it.lane], it.turn * 32 + 32)
                    dve.wait_ge(summed.sem, summed.at(it.g - SL))
                    v.scalar_tensor_tensor(out=part[it.lane][:], in0=got[0][it.lane][:], scalar=weight(it, 0), in1=res_in[it.lane][:],
                                           op0=ALU.mult, op1=ALU.add).then_inc(first.sem, 1)

                def add_second(it):
                    dve.wait_ge(first.sem, first.at(it.g))
                    dve.wait_ge(both.sem, both.at(it.g - SL))
                    v.scalar_tensor_tensor(out=x1[it.lane][:], in0=got[1][it.lane][:], scalar=weight(it, 1), in1=part[it.lane][:],
                                           op0=ALU.mult, op1=ALU.add).then_inc(summed.sem, 1)

                def measure(it):
                    dve.wait_ge(summed.sem, summed.at(it.g))
                    v.bn_stats(stats[it.lane][:], x1[it.lane][:]).then_inc(norm.sem, 1)

                def aggregate(it):
                    dve.wait_ge(norm.sem, norm.at(it.g, 1))
                    dve.wait_ge(center_s.sem, center_s.at(it.g - SL))
                    Carrier.carry(dve)
                    v.bn_aggr(mv[it.lane][:], stats[it.lane][:]).then_inc(norm.sem, 1)
                    dve.wait_ge(norm.sem, norm.at(it.g, 2))
                    dve.wait_ge(root.sem, root.at(it.g - SL))
                    v.tensor_scalar(var[it.lane][:], mv[it.lane][:, 1:2], EPS, None, ALU.add).then_inc(norm.sem, 1)

                def center(it):
                    dve.wait_ge(root.sem, root.at(it.g))
                    dve.wait_ge(turned.sem, turned.at(it.g - SL))
                    dve.wait_ge(both.sem, both.at(it.g - SL))
                    if it.again_lane:
                        dve.wait_ge(xn_stored[it.lane], it.turn * 16)
                    v.tensor_scalar(xn[it.lane][:], x1[it.lane][:], mv[it.lane][:, 0:1], rstd[it.lane][:], ALU.subtract, ALU.mult).then_inc(center_s.sem, 1)

                def low_part(it):
                    dve.wait_ge(high.sem, high.at(it.g))
                    dve.wait_ge(heads.sem, heads.at(it.g - SL))
                    if it.again_lane:
                        dve.wait_ge(xt_stored[it.lane], it.turn * 16)
                    v.tensor_tensor(xt[it.lane][:, 1], pT[it.lane][:], xt[it.lane][:, 0].bitcast(F32), ALU.subtract).then_inc(low.sem, 1)

                def keep(it):
                    dve.wait_ge(heads.sem, heads.at(it.g))
                    v.tensor_copy(logits1[:, bass.ds(it.g, 1), :], pH[it.s][:, 0:NE].unsqueeze(1))
                    v.tensor_copy(dt_raw[:, bass.ds(it.g, 1), :], pH[it.s][:, NE:NO].unsqueeze(1)).then_inc(kept.sem, 1)

                for stage in (first, summed, norm, center_s, low, kept):
                    stage.open(dve)
                pipelined(dve, 8, NT, SL, (2, add_first), (4, center), (2, add_second), (6, low_part), (2, measure), (7, keep), (2, aggregate))

            @block.scalar
            def _(act):
                def high_part(it):
                    act.wait_ge(turned.sem, turned.at(it.g))
                    act.wait_ge(heads.sem, heads.at(it.g - SL))
                    if it.again_lane:
                        act.wait_ge(xt_stored[it.lane], it.turn * 16)
                    nc.scalar.activation(xt[it.lane][:, 0], pT[it.lane][:], ACT.Copy).then_inc(high.sem, 1)

                high.open(act)
                pipelined(act, 8, NT, SL, (5, high_part))

            @block.tensor
            def _(pe):
                t_ = nc.tensor
                pe.wait_ge(w_split, 2)

                def turn(it):
                    pe.wait_ge(center_s.sem, center_s.at(it.g))
                    pe.wait_ge(low.sem, low.at(it.g - SL))
                    for k in range(KD):
                        i = t_.transpose(pT[it.lane][:, k, :], xn[it.lane][:, k * P:(k + 1) * P], env.ident[:])
                    i.then_inc(turned.sem, 1)

                def project(it):
                    pe.wait_ge(low.sem, low.at(it.g))
                    pe.wait_ge(kept.sem, kept.at(it.g - 2))
                    n = 0
                    for k in range(KD):
                        for a, b in PARTS:
                            i = t_.matmul(pH[it.s][:], xt[it.lane][:, a, k, :], w[b][:, k, :], start=(n == 0), stop=(n == 5))
                            n += 1
                    i.then_inc(heads.sem, 1)

                for stage in (turned, heads):
                    stage.open(pe)
                pipelined(pe, 8, NT, SL, (5, turn), (7, project))


P, D, KD = 128, 256, 2
PARTS = ((0, 0), (0, 1), (1, 0))
E1, CAP1 = 32, 320
SUBS = [(n * P, min(P, CAP1 - n * P)) for n in range((CAP1 + P - 1) // P)]


def experts_l1(nc, env, buf, out_buf, weights):
    with ExitStack() as ctx:
        sb = lambda n, s, d=F32: ctx.enter_context(nc.sbuf_tensor("m1_" + n, s, d))
        ps = lambda n, s, d=F32: ctx.enter_context(nc.psum_tensor("m1_" + n, s, d))
        sem = lambda n: env.sem("m1_" + n)
        two = lambda n, s, d=F32: [sb(f"{n}{i}", s, d) for i in range(2)]
        NS = len(SUBS)
        raw = two("raw", [P, 3, KD, D])
        w = [two("w_hi", [P, 3, KD, D], F32R), two("w_lo", [P, 3, KD, D], F32R)]
        x_in = two("x_in", [P, NS, D])
        xt = [two("xt_hi", [P, KD, CAP1], F32R), two("xt_lo", [P, KD, CAP1], F32R)]
        gate = two("gate", [P, KD, CAP1]); h = two("h", [P, KD, CAP1])
        ht = [two("ht_hi", [P, KD, CAP1], F32R), two("ht_lo", [P, KD, CAP1], F32R)]
        out = two("out", [P, NS, D])
        pA = [ps(f"pA{k}", [P, CAP1]) for k in range(KD)]
        pG = [ps(f"pG{k}", [P, CAP1]) for k in range(KD)]; pU = [ps(f"pU{k}", [P, CAP1]) for k in range(KD)]
        pO = [ps("pO0", [P, 2, D]), ps("pO1", [P, 1, D])]
        w_loaded = [sem(f"w_loaded{i}") for i in range(2)]; x_loaded = [sem(f"x_loaded{i}") for i in range(2)]
        stored = [sem(f"stored{i}") for i in range(2)]
        w_high = Steps(sem("w_high"), 1); w_low = Steps(sem("w_low"), 1)
        turned = Steps(sem("turned"), 2); x_high = Steps(sem("x_high"), 2); x_low = Steps(sem("x_low"), 2)
        up = Steps(sem("up"), 2); silu = Steps(sem("silu"), 2); mul = Steps(sem("mul"), 2)
        h_high = Steps(sem("h_high"), 2); h_low = Steps(sem("h_low"), 2)
        down = Steps(sem("down"), 2); kept = Steps(sem("kept"), 2)
        with nc.Block() as block:
            @block.sync
            def _(sp):
                def load(it):
                    e = it.g if isinstance(it.g, int) else sp.snap(it.g)
                    row = at_row(sp, it, CAP1)
                    sp.wait_ge(w_low.sem, w_low.at(it.g - 2))
                    Carrier.carry(sp)
                    sp.dma_start(raw[it.s][:], weights[bass.ds(e, 1)].rearrange("o w (k p) f -> p (o w) k f", p=P)).then_inc(w_loaded[it.s], 16)
                    sp.wait_ge(turned.sem, turned.at(it.g - 2))
                    Carrier.carry(sp)
                    for n, (at, m) in enumerate(SUBS):
                        sp.dma_start(x_in[it.s][0:m, n, :], buf[bass.ds(row + at, m), :]).then_inc(x_loaded[it.s], 16)

                def store(it):
                    row = at_row(sp, it, CAP1)
                    sp.wait_ge(kept.sem, kept.at(it.g))
                    Carrier.carry(sp)
                    for n, (at, m) in enumerate(SUBS):
                        sp.dma_start(out_buf[bass.ds(row + at, m), :], out[it.s][0:m, n, :]).then_inc(stored[it.s], 16)

                pipelined(sp, 4, E1, 2, (3, store), (0, load))
                for s in range(2):
                    sp.wait_ge(stored[s], 16 * NS * E1 // 2)

            @block.vector
            def _(dve):
                v = nc.vector

                def split(it):
                    dve.wait_ge(w_loaded[it.s], it.q * 16 + 16)
                    dve.wait_ge(down.sem, down.at(it.g - 2))
                    v.tensor_copy(w[0][it.s][:], raw[it.s][:]).then_inc(w_high.sem, 1)
                    for k in range(KD):
                        dve.wait_ge(x_high.sem, x_high.at(it.g, k + 1))
                        dve.wait_ge(up.sem, up.at(it.g - 2))
                        v.tensor_tensor(xt[1][it.s][:, k, :], pA[k][:], xt[0][it.s][:, k, :].bitcast(F32), ALU.subtract).then_inc(x_low.sem, 1)

                def hidden(it):
                    dve.wait_ge(h_low.sem, h_low.at(it.g - 2))
                    for k in range(KD):
                        dve.wait_ge(silu.sem, silu.at(it.g, k + 1))
                        v.tensor_tensor(h[it.s][:, k, :], pU[k][:], gate[it.s][:, k, :], ALU.mult).then_inc(mul.sem, 1)
                    dve.wait_ge(down.sem, down.at(it.g - 2))
                    for k in range(KD):
                        dve.wait_ge(mul.sem, mul.at(it.g, k + 1))
                        v.tensor_copy(ht[0][it.s][:, k, :], h[it.s][:, k, :]).then_inc(h_high.sem, 1)

                for stage in (w_high, x_low, mul, h_high):
                    stage.open(dve)
                pipelined(dve, 4, E1, 2, (2, hidden), (1, split))

            @block.gpsimd
            def _(pool):
                p = nc.gpsimd

                def split(it):
                    pool.wait_ge(w_high.sem, w_high.at(it.g))
                    p.tensor_tensor(w[1][it.s][:], raw[it.s][:], w[0][it.s][:].bitcast(F32), ALU.subtract).then_inc(w_low.sem, 1)

                def hidden(it):
                    for k in range(KD):
                        pool.wait_ge(h_high.sem, h_high.at(it.g, k + 1))
                        p.tensor_tensor(ht[1][it.s][:, k, :], h[it.s][:, k, :], ht[0][it.s][:, k, :].bitcast(F32), ALU.subtract).then_inc(h_low.sem, 1)

                for stage in (w_low, h_low):
                    stage.open(pool)
                pipelined(pool, 4, E1, 2, (2, hidden), (1, split))

            @block.scalar
            def _(act):
                a = nc.scalar

                def high_part(it):
                    for k in range(KD):
                        act.wait_ge(turned.sem, turned.at(it.g, k + 1))
                        act.wait_ge(up.sem, up.at(it.g - 2))
                        a.activation(xt[0][it.s][:, k, :], pA[k][:], ACT.Copy).then_inc(x_high.sem, 1)

                def gates(it):
                    act.wait_ge(mul.sem, mul.at(it.g - 2))
                    for k in range(KD):
                        act.wait_ge(up.sem, up.at(it.g, k + 1))
                        a.activation(gate[it.s][:, k, :], pG[k][:], ACT.Silu).then_inc(silu.sem, 1)

                def keep(it):
                    if it.again:
                        act.wait_ge(stored[it.s], it.q * (16 * NS))
                    act.wait_ge(down.sem, down.at(it.g, 1))
                    a.activation(out[it.s][:, 0:2, :], pO[0][:], ACT.Copy).then_inc(kept.sem, 1)
                    act.wait_ge(down.sem, down.at(it.g, 2))
                    m = SUBS[-1][1]
                    a.activation(out[it.s][0:m, 2, :], pO[1][0:m, 0, :], ACT.Copy).then_inc(kept.sem, 1)

                for stage in (x_high, silu, kept):
                    stage.open(act)
                pipelined(act, 4, E1, 2, (3, keep), (2, gates), (1, high_part))

            @block.tensor
            def _(pe):
                t_ = nc.tensor

                def turn(it):
                    pe.wait_ge(x_loaded[it.s], (it.q + 1) * (16 * NS))
                    for k in range(KD):
                        pe.wait_ge(x_low.sem, x_low.at(it.g - 1, k + 1))
                        for n, (at, m) in enumerate(SUBS):
                            i = t_.transpose(pA[k][:, at:at + m], x_in[it.s][0:m, n, k * P:(k + 1) * P], env.ident[0:m, 0:m])
                        i.then_inc(turned.sem, 1)

                def up_products(it):
                    pe.wait_ge(w_low.sem, w_low.at(it.g))
                    pe.wait_ge(x_low.sem, x_low.at(it.g))
                    for f in range(KD):
                        pe.wait_ge(mul.sem, mul.at(it.g - 1, f + 1))
                        for n_w, bank in ((0, pG), (1, pU)):
                            n = 0
                            for k in range(KD):
                                for i, j in PARTS:
                                    last = t_.matmul(bank[f][:], w[i][it.s][:, n_w, k, f * P:(f + 1) * P], xt[j][it.s][:, k, :],
                                                     start=(n == 0), stop=(n == 5))
                                    n += 1
                        last.then_inc(up.sem, 1)

                def down_products(it):
                    pe.wait_ge(h_low.sem, h_low.at(it.g))
                    for s_, (at, m) in enumerate(SUBS):
                        if s_ == 0:
                            pe.wait_ge(kept.sem, kept.at(it.g - 1, 1))
                        if s_ == 2:
                            pe.wait_ge(kept.sem, kept.at(it.g - 1, 2))
                        n = 0
                        for k in range(KD):
                            for i, j in PARTS:
                                last = t_.matmul(pO[s_ // 2][0:m, s_ % 2, :], ht[i][it.s][:, k, at:at + m], w[j][it.s][:, 2, k, :],
                                                 start=(n == 0), stop=(n == 5))
                                n += 1
                        if s_:
                            last.then_inc(down.sem, 1)

                for stage in (turned, up, down):
                    stage.open(pe)
                pipelined(pe, 4, E1, 2, (3, down_products), (2, up_products), (1, turn))


P, D, KD = 128, 256, 2
PARTS = ((0, 0), (0, 1), (1, 0))
EPS = 1e-5
DI, NS, NH, HD = 512, 64, 8, 64
CC = DI // P
CX = CC + 1
TAPS = 4
HALO = TAPS - 1
BATCH, SEQ = 4, 2048
TB = SEQ // P
NT = BATCH * TB
W = P + HALO


def mixer(nc, env, tag, backward, in_w, conv_cols, out_w, norm_cols, head_rows, dt_raw, dt_col, xt1, res_in_d, res_out_d, expert_rows=None, pick=None):
    with ExitStack() as ctx:
        sb = lambda n, s, d=F32: ctx.enter_context(nc.sbuf_tensor(f"{tag}_{n}", s, d))
        ps = lambda n, s, d=F32: ctx.enter_context(nc.psum_tensor(f"{tag}_{n}", s, d))
        sem = lambda n: env.sem(f"{tag}_{n}")
        two = lambda n, s, d=F32: [sb(f"{n}{i}", s, d) for i in range(2)]
        NO = DI + CX * P
        w_raw = sb("w_raw", [P, KD, NO]); w = [sb("w_hi", [P, KD, NO], F32R), sb("w_lo", [P, KD, NO], F32R)]
        conv = sb("conv", [P, CX, TAPS + 1]); norm_c = sb("norm_c", [P, CC])
        ow_raw = sb("ow_raw", [P, CC, D]); ow = sb("ow", [P, CC, D])
        rows = sb("rows", [P, 3, NH])
        dt = sb("dt", [P, NT, NH]); da = sb("da", [P, NT, NH])
        grow = sb("grow", [P, NT, NH]); fade = sb("fade", [P, NT, NH]); whole = sb("whole", [P, NT, NH])
        t1 = sb("t1", [P, NT, NH]); t2 = sb("t2", [P, NT, NH])
        upto = sb("upto", [P, P]); past = sb("past", [P, P]); ones = sb("ones", [P, P])
        state = sb("state", [NS, BATCH, DI]); faded = [sb(f"faded{i}", [NS, DI]) for i in range(2)]
        u = sb("u", [P, BATCH, CX, W])

        xt = two("xt", [P, 2, KD, P], F32R)
        gate = [sb(f"gate{i}", [P, DI]) for i in range(4)]
        cv = two("cv", [P, CX, P]); xc = two("xc", [P, CC, P]); bt = two("bt", [NS, P]); ct = two("ct", [NS, P])
        seg = two("seg", [P, NH, P])
        decay = sb("decay", [P, NH, P]); gm = sb("gm", [P, P]); mix = two("mix", [P, NH, P])
        b_tok = two("b_tok", [P, NS]); x_tok = two("x_tok", [P, DI]); xdt = two("xdt", [P, DI])
        xw = two("xw", [P, DI]); skip = two("skip", [P, DI])
        y1 = sb("y1", [P, DI]); y2 = sb("y2", [P, DI]); y3 = sb("y3", [P, DI]); yz = two("yz", [P, DI])
        sq = sb("sq", [P, DI]); ss = two("ss", [P, 1]); ms = two("ms", [P, 1]); rstd = two("rstd", [P, 1])
        yt = two("yt", [P, CC, P])
        res = two("res", [P, D]); out = two("out", [P, D])
        at = two("at", [P, 1], U32); got = two("got", [P, D]); sum_e = two("sum_e", [P, D])

        bank = [ps(f"bank{i}", [P, 512]) for i in range(8)]
        pB0 = bank[0][:].rearrange("p (c t) -> p c t", c=CC); pB1 = bank[1][:, 0:P]
        pYT = bank[0][:].rearrange("p (c t) -> p c t", c=CC); pS = bank[1][0:NS, :]
        pZ = bank[2][:]; pI = bank[2][:]
        pX = bank[3][:]
        pBT = bank[4][:, 0:NS]; pG = bank[4][:, P:2 * P]; pO = bank[4][:, 2 * P:2 * P + D]
        pD = [bank[5][:].rearrange("p (h t) -> p h t", h=4), bank[6][:].rearrange("p (h t) -> p h t", h=4)]
        pY = bank[7][:]

        loaded, made, prep, prep_pe, prep_act = sem("loaded"), sem("made"), sem("prep"), sem("prep_pe"), sem("prep_act")
        x_loaded = [sem(f"x_loaded{i}") for i in range(2)]; r_loaded = [sem(f"r_loaded{i}") for i in range(2)]
        stored = [sem(f"stored{i}") for i in range(2)]
        proj = Steps(sem("proj"), 2)
        u_kept = Steps(sem("u_kept"), 1)
        halo = Steps(sem("halo"), 1)
        conved = Steps(sem("conved"), 4)
        silu_z = Steps(sem("silu_z"), 1)
        silu = Steps(sem("silu"), 3)
        seg_p = Steps(sem("seg"), 1)
        turn = Steps(sem("turn"), 3)
        tok = Steps(sem("tok"), 4)
        tok_act = Steps(sem("tok_act"), 2)
        tok_pool = Steps(sem("tok_pool"), 2)
        scan = Steps(sem("scan"), 3)
        st_pool = Steps(sem("st_pool"), 1)
        y_dve = Steps(sem("y_dve"), 5)
        y_act = Steps(sem("y_act"), 1)
        ms_dve = Steps(sem("ms_dve"), 1); ms_pool = Steps(sem("ms_pool"), 1)
        yturn = Steps(sem("yturn"), 1); y_kept = Steps(sem("y_kept"), 1)
        gathered = [sem(f"gathered{i}") for i in range(2)]
        indexed, expert = Steps(sem("indexed"), 1), Steps(sem("expert"), 1)
        outp = Steps(sem("outp"), 1); summed = Steps(sem("summed"), 1)
        main = slice(0, P) if backward else slice(HALO, W)

        def tile(it):
            return it.turn * (-1 if backward else 1) + (it.lane * TB + (TB - 1 if backward else 0))

        def bc(ap, n):
            return ap.unsqueeze(2).to_broadcast([ap.shape[0], ap.shape[1], n])

        def heads(ap):
            return ap.rearrange("p (h d) -> p h d", h=NH)

        with nc.Block() as block:
            @block.sync
            def _(sp):
                sp.dma_start(w_raw[:], in_w.rearrange("(k p) e -> p k e", p=P)).then_inc(loaded, 16)
                sp.dma_start(conv[:], conv_cols.rearrange("p (c w) -> p c w", c=CX)).then_inc(loaded, 16)
                sp.dma_start(ow_raw[:], out_w.rearrange("(k p) e -> p k e", p=P)).then_inc(loaded, 16)
                sp.dma_start(norm_c[:], norm_cols).then_inc(loaded, 16)
                sp.dma_start(rows[:], head_rows.rearrange("p (v h) -> p v h", h=NH)).then_inc(loaded, 16)

            @block.gpsimd
            def _(pool):
                p = nc.gpsimd
                p.memset(upto[:], 1.0).then_inc(made, 1)
                p.memset(past[:], 1.0).then_inc(made, 1)
                p.memset(ones[:], 1.0).then_inc(made, 1)
                p.memset(state[:], 0.0).then_inc(made, 1)
                p.memset(u[:], 0.0).then_inc(made, 1)
                pool.wait_ge(made, 5)
                d = -1 if backward else 1
                p.affine_select(out=upto[:], in_=upto[:], compare_op=ALU.is_ge, fill=0.0, base=0,
                                pattern=[[d, P]], channel_multiplier=-d).then_inc(made, 1)
                p.affine_select(out=past[:], in_=past[:], compare_op=ALU.is_gt, fill=0.0, base=0,
                                pattern=[[-d, P]], channel_multiplier=d).then_inc(made, 1)

            @block.vector
            def _(dve):
                v = nc.vector
                n = [0]

                def done(i):
                    n[0] += 1
                    i.then_inc(prep, 1)
                    dve.wait_ge(prep, n[0])

                dve.wait_ge(loaded, 80)
                done(v.tensor_copy(w[0][:], w_raw[:]))
                done(v.tensor_tensor(w[1][:], w_raw[:], w[0][:].bitcast(F32), ALU.subtract))
                for c in range(CC):
                    done(v.tensor_scalar(ow[:, c, :], ow_raw[:, c, :], norm_c[:, c:c + 1], None, ALU.mult))
                row = lambda k: rows[:, k, :].unsqueeze(1).to_broadcast([P, NT, NH])
                done(v.tensor_tensor(t1[:], dt_raw[:, :, dt_col:dt_col + NH], row(0), ALU.add))
                assert n[0] == 7
                dve.wait_ge(prep_act, 2)
                done(v.tensor_scalar(grow[:], t2[:], 1.0, None, ALU.add))
                assert n[0] == 8
                done(v.tensor_scalar(dt[:], grow[:], -1.0, None, ALU.add))
                done(v.tensor_tensor(dt[:], dt[:], t2[:], ALU.subtract))
                done(v.reciprocal(fade[:], grow[:]))
                done(v.tensor_tensor(dt[:], dt[:], fade[:], ALU.mult))
                dve.wait_ge(prep_act, 3)
                done(v.tensor_tensor(dt[:], whole[:], dt[:], ALU.subtract))
                done(v.tensor_scalar(t1[:], t1[:], 0.0, None, ALU.max))
                done(v.tensor_tensor(dt[:], dt[:], t1[:], ALU.add))
                done(v.tensor_tensor(da[:], dt[:], row(1), ALU.mult))
                done(v.tensor_scalar(da[:], da[:], -1.0, None, ALU.mult))
                assert n[0] == 17

            @block.scalar
            def _(act):
                a = nc.scalar
                act.wait_ge(prep, 7)
                a.activation(t2[:], t1[:], ACT.Abs).then_inc(prep_act, 1)
                act.wait_ge(prep_act, 1)
                a.activation(t2[:], t2[:], ACT.Exp, scale=-1.0)
                a.activation(rows[:, 1, :], rows[:, 1, :], ACT.Exp).then_inc(prep_act, 1)
                act.wait_ge(prep, 8)
                a.activation(whole[:], grow[:], ACT.Ln).then_inc(prep_act, 1)
                act.wait_ge(prep_pe, 1)
                for n, to in enumerate((grow, fade, whole)):
                    a.activation(to[:].rearrange("p t h -> p (t h)"), bank[n][:], ACT.Exp).then_inc(prep_act, 1)

            @block.tensor
            def _(pe):
                pe.wait_ge(made, 7)
                pe.wait_ge(prep, 17)
                for n, m in enumerate((upto, past, ones)):
                    i = nc.tensor.matmul(bank[n][:], m[:], da[:].rearrange("p t h -> p (t h)"), start=True, stop=True)
                i.then_inc(prep_pe, 1)

        with nc.Block() as block:
            @block.sync
            def _(sp):
                def load(it):
                    row = tile(it) * P if isinstance(it.g, int) else sp.snap(tile(it) * P)
                    sp.wait_ge(proj.sem, proj.at(it.g - 2))
                    Carrier.carry(sp)
                    sp.dma_start(xt[it.s][:].bitcast(F32), xt1[bass.ds(row, P)]).then_inc(x_loaded[it.s], 16)

                def reload(it):
                    row = tile(it) * P if isinstance(it.g, int) else sp.snap(tile(it) * P)
                    sp.wait_ge(summed.sem, summed.at(it.g - 2))
                    Carrier.carry(sp)
                    if pick:
                        sp.wait_ge(expert.sem, expert.at(it.g - 2))
                        Carrier.carry(sp)
                    sp.dma_start(res[it.s][:], res_in_d[bass.ds(row, P), :]).then_inc(r_loaded[it.s], 16)

                def store(it):
                    row = tile(it) * P if isinstance(it.g, int) else sp.snap(tile(it) * P)
                    sp.wait_ge(summed.sem, summed.at(it.g))
                    Carrier.carry(sp)
                    sp.dma_start(res_out_d[bass.ds(row, P), :], out[it.s][:]).then_inc(stored[it.s], 16)

                pipelined(sp, 7, NT, 4, (6, store), (5, reload), (0, load))
                for s in range(2):
                    sp.wait_ge(stored[s], 16 * NT // 2)

            @block.gpsimd
            def _(pool):
                p = nc.gpsimd

                def segments(it):
                    T = tile(it)
                    pool.wait_ge(turn.sem, turn.at(it.g - 2))
                    Carrier.carry(pool)
                    p.tensor_tensor(seg[it.s][:], da[:, bass.ds(T, 1), :].rearrange("p o h -> p (o h)").unsqueeze(2).to_broadcast([P, NH, P]),
                                               upto[:].unsqueeze(1).to_broadcast([P, NH, P]), ALU.mult).then_inc(seg_p.sem, 1)

                def tokens(it):
                    T = tile(it)
                    pool.wait_ge(tok.sem, tok.at(it.g, 1))
                    Carrier.carry(pool)
                    pool.wait_ge(scan.sem, scan.at(it.g - 2))
                    Carrier.carry(pool)
                    p.tensor_tensor(heads(xw[it.s][:]), heads(xdt[it.s][:]),
                                                  fade[:, bass.ds(T, 1), :].rearrange("p o h -> p (o h)").unsqueeze(2).to_broadcast([P, NH, HD]), ALU.mult).then_inc(tok_pool.sem, 1)
                    pool.wait_ge(tok_act.sem, tok_act.at(it.g, 1))
                    Carrier.carry(pool)
                    pool.wait_ge(y_dve.sem, y_dve.at(it.g - 2))
                    Carrier.carry(pool)
                    p.tensor_tensor(heads(skip[it.s][:]), heads(x_tok[it.s][:]), bc(rows[:, 2, :], HD), ALU.mult).then_inc(tok_pool.sem, 1)

                def fade_state(it):
                    T = tile(it)
                    pool.wait_ge(y_dve.sem, y_dve.at(it.g - 2))
                    Carrier.carry(pool)
                    pool.wait_ge(y_dve.sem, y_dve.at(it.g - BATCH, 3))
                    Carrier.carry(pool)
                    p.tensor_tensor(heads(faded[it.s][:]), heads(state[:, it.lane, :]),
                                                 whole[0:NS, bass.ds(T, 1), :].rearrange("p o h -> p (o h)").unsqueeze(2).to_broadcast([NS, NH, HD]), ALU.mult).then_inc(st_pool.sem, 1)

                def root(it):
                    pool.wait_ge(ms_dve.sem, ms_dve.at(it.g))
                    pool.wait_ge(summed.sem, summed.at(it.g - 2))
                    p.tensor_tensor(rstd[it.s][:], ms[it.s][:], env.neg_half[:, 0:1], ALU.pow).then_inc(ms_pool.sem, 1)

                def index(it):
                    T = tile(it)
                    if it.again:
                        pool.wait_ge(gathered[it.s], it.q * 16)
                        Carrier.carry(pool)
                    p.tensor_copy(at[it.s][:], pick.read[:, bass.ds(T, 1)]).then_inc(indexed.sem, 1)

                def gather(it):
                    pool.wait_ge(indexed.sem, indexed.at(it.g))
                    Carrier.carry(pool)
                    pool.wait_ge(expert.sem, expert.at(it.g - 2))
                    Carrier.carry(pool)
                    pool.indirect_dma_start(got[it.s][:], None, expert_rows[:, :],
                                            bass.IndirectOffsetOnAxis(ap=at[it.s][:, 0:1], axis=0)).then_inc(gathered[it.s], 16)

                experts = [(4, index), (5, gather)] if pick else []
                for stage in (seg_p, tok_pool, st_pool, ms_pool, indexed):
                    stage.open(pool)
                pipelined(pool, 7, NT, 4, (5, root), (4, fade_state), (3, tokens), (2, segments), *experts)

            @block.vector
            def _(dve):
                v = nc.vector

                def convolve(it):
                    T_u = u[:, it.lane]
                    dve.wait_ge(u_kept.sem, u_kept.at(it.g))
                    dve.wait_ge(silu.sem, silu.at(it.g - 2))
                    for k in range(TAPS):
                        off = HALO - k if backward else k
                        for c in range(CX):
                            src = T_u[:, c, off:off + P]
                            if k == 0:
                                i = v.tensor_scalar(cv[it.s][:, c, :], src, conv[:, c, 0:1], conv[:, c, TAPS:TAPS + 1], ALU.mult, ALU.add)
                            else:
                                i = v.scalar_tensor_tensor(out=cv[it.s][:, c, :], in0=src, scalar=conv[:, c, k:k + 1],
                                                           in1=cv[it.s][:, c, :], op0=ALU.mult, op1=ALU.add)
                        i.then_inc(conved.sem, 1)
                        dve.wait_ge(conved.sem, conved.at(it.g, k + 1))

                def tokens(it):
                    T = tile(it)
                    dve.wait_ge(tok_act.sem, tok_act.at(it.g, 1))
                    dve.wait_ge(tok_pool.sem, tok_pool.at(it.g - 2))
                    dve.wait_ge(scan.sem, scan.at(it.g - 2))
                    v.tensor_tensor(heads(xdt[it.s][:]), heads(x_tok[it.s][:]), dt[:, bass.ds(T, 1), :].rearrange("p o h -> p (o h)").unsqueeze(2).to_broadcast([P, NH, HD]), ALU.mult).then_inc(tok.sem, 1)
                    dve.wait_ge(turn.sem, turn.at(it.g, 3))
                    v.tensor_copy(b_tok[it.s][:], pBT).then_inc(tok.sem, 1)
                    v.tensor_tensor(gm[:], pG, upto[:], ALU.mult).then_inc(tok.sem, 1)
                    dve.wait_ge(tok.sem, tok.at(it.g, 3))
                    dve.wait_ge(tok_act.sem, tok_act.at(it.g, 2))
                    v.tensor_tensor(mix[it.s][:], decay[:], gm[:].unsqueeze(1).to_broadcast([P, NH, P]), ALU.mult).then_inc(tok.sem, 1)

                def outputs(it):
                    T = tile(it)
                    dve.wait_ge(scan.sem, scan.at(it.g, 1))
                    v.tensor_tensor(heads(y1[:]), heads(pI), grow[:, bass.ds(T, 1), :].rearrange("p o h -> p (o h)").unsqueeze(2).to_broadcast([P, NH, HD]), ALU.mult).then_inc(y_dve.sem, 1)
                    dve.wait_ge(y_dve.sem, y_dve.at(it.g, 1))
                    dve.wait_ge(scan.sem, scan.at(it.g, 2))
                    v.tensor_tensor(y2[:], pY, y1[:], ALU.add).then_inc(y_dve.sem, 1)
                    dve.wait_ge(scan.sem, scan.at(it.g, 3))
                    dve.wait_ge(st_pool.sem, st_pool.at(it.g))
                    v.tensor_tensor(state[:, it.lane, :], pS, faded[it.s][:], ALU.add).then_inc(y_dve.sem, 1)
                    dve.wait_ge(y_dve.sem, y_dve.at(it.g, 3))
                    dve.wait_ge(tok_pool.sem, tok_pool.at(it.g))
                    v.tensor_tensor(y3[:], y2[:], skip[it.s][:], ALU.add).then_inc(y_dve.sem, 1)
                    dve.wait_ge(y_dve.sem, y_dve.at(it.g, 4))
                    dve.wait_ge(yturn.sem, yturn.at(it.g - 2))
                    dve.wait_ge(y_act.sem, y_act.at(it.g - 2))
                    v.tensor_tensor(yz[it.s][:], y3[:], gate[it.lane][:], ALU.mult).then_inc(y_dve.sem, 1)

                def mean_square(it):
                    dve.wait_ge(y_act.sem, y_act.at(it.g))
                    dve.wait_ge(ms_pool.sem, ms_pool.at(it.g - 2))
                    v.tensor_scalar(ms[it.s][:], ss[it.s][:], 1.0 / DI, EPS, ALU.mult, ALU.add).then_inc(ms_dve.sem, 1)

                def add_expert(it):
                    T = tile(it)
                    dve.wait_ge(gathered[it.s], it.q * 16 + 16)
                    dve.wait_ge(r_loaded[it.s], it.q * 16 + 16)
                    dve.wait_ge(summed.sem, summed.at(it.g - 2))
                    v.scalar_tensor_tensor(out=sum_e[it.s][:], in0=got[it.s][:], scalar=pick.weight[:, bass.ds(T, 1)],
                                           in1=res[it.s][:], op0=ALU.mult, op1=ALU.add).then_inc(expert.sem, 1)

                def add_out(it):
                    dve.wait_ge(outp.sem, outp.at(it.g))
                    dve.wait_ge(ms_pool.sem, ms_pool.at(it.g))
                    if pick:
                        dve.wait_ge(expert.sem, expert.at(it.g))
                    else:
                        dve.wait_ge(r_loaded[it.s], it.q * 16 + 16)
                    if it.again:
                        dve.wait_ge(stored[it.s], it.q * 16)
                    v.scalar_tensor_tensor(out=out[it.s][:], in0=pO, scalar=rstd[it.s][:], in1=sum_e[it.s][:] if pick else res[it.s][:], op0=ALU.mult, op1=ALU.add).then_inc(summed.sem, 1)

                experts = [(6, add_expert)] if pick else []
                for stage in (conved, tok, y_dve, ms_dve, summed, expert):
                    stage.open(dve)
                pipelined(dve, 7, NT, 4, *experts, (6, add_out), (5, mean_square), (4, outputs), (3, tokens), (2, convolve))

            @block.scalar
            def _(act):
                a = nc.scalar

                def keep(it):
                    T_u = u[:, it.lane]
                    act.wait_ge(conved.sem, conved.at(it.g - BATCH))
                    frm, to = (slice(0, HALO), slice(P, W)) if backward else (slice(P, W), slice(0, HALO))
                    a.activation(T_u[:, :, to], T_u[:, :, frm], ACT.Copy).then_inc(halo.sem, 1)
                    act.wait_ge(halo.sem, halo.at(it.g, 1))
                    act.wait_ge(proj.sem, proj.at(it.g, 1))
                    a.activation(T_u[:, 0:CC, main], pB0, ACT.Copy)
                    a.activation(T_u[:, CC, main], pB1, ACT.Copy).then_inc(u_kept.sem, 1)

                def project(it):
                    keep(it)
                    act.wait_ge(proj.sem, proj.at(it.g, 2))
                    act.wait_ge(y_dve.sem, y_dve.at(it.g - 4))
                    a.activation(gate[it.lane][:], pZ, ACT.Silu).then_inc(silu_z.sem, 1)

                def activate(it):
                    act.wait_ge(conved.sem, conved.at(it.g))
                    act.wait_ge(turn.sem, turn.at(it.g - 2))
                    act.wait_ge(scan.sem, scan.at(it.g - 2))
                    a.activation(xc[it.s][:], cv[it.s][:, 0:CC, :], ACT.Silu).then_inc(silu.sem, 1)
                    a.activation(bt[it.s][:], cv[it.s][0:NS, CC, :], ACT.Silu).then_inc(silu.sem, 1)
                    a.activation(ct[it.s][:], cv[it.s][NS:P, CC, :], ACT.Silu).then_inc(silu.sem, 1)

                def tokens(it):
                    act.wait_ge(turn.sem, turn.at(it.g, 2))
                    act.wait_ge(tok_pool.sem, tok_pool.at(it.g - 2))
                    act.wait_ge(tok.sem, tok.at(it.g - 2))
                    a.activation(x_tok[it.s][:], pX, ACT.Copy).then_inc(tok_act.sem, 1)
                    act.wait_ge(turn.sem, turn.at(it.g, 1))
                    act.wait_ge(tok.sem, tok.at(it.g - 1))
                    for half in range(2):
                        i = a.activation(decay[:, half * 4:half * 4 + 4, :], pD[half], ACT.Exp)
                    i.then_inc(tok_act.sem, 1)

                def square(it):
                    act.wait_ge(y_dve.sem, y_dve.at(it.g))
                    act.wait_ge(ms_dve.sem, ms_dve.at(it.g - 2))
                    a.activation(sq[:], yz[it.s][:], ACT.Square, accum_out=ss[it.s][:]).then_inc(y_act.sem, 1)

                def keep_turned(it):
                    act.wait_ge(yturn.sem, yturn.at(it.g))
                    act.wait_ge(outp.sem, outp.at(it.g - 2))
                    a.activation(yt[it.s][:], pYT, ACT.Copy).then_inc(y_kept.sem, 1)

                for stage in (u_kept, halo, silu_z, silu, tok_act, y_act, y_kept):
                    stage.open(act)
                pipelined(act, 7, NT, 4, (5, keep_turned), (3, tokens), (1, project), (4, square), (2, activate))

            @block.tensor
            def _(pe):
                t_ = nc.tensor

                def cap(g):
                    return min(g, NT - 1) if isinstance(g, int) else g

                def project(it):
                    pe.wait_ge(x_loaded[it.s], it.q * 16 + 16)
                    pe.wait_ge(y_kept.sem, y_kept.at(it.g - 4))
                    pe.wait_ge(y_dve.sem, y_dve.at(it.g - 3, 3))
                    pe.wait_ge(u_kept.sem, u_kept.at(it.g - 1))
                    for c in range(CX):
                        n = 0
                        for k in range(KD):
                            for i, j in PARTS:
                                last = t_.matmul(pB0[:, c, :] if c < CC else pB1, w[i][:, k, DI + c * P:DI + (c + 1) * P],
                                                 xt[it.s][:, j, k, :], start=(n == 0), stop=(n == 5))
                                n += 1
                    last.then_inc(proj.sem, 1)
                    pe.wait_ge(silu_z.sem, silu_z.at(it.g - 1))
                    n = 0
                    for k in range(KD):
                        for i, j in PARTS:
                            last = t_.matmul(pZ, xt[it.s][:, i, k, :], w[j][:, k, 0:DI], start=(n == 0), stop=(n == 5))
                            n += 1
                    last.then_inc(proj.sem, 1)

                def tokens(it):
                    pe.wait_ge(seg_p.sem, seg_p.at(it.g))
                    pe.wait_ge(tok_act.sem, tok_act.at(it.g - 1))
                    for half in range(2):
                        i = t_.matmul(pD[half], past[:], seg[it.s][:, half * 4:half * 4 + 4, :], start=True, stop=True)
                    i.then_inc(turn.sem, 1)
                    pe.wait_ge(silu.sem, silu.at(it.g))
                    pe.wait_ge(tok_act.sem, tok_act.at(it.g - 1))
                    for c in range(CC):
                        i = t_.transpose(pX[:, c * P:(c + 1) * P], xc[it.s][:, c, :], env.ident[:])
                    i.then_inc(turn.sem, 1)
                    pe.wait_ge(summed.sem, summed.at(it.g - 3))
                    pe.wait_ge(tok.sem, tok.at(it.g - 1, 3))
                    t_.matmul(pG, bt[it.s][:], ct[it.s][:], start=True, stop=True)
                    t_.transpose(pBT, bt[it.s][:], env.ident[0:NS, 0:NS]).then_inc(turn.sem, 1)

                def scans(it):
                    pe.wait_ge(y_dve.sem, y_dve.at(it.g - BATCH, 3))
                    pe.wait_ge(silu_z.sem, silu_z.at(cap(it.g + 2)))
                    t_.matmul(pI, ct[it.s][:], state[:, it.lane, :], start=True, stop=True).then_inc(scan.sem, 1)
                    pe.wait_ge(tok.sem, tok.at(it.g))
                    pe.wait_ge(y_dve.sem, y_dve.at(it.g - 1, 2))
                    for h in range(NH):
                        i = t_.matmul(pY[:, h * HD:(h + 1) * HD], mix[it.s][:, h, :], xdt[it.s][:, h * HD:(h + 1) * HD], start=True, stop=True)
                    i.then_inc(scan.sem, 1)
                    pe.wait_ge(tok_pool.sem, tok_pool.at(it.g, 1))
                    pe.wait_ge(u_kept.sem, u_kept.at(cap(it.g + 2)))
                    t_.matmul(pS, b_tok[it.s][:], xw[it.s][:], start=True, stop=True).then_inc(scan.sem, 1)

                def turn_y(it):
                    pe.wait_ge(y_dve.sem, y_dve.at(it.g))
                    pe.wait_ge(u_kept.sem, u_kept.at(cap(it.g + 3)))
                    for c in range(CC):
                        i = t_.transpose(pYT[:, c, :], yz[it.s][:, c * P:(c + 1) * P], env.ident[:])
                    i.then_inc(yturn.sem, 1)

                def project_out(it):
                    pe.wait_ge(y_kept.sem, y_kept.at(it.g))
                    pe.wait_ge(summed.sem, summed.at(it.g - 1))
                    pe.wait_ge(tok.sem, tok.at(cap(it.g + 2), 3))
                    for c in range(CC):
                        i = t_.matmul(pO, yt[it.s][:, c, :], ow[:, c, :], start=(c == 0), stop=(c == CC - 1))
                    i.then_inc(outp.sem, 1)

                for stage in (proj, turn, scan, yturn, outp):
                    stage.open(pe)
                pipelined(pe, 7, NT, 4, (6, project_out), (5, turn_y), (4, scans), (3, tokens), (1, project))


def program(nc, x, attn_w, router_w, cols0, bo_rows, rb_rows, w_fc, w_gate, w_proj, e_cols, e_rows, head_w,
            f_in, f_conv, f_out, f_norm, f_heads, b_in, b_conv, b_out, b_norm, b_heads, w_experts, final):
    NT = T // P
    rows_l0, rows_l1 = E0 * ROWS0, E1 * CAP1

    def dram(name, shape):
        return nc.dram_tensor("dram_" + name, shape, F32, kind="Internal").ap()

    xn0, res0, res1, res2, xn1 = (dram(n, [T, D]) for n in ("xn0", "res0", "res1", "res2", "xn1"))
    xt1 = dram("xt1", [T, 2, KD, P])
    buf0, buf1 = dram("buf0", [rows_l0 + 2 * T, D]), dram("buf1", [rows_l1 + T, D])
    out0, out1 = dram("out0", [rows_l0, D]), dram("out1", [rows_l1, D])

    env = Env(nc)
    with ExitStack() as outer:
        keep = lambda n, s, d=F32: outer.enter_context(nc.sbuf_tensor(n, s, d))
        Carrier.sem = nc.alloc_semaphore("carrier")
        env.ident, env.neg_half = keep("ident", [P, P]), keep("neg_half", [P, 4])
        env.logits = keep("logits0", [P, NT, 8])
        logits1, dt_raw = keep("logits1", [P, NT, E1]), keep("dt_raw", [P, NT, 2 * NH])
        picks0 = [Pick(keep, f"pick0_{k}", NT) for k in range(2)]
        picks1 = [Pick(keep, "pick1", NT)]
        with env.phase(), ExitStack() as ctx:
            setup_l0(nc, env, ctx, attn_w, router_w, cols0, bo_rows, rb_rows)
            tokens_l0(nc, env, x, xn0, res0, ((buf0, rows_l0), (buf1, rows_l1)))
        with env.phase():
            route(nc, env, "r0", env.logits, E0, 2, BATCH, CAP0, ROWS0, rows_l0, picks0)
        with env.phase():
            scatter(nc, env, "s0", xn0, buf0, picks0, NT)
        with env.phase():
            experts_l0(nc, env, buf0, out0, w_fc, w_gate, w_proj, e_cols, e_rows)
        with env.phase():
            combine_l0(nc, env, out0, picks0, res0, res1, xn1, xt1, head_w, logits1, dt_raw, NT)
        with env.phase():
            route(nc, env, "r1", logits1, E1, 1, 1, CAP1, CAP1, rows_l1, picks1)
        with env.phase():
            scatter(nc, env, "s1", xn1, buf1, picks1, NT)
        with env.phase():
            experts_l1(nc, env, buf1, out1, w_experts)
        with env.phase():
            mixer(nc, env, "mf", False, f_in, f_conv, f_out, f_norm, f_heads, dt_raw, 0, xt1, res1, res2)
        with env.phase():
            mixer(nc, env, "mb", True, b_in, b_conv, b_out, b_norm, b_heads, dt_raw, NH, xt1, res2, final, out1, picks1[0])


class Env:

    def __init__(self, nc):
        self.nc = nc

    def phase(self):
        return self.nc.cleanup_on_exit()

    def sem(self, name):
        return self.nc.alloc_semaphore(name)



def _laid_out(i):
    import numpy as np

    p0, p1 = "L0_attn_", "L0_ffn_"

    def columns(a):
        return a.reshape(-1, P).T

    out = {
        "x": i[p0 + "x"].reshape(T, D),
        "attn_w": np.stack([i[p0 + n].T for n in ("Wk", "Wq", "Wv", "Wkp", "Wqp", "Wo")]),
        "router_w": i[p1 + "router_w"],
        "cols0": np.concatenate([columns(i[p0 + n]) for n in ("bk", "bq", "bv", "bkp", "bqp", "phase_scale", "ln_g", "ln_b")], 1),
        "bo_rows": np.tile(i[p0 + "bo"], (P, 1)),
        "rb_rows": np.tile(i[p1 + "router_b"], (P, 1)),
        "w_fc": i[p1 + "w_c_fc"], "w_gate": i[p1 + "w_gate"], "w_proj": i[p1 + "w_c_proj"],
        "e_cols": np.concatenate([columns(i[p1 + "b_c_fc"]), columns(i[p1 + "b_gate"])], 1),
        "e_rows": np.tile(i[p1 + "b_c_proj"].reshape(1, -1), (P, 1)),
        "head_w": np.concatenate([i["L1_ffn_w_router"]] + [i[f"L1_attn_{d}_in_w"][-NH:].T for d in "fb"], 1),
    }
    for d in "fb":
        q = f"L1_attn_{d}_"
        conv = np.concatenate([i[q + "conv_w"], i[q + "conv_b"][:, None]], 1)
        out[d + "_in"] = i[q + "in_w"][:-NH].T
        out[d + "_conv"] = conv.reshape(CX, P, TAPS + 1).transpose(1, 0, 2).reshape(P, -1)
        out[d + "_out"] = i[q + "out_w"].T
        out[d + "_norm"] = columns(i[q + "norm_w"])
        out[d + "_heads"] = np.tile(np.concatenate([i[q + n] for n in ("dt_bias", "A_log", "Dp")]), (P, 1))
    out["w_experts"] = np.stack([i["L1_ffn_" + n] for n in ("w_gate", "w_up", "w_down")], 1)
    return {n: np.ascontiguousarray(a) for n, a in out.items()}


def kernel(**inputs):
    import numpy as _np
    import concourse.bacc as _bacc
    from concourse.bass_utils import run_bass_kernel_spmd as _run

    nc = _bacc.Bacc("TRN2", target_bir_lowering=False, num_devices=1)
    laid = _laid_out({n: _np.asarray(a) for n, a in inputs.items()})
    arrays, args = {}, []
    for name, a in laid.items():
        arrays[f"in_{name}"] = a
        args.append(nc.dram_tensor(f"in_{name}", a.shape, mybir.dt.from_np(a.dtype), kind="ExternalInput").ap())
    args.append(nc.dram_tensor("final", (T, D), F32, kind="ExternalOutput").ap())
    program(nc, *args)
    r = _run(nc, [arrays], core_ids=[0])
    return r.results[0]["final"].reshape(BATCH, SEQ, D)
```

```python
import concourse.bass as bass
from concourse import mybir
from contextlib import ExitStack

F32 = mybir.dt.float32
F32R = mybir.dt.float32r
U32 = mybir.dt.uint32
ALU = mybir.AluOpType
ACT = mybir.ActivationFunctionType
AX = mybir.AxisListType.X




class Item:

    def __init__(self, c, r=None, unroll=2):
        self.g = c if r is None else r * unroll + c
        self.s = c % 2
        self.q = c // 2 if r is None else r * (unroll // 2) + c // 2
        self.lane = c % unroll
        self.turn = c // unroll if r is None else r + c // unroll
        self.again = r is not None or c >= 2
        self.again_lane = r is not None or c >= unroll


class Carrier:

    sem = None

    @classmethod
    def carry(cls, eng):
        eng.sem_inc(cls.sem, 1)


def pipelined(eng, depth, items, unroll, *stages):
    head = depth + 1
    rounds = (items - head) // unroll

    def step(base, r):
        for lag, stage in stages:
            c = base - lag
            if r is not None or 0 <= c < items:
                stage(Item(c, r, unroll))

    for t in range(head):
        step(t, None)
    with eng.Fori(0, rounds) as r:
        for u in range(unroll):
            step(head + u, r)
    for t in range(head + unroll * rounds, items + depth - 1):
        step(t, None)


class Steps:

    AHEAD = 4

    def __init__(self, sem, per):
        self.sem, self.per = sem, per
        self.credit = self.AHEAD * per + 1

    def open(self, eng):
        eng.sem_inc(self.sem, self.credit)

    def at(self, g, k=None):
        return g * self.per + ((self.per if k is None else k) + self.credit)


def at_row(eng, it, rows):
    return it.g * rows if isinstance(it.g, int) else eng.snap(it.g * rows)


import math

T, D, P = 8192, 256, 128
NT = T // P
KD = D // P
INV_2PI = 1.0 / (2.0 * math.pi)
ROUND = 1.5 * 2.0 ** 23
TWO_PI_HI = 6.28125
TWO_PI_LO = 2.0 * math.pi - TWO_PI_HI
PI_BELOW = 3.1415925
HALF_PI = math.pi / 2
CHUNK = 64
EPS = 1e-5
ZERO_ROWS = 5

PARTS = ((0, 0), (0, 1), (1, 0))


def setup_l0(nc, env, ctx, attn_w, router_w, cols0, bo_rows, rb_rows):
    sb, sem = lambda n, s, d=F32: ctx.enter_context(nc.sbuf_tensor(n, s, d)), env.sem
    env.half_pi = sb("half_pi", [P, 1])
    env.cols = sb("cols", [P, 8, KD])
    env.scale4 = sb("scale4", [P, 4])
    env.bo_rows = sb("bo_rows", [P, D])
    env.rb_rows = sb("rb_rows", [P, 8])
    env.seg = sb("seg", [P, D])
    env.wraw = sb("wraw", [P, 6, KD, D])
    env.w = [sb("w_hi", [P, 6, KD, D], F32R), sb("w_lo", [P, 6, KD, D], F32R)]
    env.rwraw = sb("rwraw", [P, KD, 8])
    env.rw = [sb("rw_hi", [P, KD, 8], F32R), sb("rw_lo", [P, KD, 8], F32R)]
    loaded, pool_done, dve_done = sem("const_loaded"), sem("const_pool"), sem("const_dve")
    with nc.Block() as block:
        @block.sync
        def _(sp):
            sp.dma_start(env.wraw[:], attn_w.rearrange("w (k p) e -> p w k e", p=P)).then_inc(loaded, 16)
            sp.dma_start(env.rwraw[:], router_w.rearrange("(k p) e -> p k e", p=P)).then_inc(loaded, 16)
            sp.dma_start(env.cols[:], cols0.rearrange("p (v k) -> p v k", k=KD)).then_inc(loaded, 16)
            sp.dma_start(env.bo_rows[:], bo_rows).then_inc(loaded, 16)
            sp.dma_start(env.rb_rows[:], rb_rows).then_inc(loaded, 16)

        @block.gpsimd
        def _(pool):
            nc.gpsimd.memset(env.ident[:], 0.0).then_inc(pool_done, 1)
            pool.wait_ge(pool_done, 1)
            nc.gpsimd.affine_select(out=env.ident[:], in_=env.ident[:], compare_op=ALU.not_equal, fill=1.0,
                                    base=0, pattern=[[-1, P]], channel_multiplier=1).then_inc(pool_done, 1)

        @block.vector
        def _(dve):
            nc.vector.memset(env.neg_half[:], -0.5)
            nc.vector.memset(env.seg[:], 1.0).then_inc(dve_done, 1)
            nc.vector.memset(env.half_pi[:], HALF_PI)
            dve.wait_ge(dve_done, 1)
            nc.vector.memset(env.seg[:].rearrange("p (c t) -> p c t", t=CHUNK)[:, :, 0:1], 0.0).then_inc(dve_done, 1)
            dve.wait_ge(loaded, 80)
            nc.vector.tensor_copy(env.w[0][:], env.wraw[:]).then_inc(dve_done, 1)
            nc.vector.tensor_copy(env.rw[0][:], env.rwraw[:]).then_inc(dve_done, 1)
            for n in range(2):
                nc.vector.tensor_copy(env.scale4[:, n * KD:(n + 1) * KD], env.cols[:, 5, :])
            nc.vector.tensor_scalar(env.cols[:, 2, :], env.cols[:, 2, :], 1.0 / math.sqrt(D), None, ALU.mult).then_inc(dve_done, 1)
            dve.wait_ge(dve_done, 5)
            nc.vector.tensor_tensor(env.w[1][:], env.wraw[:], env.w[0][:].bitcast(F32), ALU.subtract).then_inc(dve_done, 1)
            nc.vector.tensor_tensor(env.rw[1][:], env.rwraw[:], env.rw[0][:].bitcast(F32), ALU.subtract).then_inc(dve_done, 1)
            dve.wait_ge(dve_done, 7)


BK, BQ, BV, BKP, BQP, PSC, LNG, LNB = range(8)
WK, WQ, WV, WKP, WQP, WO = range(6)


def tokens_l0(nc, env, x, xn0, res0, buffers):
    G = 2 * P
    ITEMS = T // G
    with ExitStack() as ctx:
        sb = lambda n, s, d=F32: ctx.enter_context(nc.sbuf_tensor(n, s, d))
        ps = lambda n, s, d=F32: ctx.enter_context(nc.psum_tensor(n, s, d))
        sem = env.sem
        two = lambda n, s, d=F32: [sb(f"{n}{i}", s, d) for i in range(2)]
        x_in = two("x_in", [P, 2, D])
        stats = sb("stats", [P, 2, 6]); mv = sb("mv", [P, 2, 2]); var = sb("var", [P, 2]); rstd = sb("rstd", [P, 2])
        xn = two("xn", [P, 2, D])
        res = two("res", [P, 2, D]); res_t = sb("res_t", [P, 2, D])
        xt = [two("xt_hi", [P, KD, G], F32R), two("xt_lo", [P, KD, G], F32R)]
        kq = [two("kq_hi", [P, 4, G], F32R), two("kq_lo", [P, 4, G], F32R)]
        val = [sb(f"val{i}", [P, KD, G]) for i in range(4)]
        ph = two("ph", [P, 4, G]); turns = sb("turns", [P, 4, G]); ang = sb("ang", [P, 4, G])
        sin = two("sin", [P, 4, G]); cos = two("cos", [P, 4, G])
        apart = sb("apart", [P, 4, G])
        bound = sb("bound", [P, 4, G]); mem = sb("mem", [P, 4, G]); ret = two("ret", [P, KD, G])
        prod = sb("prod", [P, 4, G])
        stats2 = sb("stats2", [P, 2, 6]); mv2 = sb("mv2", [P, 2, 2]); var2 = sb("var2", [P, 2]); rstd2 = sb("rstd2", [P, 2])
        zt = two("zt", [P, 2, D])
        zf = sb("zf", [P, KD, G])
        z = [two("z_hi", [P, KD, G], F32R), two("z_lo", [P, KD, G], F32R)]
        res_in = two("res_in", [P, 2, D]); res_out = two("res_out", [P, 2, D])
        pT = ps("pT", [P, KD, G]); pK = ps("pK", [P, KD, G]); pQ = ps("pQ", [P, KD, G]); pC = ps("pC", [P, KD, G])
        pE = ps("pE", [P, 2, D]); pF = ps("pF", [P, KD, G]); pG = ps("pG", [P, 2, D]); pL = ps("pL", [P, 2, 8])

        shares = [n // ITEMS for _, n in buffers]
        zeros = sb("zeros", [P, ZERO_ROWS * D]); zeroed, zeros_set = sem("zeroed"), sem("zeros_set")
        x_loaded = [sem(f"x_loaded{i}") for i in range(2)]
        r_loaded = [sem(f"r_loaded{i}") for i in range(2)]
        xn_stored, res_stored, out_stored = ([sem(f"{n}{i}") for i in range(2)] for n in ("xn_stored", "res_stored", "out_stored"))
        norm = Steps(sem("norm_dve"), 7)
        low = Steps(sem("x_low"), 1)
        norm_pool = Steps(sem("norm_pool"), 3)
        turned = Steps(sem("x_turned"), 1)
        high = Steps(sem("x_high"), 1)
        projected = Steps(sem("projected"), 4)
        proj_act = Steps(sem("proj_act"), 3)
        proj_dve = Steps(sem("proj_dve"), 3)
        phased = Steps(sem("phase_pe"), 2)
        tanhs = Steps(sem("tanhs"), 2)
        scaled = Steps(sem("scaled"), 1)
        ph_dve = Steps(sem("phase_dve"), 5)
        sines = Steps(sem("sines"), 3)
        bound_p = Steps(sem("bound_pool"), 2)
        mem_dve = Steps(sem("memory_dve"), 7)
        back = Steps(sem("ret_turned"), 1)
        ln_dve = Steps(sem("ln_dve"), 7)
        ln_pool = Steps(sem("ln_pool"), 1)
        z_turned = Steps(sem("z_turned"), 1)
        z_act = Steps(sem("z_act"), 1)
        z_dve = Steps(sem("z_dve"), 1)
        z_pool = Steps(sem("z_pool"), 1)
        out_pe = Steps(sem("out_pe"), 1)
        out_dve = Steps(sem("out_dve"), 1)

        def rows(ap, row):
            return ap[bass.ds(row, G), :].rearrange("(t p) d -> p t d", p=P)

        with nc.Block() as block:
            @block.sync
            def _(sp):
                def load(it):
                    row = at_row(sp, it, G)
                    sp.wait_ge(norm.sem, norm.at(it.g - 2, 7))
                    Carrier.carry(sp)
                    sp.wait_ge(norm_pool.sem, norm_pool.at(it.g - 2, 2))
                    Carrier.carry(sp)
                    sp.dma_start(x_in[it.s][:], rows(x, row)).then_inc(x_loaded[it.s], 16)

                def store(it):
                    row = at_row(sp, it, G)
                    sp.wait_ge(norm.sem, norm.at(it.g, 7))
                    Carrier.carry(sp)
                    sp.dma_start(rows(xn0, row), xn[it.s][:]).then_inc(xn_stored[it.s], 16)
                    sp.wait_ge(norm_pool.sem, norm_pool.at(it.g, 3))
                    Carrier.carry(sp)
                    sp.dma_start(rows(res0, row), res[it.s][:]).then_inc(res_stored[it.s], 16)

                def reload(it):
                    row = at_row(sp, it, G)
                    sp.wait_ge(out_dve.sem, out_dve.at(it.g - 2))
                    Carrier.carry(sp)
                    sp.wait_ge(res_stored[it.s], 16 * it.q + 16)
                    Carrier.carry(sp)
                    sp.dma_start(res_in[it.s][:], rows(res0, row)).then_inc(r_loaded[it.s], 16)

                def zero(it):
                    for (buf, _), share in zip(buffers, shares):
                        row = it.g * share if isinstance(it.g, int) else sp.snap(it.g * share)
                        part = share // ZERO_ROWS
                        sp.dma_start(buf[bass.ds(row, share), :].rearrange("(p r) d -> p (r d)", r=ZERO_ROWS), zeros[0:part, :]).then_inc(zeroed, 16)

                def finish(it):
                    row = at_row(sp, it, G)
                    sp.wait_ge(out_dve.sem, out_dve.at(it.g))
                    Carrier.carry(sp)
                    sp.dma_start(rows(res0, row), res_out[it.s][:]).then_inc(out_stored[it.s], 16)

                sp.wait_ge(zeros_set, 1)
                pipelined(sp, 8, ITEMS, 4, (0, load), (0, zero), (1, store), (7, finish), (6, reload))
                sp.wait_ge(zeroed, 16 * len(buffers) * ITEMS)
                for s in range(2):
                    sp.wait_ge(xn_stored[s], 16 * ITEMS // 2)
                    sp.wait_ge(out_stored[s], 16 * ITEMS // 2)

            @block.vector
            def _(dve):
                v = nc.vector
                v.memset(zeros[:], 0.0).then_inc(zeros_set, 1)

                def normalise(it):
                    dve.wait_ge(x_loaded[it.s], 16 * it.q + 16)
                    dve.wait_ge(norm_pool.sem, norm_pool.at(it.g - 1, 1))
                    for t in range(2):
                        v.bn_stats(stats[:, t, :], x_in[it.s][:, t, :]).then_inc(norm.sem, 1)
                    dve.wait_ge(norm.sem, norm.at(it.g, 2))
                    Carrier.carry(dve)
                    for t in range(2):
                        v.bn_aggr(mv[:, t, :], stats[:, t, :]).then_inc(norm.sem, 1)
                    dve.wait_ge(norm.sem, norm.at(it.g, 4))
                    v.tensor_scalar(var[:], mv[:, :, 1], EPS, None, ALU.add).then_inc(norm.sem, 1)

                def center(it):
                    dve.wait_ge(norm_pool.sem, norm_pool.at(it.g, 1))
                    if it.again:
                        dve.wait_ge(xn_stored[it.s], 16 * it.q)
                    dve.wait_ge(turned.sem, turned.at(it.g - 2))
                    dve.wait_ge(norm_pool.sem, norm_pool.at(it.g - 2))
                    for t in range(2):
                        v.tensor_scalar(xn[it.s][:, t, :], x_in[it.s][:, t, :], mv[:, t, 0:1], rstd[:, t:t + 1],
                                                  ALU.subtract, ALU.mult).then_inc(norm.sem, 1)

                def x_low(it):
                    dve.wait_ge(high.sem, high.at(it.g))
                    dve.wait_ge(projected.sem, projected.at(it.g - 2))
                    v.tensor_tensor(xt[1][it.s][:], pT[:], xt[0][it.s][:].bitcast(F32), ALU.subtract).then_inc(low.sem, 1)

                def project(it):
                    for n, (bank, bias) in enumerate(((pK, BK), (pQ, BQ))):
                        dve.wait_ge(proj_act.sem, proj_act.at(it.g, n + 1))
                        dve.wait_ge(phased.sem, phased.at(it.g - 2))
                        for c in range(KD):
                            i = v.scalar_tensor_tensor(out=kq[1][it.s][:, 2 * n + c, :], in0=bank[:, c, :],
                                                       scalar=env.cols[:, bias, c:c + 1],
                                                       in1=kq[0][it.s][:, 2 * n + c, :].bitcast(F32), op0=ALU.add, op1=ALU.subtract)
                        i.then_inc(proj_dve.sem, 1)
                    dve.wait_ge(projected.sem, projected.at(it.g, 3))
                    for t in range(2):
                        i = v.tensor_tensor(env.logits[:, bass.ds(it.g * 2 + t, 1), :] if not isinstance(it.g, int) else
                                            env.logits[:, it.g * 2 + t:it.g * 2 + t + 1, :],
                                            pL[:, t:t + 1, :], env.rb_rows[:].rearrange("p (o e) -> p o e", o=1), ALU.add)
                    i.then_inc(proj_dve.sem, 1)

                def phase(it):
                    dve.wait_ge(scaled.sem, scaled.at(it.g))
                    v.tensor_scalar(turns[:], ph[it.s][:], INV_2PI, ROUND, ALU.mult, ALU.add).then_inc(ph_dve.sem, 1)
                    dve.wait_ge(ph_dve.sem, ph_dve.at(it.g, 1))
                    v.tensor_scalar(turns[:], turns[:], ROUND, None, ALU.subtract).then_inc(ph_dve.sem, 1)
                    dve.wait_ge(ph_dve.sem, ph_dve.at(it.g, 2))
                    v.scalar_tensor_tensor(out=ph[it.s][:], in0=turns[:], scalar=-TWO_PI_HI, in1=ph[it.s][:], op0=ALU.mult, op1=ALU.add).then_inc(ph_dve.sem, 1)
                    dve.wait_ge(ph_dve.sem, ph_dve.at(it.g, 3))
                    v.scalar_tensor_tensor(out=ph[it.s][:], in0=turns[:], scalar=-TWO_PI_LO, in1=ph[it.s][:], op0=ALU.mult, op1=ALU.add).then_inc(ph_dve.sem, 1)
                    dve.wait_ge(ph_dve.sem, ph_dve.at(it.g, 4))
                    dve.wait_ge(sines.sem, sines.at(it.g - 1))
                    v.tensor_scalar(ang[:], ph[it.s][:], PI_BELOW, -PI_BELOW, ALU.min, ALU.max).then_inc(ph_dve.sem, 1)

                def memory(it):
                    for n in range(2):
                        dve.wait_ge(bound_p.sem, bound_p.at(it.g, n + 1))
                        for c in range(KD):
                            v.tensor_tensor_scan(mem[:, 2 * n + c, :], env.seg[:], bound[:, 2 * n + c, :], 0.0, ALU.mult, ALU.add).then_inc(mem_dve.sem, 1)
                    dve.wait_ge(mem_dve.sem, mem_dve.at(it.g, 4))
                    v.tensor_tensor(prod[:, 0:2, :], mem[:, 0:2, :], cos[it.s][:, 2:4, :], ALU.mult).then_inc(mem_dve.sem, 1)
                    v.tensor_tensor(prod[:, 2:4, :], mem[:, 2:4, :], sin[it.s][:, 2:4, :], ALU.mult).then_inc(mem_dve.sem, 1)
                    dve.wait_ge(mem_dve.sem, mem_dve.at(it.g, 6))
                    dve.wait_ge(back.sem, back.at(it.g - 2))
                    v.tensor_tensor(ret[it.s][:], prod[:, 0:2, :], prod[:, 2:4, :], ALU.add).then_inc(mem_dve.sem, 1)

                def normalise_ret(it):
                    dve.wait_ge(back.sem, back.at(it.g))
                    for t in range(2):
                        v.bn_stats(stats2[:, t, :], pE[:, t, :]).then_inc(ln_dve.sem, 1)
                    dve.wait_ge(ln_dve.sem, ln_dve.at(it.g, 2))
                    Carrier.carry(dve)
                    for t in range(2):
                        v.bn_aggr(mv2[:, t, :], stats2[:, t, :]).then_inc(ln_dve.sem, 1)
                    dve.wait_ge(ln_dve.sem, ln_dve.at(it.g, 4))
                    v.tensor_scalar(var2[:], mv2[:, :, 1], EPS, None, ALU.add).then_inc(ln_dve.sem, 1)

                def center_ret(it):
                    dve.wait_ge(ln_pool.sem, ln_pool.at(it.g))
                    dve.wait_ge(z_turned.sem, z_turned.at(it.g - 2))
                    for t in range(2):
                        v.tensor_scalar(zt[it.s][:, t, :], pE[:, t, :], mv2[:, t, 0:1], rstd2[:, t:t + 1],
                                                    ALU.subtract, ALU.mult).then_inc(ln_dve.sem, 1)

                def z_high(it):
                    dve.wait_ge(z_act.sem, z_act.at(it.g))
                    dve.wait_ge(out_pe.sem, out_pe.at(it.g - 2))
                    v.tensor_copy(z[0][it.s][:], zf[:]).then_inc(z_dve.sem, 1)

                def add_out(it):
                    dve.wait_ge(out_pe.sem, out_pe.at(it.g))
                    dve.wait_ge(r_loaded[it.s], 16 * it.q + 16)
                    if it.again:
                        dve.wait_ge(out_stored[it.s], 16 * it.q)
                    v.tensor_tensor(res_out[it.s][:], pG[:], res_in[it.s][:], ALU.add).then_inc(out_dve.sem, 1)

                for stage in (norm, low, proj_dve, ph_dve, mem_dve, ln_dve, z_dve, out_dve):
                    stage.open(dve)
                pipelined(dve, 8, ITEMS, 4, (1, x_low), (5, normalise_ret), (6, z_high), (0, normalise), (5, center_ret),
                          (3, phase), (7, add_out), (0, center), (1, project), (4, memory))

            @block.gpsimd
            def _(pool):
                p = nc.gpsimd

                def rstd_x(it):
                    pool.wait_ge(norm.sem, norm.at(it.g, 5))
                    p.tensor_tensor(rstd[:], var[:], env.neg_half[:, 0:2], ALU.pow).then_inc(norm_pool.sem, 1)

                def residual(it):
                    pool.wait_ge(norm_pool.sem, norm_pool.at(it.g - 1))
                    for t in range(2):
                        i = p.tensor_tensor(res_t[:, t, :], x_in[it.s][:, t, :], env.bo_rows[:], ALU.add)
                    i.then_inc(norm_pool.sem, 1)
                    pool.wait_ge(norm_pool.sem, norm_pool.at(it.g, 2))
                    pool.wait_ge(norm.sem, norm.at(it.g, 7))
                    if it.again:
                        pool.wait_ge(res_stored[it.s], 16 * it.q)
                    p.tensor_tensor(res[it.s][:], res_t[:], xn[it.s][:], ALU.add).then_inc(norm_pool.sem, 1)

                def scale(it):
                    pool.wait_ge(tanhs.sem, tanhs.at(it.g))
                    p.tensor_tensor(ph[it.s][:], ph[it.s][:], env.scale4[:].unsqueeze(2).to_broadcast([P, 4, G]), ALU.mult).then_inc(scaled.sem, 1)

                def bind(it):
                    pool.wait_ge(sines.sem, sines.at(it.g))
                    pool.wait_ge(mem_dve.sem, mem_dve.at(it.g - 1))
                    p.tensor_tensor(bound[:, 0:2, :], val[it.lane][:], cos[it.s][:, 0:2, :], ALU.mult).then_inc(bound_p.sem, 1)
                    p.tensor_tensor(bound[:, 2:4, :], val[it.lane][:], sin[it.s][:, 0:2, :], ALU.mult).then_inc(bound_p.sem, 1)

                def rstd_ret(it):
                    pool.wait_ge(ln_dve.sem, ln_dve.at(it.g, 5))
                    p.tensor_tensor(rstd2[:], var2[:], env.neg_half[:, 0:2], ALU.pow).then_inc(ln_pool.sem, 1)

                def z_low(it):
                    pool.wait_ge(z_dve.sem, z_dve.at(it.g))
                    p.tensor_tensor(z[1][it.s][:], zf[:], z[0][it.s][:].bitcast(F32), ALU.subtract).then_inc(z_pool.sem, 1)

                for stage in (norm_pool, scaled, bound_p, ln_pool, z_pool):
                    stage.open(pool)
                pipelined(pool, 8, ITEMS, 4, (3, scale), (5, rstd_ret), (0, rstd_x), (4, bind), (0, residual), (6, z_low))

            @block.scalar
            def _(act):
                a = nc.scalar

                def x_high(it):
                    act.wait_ge(turned.sem, turned.at(it.g))
                    act.wait_ge(projected.sem, projected.at(it.g - 2))
                    a.activation(xt[0][it.s][:], pT[:], ACT.Copy).then_inc(high.sem, 1)

                def project(it):
                    for n, (bank, bias) in enumerate(((pK, BK), (pQ, BQ))):
                        act.wait_ge(projected.sem, projected.at(it.g, n + 1))
                        act.wait_ge(phased.sem, phased.at(it.g - 2))
                        for c in range(KD):
                            i = a.activation(kq[0][it.s][:, 2 * n + c, :], bank[:, c, :], ACT.Identity, bias=env.cols[:, bias, c:c + 1])
                        i.then_inc(proj_act.sem, 1)

                def value(it):
                    act.wait_ge(projected.sem, projected.at(it.g, 4))
                    act.wait_ge(bound_p.sem, bound_p.at(it.g - 4))
                    for c in range(KD):
                        i = a.activation(val[it.lane][:, c, :], pK[:, c, :], ACT.Identity, bias=env.cols[:, BV, c:c + 1],
                                         scale=1.0 / math.sqrt(D))
                    i.then_inc(proj_act.sem, 1)

                def tanh(it):
                    for n, bias in enumerate((BKP, BQP)):
                        act.wait_ge(phased.sem, phased.at(it.g, n + 1))
                        act.wait_ge(ph_dve.sem, ph_dve.at(it.g - 2))
                        for c in range(KD):
                            i = a.activation(ph[it.s][:, 2 * n + c, :], pC[:, c, :], ACT.Tanh, bias=env.cols[:, bias, c:c + 1])
                        i.then_inc(tanhs.sem, 1)

                def sine(it):
                    act.wait_ge(ph_dve.sem, ph_dve.at(it.g))
                    act.wait_ge(mem_dve.sem, mem_dve.at(it.g - 2))
                    act.wait_ge(bound_p.sem, bound_p.at(it.g - 2))
                    a.activation(apart[:], ang[:], ACT.Abs).then_inc(sines.sem, 1)
                    a.activation(sin[it.s][:], ang[:], ACT.Sin).then_inc(sines.sem, 1)
                    act.wait_ge(sines.sem, sines.at(it.g, 1))
                    a.activation(cos[it.s][:], apart[:], ACT.Sin, bias=env.half_pi[:, 0:1], scale=-1.0).then_inc(sines.sem, 1)

                def affine(it):
                    act.wait_ge(z_turned.sem, z_turned.at(it.g))
                    act.wait_ge(z_pool.sem, z_pool.at(it.g - 1))
                    for c in range(KD):
                        i = a.activation(zf[:, c, :], pF[:, c, :], ACT.Identity, bias=env.cols[:, LNB, c:c + 1], scale=env.cols[:, LNG, c:c + 1])
                    i.then_inc(z_act.sem, 1)

                for stage in (high, proj_act, tanhs, sines, z_act):
                    stage.open(act)
                pipelined(act, 8, ITEMS, 4, (1, x_high), (6, affine), (2, value), (2, tanh), (1, project), (3, sine))

            @block.tensor
            def _(pe):
                t_ = nc.tensor

                def product(out, weights, w_cols, acts, a_slot, a_rows):
                    n = 0
                    for k in range(KD):
                        for i, j in PARTS:
                            last = t_.matmul(out, weights[i][:, w_cols[0], k, w_cols[1]], acts[j][a_slot][:, a_rows + k, :],
                                             start=(n == 0), stop=(n == 3 * KD - 1))
                            n += 1
                    return last

                def turn_x(it):
                    pe.wait_ge(norm.sem, norm.at(it.g, 7))
                    pe.wait_ge(low.sem, low.at(it.g - 1))
                    for t in range(2):
                        for k in range(KD):
                            i = t_.transpose(pT[:, k, t * P:(t + 1) * P], xn[it.s][:, t, k * P:(k + 1) * P], env.ident[:])
                    i.then_inc(turned.sem, 1)

                def project(it):
                    pe.wait_ge(high.sem, high.at(it.g))
                    pe.wait_ge(low.sem, low.at(it.g))
                    pe.wait_ge(proj_act.sem, proj_act.at(it.g - 1))
                    for c in range(KD):
                        i = product(pK[:, c, :], env.w, (WK, slice(c * P, (c + 1) * P)), xt, it.s, 0)
                    i.then_inc(projected.sem, 1)
                    pe.wait_ge(proj_dve.sem, proj_dve.at(it.g - 1, 2))
                    for c in range(KD):
                        i = product(pQ[:, c, :], env.w, (WQ, slice(c * P, (c + 1) * P)), xt, it.s, 0)
                    i.then_inc(projected.sem, 1)
                    pe.wait_ge(proj_dve.sem, proj_dve.at(it.g - 1))
                    for t in range(2):
                        n = 0
                        for k in range(KD):
                            for a, b in PARTS:
                                i = t_.matmul(pL[:, t, :], xt[a][it.s][:, k, t * P:(t + 1) * P], env.rw[b][:, k, :],
                                              start=(n == 0), stop=(n == 3 * KD - 1))
                                n += 1
                    i.then_inc(projected.sem, 1)

                def values(it):
                    pe.wait_ge(proj_act.sem, proj_act.at(it.g, 1))
                    pe.wait_ge(proj_dve.sem, proj_dve.at(it.g, 1))
                    for c in range(KD):
                        i = product(pK[:, c, :], env.w, (WV, slice(c * P, (c + 1) * P)), xt, it.s, 0)
                    i.then_inc(projected.sem, 1)

                def phase(it, n):
                    pe.wait_ge(proj_act.sem, proj_act.at(it.g, n + 1))
                    pe.wait_ge(proj_dve.sem, proj_dve.at(it.g, n + 1))
                    pe.wait_ge(tanhs.sem, tanhs.at(it.g, n))
                    for c in range(KD):
                        i = product(pC[:, c, :], env.w, ((WKP, WQP)[n], slice(c * P, (c + 1) * P)), kq, it.s, 2 * n)
                    i.then_inc(phased.sem, 1)

                def phase_keys(it):
                    phase(it, 0)

                def phase_queries(it):
                    phase(it, 1)

                def turn_ret(it):
                    pe.wait_ge(mem_dve.sem, mem_dve.at(it.g))
                    pe.wait_ge(ln_dve.sem, ln_dve.at(it.g - 1))
                    for t in range(2):
                        for k in range(KD):
                            i = t_.transpose(pE[:, t, k * P:(k + 1) * P], ret[it.s][:, k, t * P:(t + 1) * P], env.ident[:])
                    i.then_inc(back.sem, 1)

                def turn_z(it):
                    pe.wait_ge(ln_dve.sem, ln_dve.at(it.g))
                    pe.wait_ge(z_act.sem, z_act.at(it.g - 1))
                    for t in range(2):
                        for k in range(KD):
                            i = t_.transpose(pF[:, k, t * P:(t + 1) * P], zt[it.s][:, t, k * P:(k + 1) * P], env.ident[:])
                    i.then_inc(z_turned.sem, 1)

                def project_out(it):
                    pe.wait_ge(z_dve.sem, z_dve.at(it.g))
                    pe.wait_ge(z_pool.sem, z_pool.at(it.g))
                    pe.wait_ge(out_dve.sem, out_dve.at(it.g - 1))
                    for t in range(2):
                        n = 0
                        for k in range(KD):
                            for a, b in PARTS:
                                i = t_.matmul(pG[:, t, :], z[a][it.s][:, k, t * P:(t + 1) * P], env.w[b][:, WO, k, :],
                                              start=(n == 0), stop=(n == 3 * KD - 1))
                                n += 1
                    i.then_inc(out_pe.sem, 1)

                for stage in (turned, projected, phased, back, z_turned, out_pe):
                    stage.open(pe)
                pipelined(pe, 8, ITEMS, 4, (6, turn_z), (5, turn_ret), (7, project_out), (2, phase_keys), (2, phase_queries),
                          (1, project), (1, values), (0, turn_x))


P = 128
BF16 = mybir.dt.bfloat16


def route(nc, env, name, logits, experts, choices, segments, cap, expert_rows, trash, picks):
    NT = logits.shape[1]
    per_seg = NT // segments
    W = NT * experts
    NB = (W + 511) // 512
    with ExitStack() as ctx:
        sb = lambda n, s, d=F32: ctx.enter_context(nc.sbuf_tensor(f"{name}_{n}", s, d))
        ps = lambda n, s, d=F32: ctx.enter_context(nc.psum_tensor(f"{name}_{n}", s, d))
        best = sb("best", [P, NT, 8]); which = sb("which", [P, NT, 8], U32); which_f = sb("which_f", [P, NT, 8])
        number = sb("number", [P, experts]); own = sb("own", [P, choices, NT])
        upper = sb("upper", [P, P], BF16); ones = sb("ones", [P, P], BF16)
        chosen = [sb(f"chosen{k}", [P, NT, experts], BF16) for k in range(choices)]
        upto_t = sb("upto_t", [P, choices, experts, NT])
        reset = sb("reset", [P, experts, NT])
        before = sb("before", [P, NT, experts])
        place = sb("place", [P, NT, experts])
        pos = sb("pos", [P, NT]); row = sb("row", [P, NT]); over = sb("over", [P, NT]); tmp = sb("tmp", [P, NT])
        seg_base = sb("seg_base", [P, NT])
        rel = sb("rel", [P, NT, experts]); total = sb("total", [P, NT])
        run = ps("run", [P, W]); tot = ps("tot", [P, W])
        made = env.sem(f"{name}_consts"); steps = env.sem(f"{name}_dve"); counted = env.sem(f"{name}_counted")
        weighed = env.sem(f"{name}_exp")
        bc = lambda ap, shape: ap.to_broadcast(shape)
        count = {}

        with nc.Block() as block:
            @block.gpsimd
            def _(pool):
                p = nc.gpsimd
                p.iota(number[:], [[1, experts]], base=0, channel_multiplier=0,
                       allow_small_or_imprecise_dtypes=True).then_inc(made, 1)
                for k in range(choices):
                    p.iota(own[:, k, :], [[P, NT]], base=trash + k * NT * P, channel_multiplier=1,
                           allow_small_or_imprecise_dtypes=True).then_inc(made, 1)
                p.memset(upper[:], 1.0).then_inc(made, 1)
                p.memset(ones[:], 1.0).then_inc(made, 1)
                for b in range(segments):
                    p.memset(seg_base[:, b * per_seg:(b + 1) * per_seg], float(b * cap)).then_inc(made, 1)
                pool.wait_ge(made, 3 + choices + segments)
                p.affine_select(out=upper[:], in_=upper[:], compare_op=ALU.is_ge, fill=0.0, base=0,
                                pattern=[[1, P]], channel_multiplier=-1).then_inc(made, 1)

            @block.vector
            def _(dve):
                v = nc.vector
                n = [0]

                def done(i):
                    n[0] += 1
                    i.then_inc(steps, 1)

                def settle():
                    dve.wait_ge(steps, n[0])

                done(v.memset(reset[:], 1.0))
                settle()
                done(v.memset(reset[:].rearrange("p e (b t) -> p e b t", b=segments)[:, :, :, 0:1], 0.0))
                for t in range(NT):
                    done(v.max(best[:, t, :], logits[:, t, :]))
                settle()
                for t in range(NT):
                    done(v.max_index(which[:, t, :], best[:, t, :], logits[:, t, :]))
                settle()
                done(v.tensor_copy(which_f[:], which[:]))
                if choices == 2:
                    done(v.tensor_tensor(tmp[:], best[:, :, 1], best[:, :, 0], ALU.subtract))
                    settle()
                else:
                    done(v.tensor_tensor(rel[:], logits[:], bc(best[:, :, 0:1], [P, NT, experts]), ALU.subtract))
                    settle()
                count["weigh"] = n[0]
                dve.wait_ge(made, 4 + choices + segments)
                for k in range(choices):
                    done(v.tensor_tensor(chosen[k][:], bc(which_f[:, :, k:k + 1], [P, NT, experts]),
                                         bc(number[:].unsqueeze(1), [P, NT, experts]), ALU.is_equal))
                    count[k] = n[0]
                for k in range(choices):
                    dve.wait_ge(counted, k + 1)
                    per_tile = tot[:].rearrange("p (t e) -> p e t", e=experts)
                    for e in range(experts):
                        done(v.tensor_tensor_scan(upto_t[:, k, e, :], reset[:, e, :], per_tile[:, e, :], 0.0, ALU.mult, ALU.add))
                    settle()
                    done(v.tensor_tensor(before[:].rearrange("p t e -> p e t"), upto_t[:, k], per_tile, ALU.subtract))
                    settle()
                    if k:
                        ends = upto_t[:, 0].rearrange("p e (b t) -> p e b t", b=segments)[:, :, :, per_seg - 1:per_seg]
                        b4 = before[:].rearrange("p (b t) e -> p e b t", b=segments)
                        for b in range(segments):
                            done(v.tensor_tensor(b4[:, :, b, :], b4[:, :, b, :], ends[:, :, b, :].to_broadcast([P, experts, per_seg]), ALU.add))
                        settle()
                    flat = before[:].rearrange("p t e -> p (t e)")
                    done(v.tensor_tensor(place[:].rearrange("p t e -> p (t e)"), run[:], flat, ALU.add))
                    settle()
                    done(v.tensor_tensor(place[:], place[:], chosen[k][:], ALU.mult))
                    settle()
                    done(v.tensor_reduce(pos[:], place[:], axis=AX, op=ALU.add))
                    count["run%d" % k] = n[0]
                    settle()
                    done(v.tensor_scalar(over[:], pos[:], cap + 0.5, None, ALU.is_gt))
                    done(v.tensor_scalar(pos[:], pos[:], -1.0, cap - 1.0, ALU.add, ALU.min))
                    done(v.tensor_scalar(row[:], which_f[:, :, k], float(expert_rows), None, ALU.mult))
                    settle()
                    done(v.tensor_tensor(row[:], row[:], seg_base[:], ALU.add))
                    settle()
                    done(v.tensor_tensor(row[:], row[:], pos[:], ALU.add))
                    settle()
                    done(v.tensor_copy(picks[k].read[:], row[:]))
                    done(v.tensor_tensor(tmp[:] if choices == 1 else total[:], own[:, k, :], row[:], ALU.subtract))
                    settle()
                    t_ = tmp if choices == 1 else total
                    done(v.tensor_tensor(t_[:], t_[:], over[:], ALU.mult))
                    settle()
                    done(v.tensor_tensor(row[:], row[:], t_[:], ALU.add))
                    settle()
                    done(v.tensor_copy(picks[k].write[:], row[:]))
                    settle()
                dve.wait_ge(weighed, 1)
                if choices == 2:
                    done(v.tensor_scalar(total[:], tmp[:], 1.0, None, ALU.add))
                    settle()
                    done(v.reciprocal(picks[0].weight[:], total[:]))
                    settle()
                    done(v.tensor_tensor(picks[1].weight[:], picks[0].weight[:], tmp[:], ALU.mult))
                else:
                    done(v.tensor_reduce(total[:], rel[:], axis=AX, op=ALU.add))
                    done(v.tensor_scalar(over[:], over[:], -1.0, 1.0, ALU.mult, ALU.add))
                    settle()
                    done(v.reciprocal(total[:], total[:]))
                    settle()
                    done(v.tensor_tensor(picks[0].weight[:], total[:], over[:], ALU.mult))
                settle()

            @block.scalar
            def _(act):
                act.wait_ge(steps, count["weigh"])
                if choices == 2:
                    nc.scalar.activation(tmp[:], tmp[:], ACT.Exp).then_inc(weighed, 1)
                else:
                    nc.scalar.activation(rel[:], rel[:], ACT.Exp).then_inc(weighed, 1)

            @block.tensor
            def _(pe):
                pe.wait_ge(made, 4 + choices + segments)
                for k in range(choices):
                    pe.wait_ge(steps, count[k])
                    if k:
                        pe.wait_ge(steps, count["run%d" % (k - 1)])
                    flat = chosen[k][:].rearrange("p t e -> p (t e)")
                    for b in range(NB):
                        c = slice(b * 512, min(W, (b + 1) * 512))
                        nc.tensor.matmul(run[:, c], upper[:], flat[:, c], start=True, stop=True)
                        i = nc.tensor.matmul(tot[:, c], ones[:], flat[:, c], start=True, stop=True)
                    i.then_inc(counted, 1)


class Pick:

    def __init__(self, keep, name, NT):
        self.write = keep(f"{name}_write", [P, NT], U32)
        self.read = keep(f"{name}_read", [P, NT], U32)
        self.weight = keep(f"{name}_weight", [P, NT])


class Scatter:

    def __init__(self, nc, env, ctx, name, src, buf, picks, NT):
        self.SL = 8 // len(picks)
        sb = lambda n, s, d=F32: ctx.enter_context(nc.sbuf_tensor(f"{name}_{n}", s, d))
        self.nc, self.src, self.buf, self.picks, self.NT, self.K = nc, src, buf, picks, NT, len(picks)
        self.rows = [sb(f"rows{i}", [P, src.shape[1]]) for i in range(self.SL)]
        self.at = [sb(f"at{h}", [P, self.K, self.SL], U32) for h in range(2)]
        self.loaded = [env.sem(f"{name}_loaded{i}") for i in range(self.SL)]
        self.sent = [env.sem(f"{name}_sent{i}") for i in range(self.SL)]
        self.indexed = env.sem(f"{name}_indexed")

    def load(self, sp):
        for i in range(self.SL):
            sp.dma_start(self.rows[i][:], self.src[i * P:(i + 1) * P, :]).then_inc(self.loaded[i], 16)
        with sp.Fori(1, self.NT // self.SL) as r:
            for i in range(self.SL):
                row = sp.snap((r * self.SL + i) * P)
                sp.wait_ge(self.sent[i], r * (16 * self.K))
                Carrier.carry(sp)
                sp.dma_start(self.rows[i][:], self.src[bass.ds(row, P), :]).then_inc(self.loaded[i], 16)

    def send_round(self, pool, r):
        for h in range(2):
            if not isinstance(r, int):
                for i in range(self.SL):
                    pool.wait_ge(self.sent[i], r * (32 * self.K) + (h - 1) * (16 * self.K))
                    Carrier.carry(pool)
            for k in range(self.K):
                self.nc.gpsimd.tensor_copy(self.at[h][:, k, :], self.picks[k].write[:, bass.ds((r * 2 + h) * self.SL, self.SL)]).then_inc(self.indexed, 1)
            pool.wait_ge(self.indexed, r * (2 * self.K) + (h + 1) * self.K)
            Carrier.carry(pool)
            for i in range(self.SL):
                pool.wait_ge(self.loaded[i], r * 32 + (16 * h + 16))
                Carrier.carry(pool)
                for k in range(self.K):
                    pool.indirect_dma_start(self.buf[:, :], bass.IndirectOffsetOnAxis(ap=self.at[h][:, k, i:i + 1], axis=0),
                                            self.rows[i][:], None).then_inc(self.sent[i], 16)

    def send(self, pool):
        self.send_round(pool, 0)
        with pool.Fori(1, self.NT // (2 * self.SL)) as r:
            self.send_round(pool, r)

    def finish(self, eng):
        for i in range(self.SL):
            eng.wait_ge(self.sent[i], 16 * self.K * (self.NT // self.SL))


T, P, D, KD = 8192, 128, 256, 2
PARTS = ((0, 0), (0, 1), (1, 0))
E0, H0 = 8, 1024
HC = H0 // P
CAP0 = 614
PER = 5
SUB = 4
GP = -(-4 * CAP0 // (PER * SUB))
GR = SUB * GP
ROWS0 = PER * GR


def experts_l0(nc, env, tokens, buf, out_buf, w_fc, w_gate, w_proj, bias_cols, bias_rows):
    with ExitStack() as ctx:
        scatter = Scatter(nc, env, ctx, "s0", tokens[0], buf, tokens[1], T // P)
        sb = lambda n, s, d=F32: ctx.enter_context(nc.sbuf_tensor("m0_" + n, s, d))
        ps = lambda n, s, d=F32: ctx.enter_context(nc.psum_tensor("m0_" + n, s, d))
        sem = lambda n: env.sem("m0_" + n)
        two = lambda n, s, d=F32: [sb(f"{n}{i}", s, d) for i in range(2)]
        cols = sb("cols", [P, 2, E0, HC]); rows_b = sb("rows", [P, E0, D])
        gate_bias = two("gate_bias", [P, HC]); bias_set = sem("bias_set")
        raw = sb("raw", [P, KD * H0])
        wt = [two("w_hi", [P, 3, KD * H0], F32R), two("w_lo", [P, 3, KD * H0], F32R)]
        x_in = two("x_in", [P, SUB, D])
        xt = [two("xt_hi", [P, KD, GR], F32R), two("xt_lo", [P, KD, GR], F32R)]
        gate = two("gate", [P, GR]); prod = two("prod", [P, GR]); act_f = two("act", [P, GR])
        ht = [sb("ht_hi", [P, HC, GR], F32R), sb("ht_lo", [P, HC, GR], F32R)]
        out = two("out", [P, SUB, D])
        pA = [ps(f"pA{i}", [P, GR]) for i in range(2)]
        pH = [ps(f"pH{i}", [P, GR]) for i in range(2)]; pG = [ps(f"pG{i}", [P, GR]) for i in range(2)]
        pO = [ps(f"pO{i}", [P, 2, D]) for i in range(2)]
        fc = lambda part, u, k, hc: wt[part][u][:, 0, :].rearrange("p (k h) -> p k h", k=KD)[:, k, hc * P:(hc + 1) * P]
        gt = lambda part, u, k, hc: wt[part][u][:, 1, :].rearrange("p (k h) -> p k h", k=KD)[:, k, hc * P:(hc + 1) * P]
        pj = lambda part, u, hc: wt[part][u][:, 2, :].rearrange("p (c d) -> p c d", c=HC)[:, hc, :]

        consts = sem("consts"); w_loaded = sem("w_loaded")
        first_loaded, first_split = sem("first_loaded"), sem("first_split")
        w_high, w_low = sem("w_high"), sem("w_low")
        x_loaded = [sem(f"x_loaded{i}") for i in range(2)]; out_stored = [sem(f"out_stored{i}") for i in range(2)]
        turned = Steps(sem("turned"), 2); x_high = Steps(sem("x_high"), 2); x_low = Steps(sem("x_low"), 2)
        up = Steps(sem("up"), 2 * HC)
        gated = Steps(sem("gated"), HC); glu = Steps(sem("glu"), HC); silu = Steps(sem("silu"), HC)
        h_high = Steps(sem("h_high"), HC); h_low = Steps(sem("h_low"), HC)
        down = Steps(sem("down"), 2); added = Steps(sem("added"), 2); freed = Steps(sem("freed"), 1)

        ITEMS, UN = E0 * PER, 2 * PER

        def expert(eng, it):
            e = it.turn * 2 + it.lane // PER
            return (e if isinstance(e, int) else eng.snap(e)), it.lane // PER, it.lane % PER

        def weight(e, n):
            return (w_fc, w_gate, w_proj)[n][bass.ds(e, 1)].rearrange("o (k p) h -> p (o k) h", p=P)

        def raw_as(n):
            return raw[:].rearrange("p (k h) -> p k h", h=(H0, H0, D)[n])

        with nc.Block() as block:
            @block.sync
            def _(sp):
                sp.dma_start(cols[:], bias_cols.rearrange("p (w e c) -> p w e c", w=2, e=E0)).then_inc(consts, 16)
                sp.dma_start(rows_b[:], bias_rows.rearrange("p (e d) -> p e d", e=E0)).then_inc(consts, 16)

                def load_x(it):
                    row = at_row(sp, it, GR)
                    sp.wait_ge(turned.sem, turned.at(it.g - 2))
                    Carrier.carry(sp)
                    sp.dma_start(x_in[it.s][0:GP], buf[bass.ds(row, GR), :].rearrange("(p t) d -> p t d", t=SUB)).then_inc(x_loaded[it.s], 16)

                def free(it):
                    sp.wait_ge(out_stored[it.s], it.q * 16 + 16)
                    sp.sem_inc(freed.sem, 1)

                def store(it):
                    row = at_row(sp, it, GR)
                    sp.wait_ge(added.sem, added.at(it.g))
                    Carrier.carry(sp)
                    sp.dma_start(out_buf[bass.ds(row, GR), :].rearrange("(p t) d -> p t d", t=SUB), out[it.s][0:GP]).then_inc(out_stored[it.s], 16)

                def next_weights(it):
                    e, u, j = expert(sp, it)
                    if 1 <= j <= 3 and (not isinstance(e, int) or e + 1 < E0):
                        nxt = e + 1 if isinstance(e, int) else sp.snap(e + 1)
                        sp.wait_ge(w_low, it.turn * 6 + (u * 3 + 2 + j))
                        Carrier.carry(sp)
                        sp.dma_start(raw_as(j - 1), weight(nxt, j - 1)).then_inc(w_loaded, 16)

                scatter.load(sp)
                freed.open(sp)
                scatter.finish(sp)
                pipelined(sp, 5, ITEMS, UN, (0, load_x), (2, store), (3, free), (1, next_weights))
                for s in range(2):
                    sp.wait_ge(out_stored[s], 16 * E0 * PER // 2)

            @block.vector
            def _(dve):
                v = nc.vector

                def split_high(u, n, loaded, used):
                    dve.wait_ge(w_loaded, loaded)
                    dve.wait_ge(down.sem, down.at(used))
                    v.tensor_copy(wt[0][u][:, n, :], raw[:]).then_inc(w_high, 1)

                def low_x(it):
                    for k in range(KD):
                        dve.wait_ge(x_high.sem, x_high.at(it.g, k + 1))
                        if k == 0:
                            dve.wait_ge(up.sem, up.at(it.g - 2))
                        v.tensor_tensor(xt[1][it.s][:, k, :], pA[k][:], xt[0][it.s][:, k, :].bitcast(F32), ALU.subtract).then_inc(x_low.sem, 1)

                def hidden(it):
                    e, u, j = expert(dve, it)

                    def high(hc):
                        dve.wait_ge(silu.sem, silu.at(it.g, hc + 1))
                        if hc == 0:
                            dve.wait_ge(down.sem, down.at(it.g - 1))
                        v.tensor_copy(ht[0][:, hc, :], act_f[hc % 2][:]).then_inc(h_high.sem, 1)

                    for hc in range(HC):
                        dve.wait_ge(up.sem, up.at(it.g, 2 * hc + 1))
                        dve.wait_ge(gated.sem, gated.at(it.g, hc + 1))
                        dve.wait_ge(silu.sem, silu.at(it.g, hc - 1))
                        v.scalar_tensor_tensor(out=prod[hc % 2][:], in0=pH[hc % 2][:], scalar=cols[:, 0, bass.ds(e, 1), hc:hc + 1].rearrange("p o c -> p (o c)"),
                                                        in1=gate[hc % 2][:], op0=ALU.add, op1=ALU.mult).then_inc(glu.sem, 1)
                        if hc:
                            high(hc - 1)
                    high(HC - 1)

                def add_bias(it):
                    e, u, j = expert(dve, it)
                    for half in range(2):
                        dve.wait_ge(down.sem, down.at(it.g, half + 1))
                        if half == 0:
                            dve.wait_ge(freed.sem, freed.at(it.g - 2))
                        for t in range(2):
                            i = v.tensor_tensor(out[it.s][0:GP, half * 2 + t, :].unsqueeze(1), pO[half][0:GP, t:t + 1, :], rows_b[0:GP, bass.ds(e, 1), :], ALU.add)
                        i.then_inc(added.sem, 1)

                def next_weights(it):
                    e, u, j = expert(dve, it)
                    if 1 <= j <= 3 and (not isinstance(e, int) or e + 1 < E0):
                        split_high(1 - u, j - 1, it.turn * 96 + (u * 48 + 16 * j), it.g - (j + 1))

                for stage in (x_low, glu, h_high, added):
                    stage.open(dve)
                dve.wait_ge(consts, 32)
                for n in range(3):
                    dve.wait_ge(first_loaded, 16 * n + 16)
                    v.tensor_copy(wt[0][0][:, n, :], raw[:]).then_inc(w_high, 1)
                    dve.wait_ge(w_high, n + 1)
                    v.tensor_tensor(wt[1][0][:, n, :], raw[:], wt[0][0][:, n, :].bitcast(F32), ALU.subtract).then_inc(first_split, 1)
                pipelined(dve, 5, ITEMS, UN, (2, add_bias), (1, hidden), (0, low_x), (1, next_weights))

            @block.gpsimd
            def _(pool):
                p = nc.gpsimd

                def split_low(u, n, high):
                    pool.wait_ge(w_high, high)
                    p.tensor_tensor(wt[1][u][:, n, :], raw[:], wt[0][u][:, n, :].bitcast(F32), ALU.subtract).then_inc(w_low, 1)

                def hidden(it):
                    for hc in range(HC):
                        pool.wait_ge(h_high.sem, h_high.at(it.g, hc + 1))
                        p.tensor_tensor(ht[1][:, hc, :], act_f[hc % 2][:], ht[0][:, hc, :].bitcast(F32), ALU.subtract).then_inc(h_low.sem, 1)

                def next_weights(it):
                    e, u, j = expert(pool, it)
                    if 1 <= j <= 3 and (not isinstance(e, int) or e + 1 < E0):
                        split_low(1 - u, j - 1, it.turn * 6 + (u * 3 + 3 + j))

                scatter.send(pool)
                pool.wait_ge(first_split, 3)
                pool.sem_inc(w_low, 3)
                for stage in (h_low,):
                    stage.open(pool)
                pipelined(pool, 5, ITEMS, UN, (1, hidden), (1, next_weights))

            @block.scalar
            def _(act):
                a = nc.scalar

                def high_x(it):
                    for k in range(KD):
                        act.wait_ge(turned.sem, turned.at(it.g, k + 1))
                        if k == 0:
                            act.wait_ge(up.sem, up.at(it.g - 2))
                        a.activation(xt[0][it.s][:, k, :], pA[k][:], ACT.Copy).then_inc(x_high.sem, 1)

                def hidden(it):
                    e, u, j = expert(act, it)

                    def activate(hc):
                        act.wait_ge(glu.sem, glu.at(it.g, hc + 1))
                        act.wait_ge(h_high.sem, h_high.at(it.g, hc - 1))
                        act.wait_ge(h_low.sem, h_low.at(it.g, hc - 1))
                        a.activation(act_f[hc % 2][:], prod[hc % 2][:], ACT.Silu).then_inc(silu.sem, 1)

                    for hc in range(HC):
                        act.wait_ge(up.sem, up.at(it.g, 2 * hc + 2))
                        act.wait_ge(glu.sem, glu.at(it.g, hc - 1))
                        a.activation(gate[hc % 2][:], pG[hc % 2][:], ACT.Identity, bias=gate_bias[u][:, hc:hc + 1]).then_inc(gated.sem, 1)
                        if hc:
                            activate(hc - 1)
                    activate(HC - 1)

                def set_bias(it):
                    e, u, j = expert(act, it)
                    if j == 0:
                        a.activation(gate_bias[u][:].unsqueeze(1), cols[:, 1, bass.ds(e, 1), :], ACT.Copy).then_inc(bias_set, 1)
                        act.wait_ge(bias_set, e + 1)

                for n in range(3):
                    if n:
                        act.wait_ge(first_split, n)
                    act.dma_start(raw_as(n), weight(0, n)).then_inc(first_loaded, 16)
                for stage in (x_high, gated, silu):
                    stage.open(act)
                pipelined(act, 5, ITEMS, UN, (1, set_bias), (1, hidden), (0, high_x))

            @block.tensor
            def _(pe):
                t_ = nc.tensor

                def turn_x(it):
                    pe.wait_ge(x_loaded[it.s], it.q * 16 + 16)
                    for k in range(KD):
                        pe.wait_ge(x_low.sem, x_low.at(it.g - 1, k + 1))
                        for t in range(SUB):
                            i = t_.transpose(pA[k][:, t * GP:(t + 1) * GP], x_in[it.s][0:GP, t, k * P:(k + 1) * P], env.ident[0:GP, 0:GP])
                        i.then_inc(turned.sem, 1)

                def up_products(it):
                    e, u, j = expert(pe, it)
                    if j == 0:
                        pe.wait_ge(w_low, it.turn * 6 + (u * 3 + 3))
                    pe.wait_ge(x_low.sem, x_low.at(it.g))
                    for hc in range(HC):
                        pe.wait_ge(glu.sem, glu.at(it.g, hc - 1))
                        for bank, w in ((pH, fc), (pG, gt)):
                            n = 0
                            for k in range(KD):
                                for a, b in PARTS:
                                    last = t_.matmul(bank[hc % 2][:], w(a, u, k, hc), xt[b][it.s][:, k, :], start=(n == 0), stop=(n == 5))
                                    n += 1
                            last.then_inc(up.sem, 1)

                def down_products(it):
                    e, u, j = expert(pe, it)
                    for half in range(2):
                        pe.wait_ge(added.sem, added.at(it.g - 1, half + 1))
                        for t in range(2):
                            n = 0
                            sub = half * 2 + t
                            for hc in range(HC):
                                if sub == 0:
                                    pe.wait_ge(h_low.sem, h_low.at(it.g, hc + 1))
                                for a, b in PARTS:
                                    last = t_.matmul(pO[half][0:GP, t, :], ht[a][:, hc, sub * GP:(sub + 1) * GP], pj(b, u, hc),
                                                     start=(n == 0), stop=(n == 3 * HC - 1))
                                    n += 1
                        last.then_inc(down.sem, 1)

                for stage in (turned, up, down):
                    stage.open(pe)
                pipelined(pe, 5, ITEMS, UN, (2, down_products), (1, up_products), (0, turn_x))


P, D, KD = 128, 256, 2
PARTS = ((0, 0), (0, 1), (1, 0))
EPS = 1e-5


def combine_l0(nc, env, out0, picks, res0, res1, xn1, xt1, head_w, logits1, dt_raw, NT):
    NO = head_w.shape[1]
    NE = logits1.shape[2]
    SL = 4
    with ExitStack() as ctx:
        sb = lambda n, s, d=F32: ctx.enter_context(nc.sbuf_tensor("c0_" + n, s, d))
        ps = lambda n, s, d=F32: ctx.enter_context(nc.psum_tensor("c0_" + n, s, d))
        sem = lambda n: env.sem("c0_" + n)
        slots = lambda n, s, d=F32: [sb(f"{n}{i}", s, d) for i in range(SL)]
        sems = lambda n: [sem(f"{n}{i}") for i in range(SL)]
        w_raw = sb("w_raw", [P, KD, NO]); w = [sb("w_hi", [P, KD, NO], F32R), sb("w_lo", [P, KD, NO], F32R)]
        res_in = slots("res_in", [P, D])
        at = [slots(f"at{k}_", [P, 1], U32) for k in range(2)]
        got = [slots(f"got{k}_", [P, D]) for k in range(2)]
        x1 = slots("x1", [P, D]); part = slots("part", [P, D])
        stats = slots("stats", [P, 6]); mv = slots("mv", [P, 2]); var = slots("var", [P, 1]); rstd = slots("rstd", [P, 1])
        xn = slots("xn", [P, D]); res = slots("res", [P, D])
        xt = slots("xt", [P, 2, KD, P], F32R)
        pT = [ps(f"pT{i}", [P, KD, P]) for i in range(SL)]; pH = [ps(f"pH{i}", [P, NO]) for i in range(2)]
        w_loaded = sem("w_loaded"); w_split = sem("w_split")
        loaded, gathered = sems("loaded"), sems("gathered")
        xn_stored, res_stored, xt_stored = sems("xn_stored"), sems("res_stored"), sems("xt_stored")
        indexed = Steps(sem("indexed"), 2)
        first, summed = Steps(sem("first"), 1), Steps(sem("summed"), 1)
        norm = Steps(sem("norm"), 3)
        center_s = Steps(sem("center"), 1)
        root, both = Steps(sem("root"), 1), Steps(sem("both"), 1)
        turned = Steps(sem("turned"), 1); high = Steps(sem("high"), 1); low = Steps(sem("low"), 1)
        heads = Steps(sem("heads"), 1); kept = Steps(sem("kept"), 1)
        with nc.Block() as block:
            @block.sync
            def _(sp):
                sp.dma_start(w_raw[:], head_w.rearrange("(k p) e -> p k e", p=P)).then_inc(w_loaded, 16)

                def load(it):
                    row = at_row(sp, it, P)
                    sp.wait_ge(first.sem, first.at(it.g - SL))
                    Carrier.carry(sp)
                    sp.dma_start(res_in[it.lane][:], res0[bass.ds(row, P), :]).then_inc(loaded[it.lane], 16)

                def store(it):
                    row = at_row(sp, it, P)
                    sp.wait_ge(center_s.sem, center_s.at(it.g))
                    Carrier.carry(sp)
                    sp.dma_start(xn1[bass.ds(row, P), :], xn[it.lane][:]).then_inc(xn_stored[it.lane], 16)

                def store_sum(it):
                    row = at_row(sp, it, P)
                    sp.wait_ge(both.sem, both.at(it.g))
                    Carrier.carry(sp)
                    sp.dma_start(res1[bass.ds(row, P), :], res[it.lane][:]).then_inc(res_stored[it.lane], 16)

                def store_turned(it):
                    row = at_row(sp, it, P)
                    sp.wait_ge(high.sem, high.at(it.g))
                    Carrier.carry(sp)
                    sp.wait_ge(low.sem, low.at(it.g))
                    Carrier.carry(sp)
                    sp.dma_start(xt1[bass.ds(row, P)], xt[it.lane][:].bitcast(F32)).then_inc(xt_stored[it.lane], 16)

                pipelined(sp, 8, NT, SL, (0, load), (5, store), (5, store_sum), (6, store_turned))
                for s in range(SL):
                    for q in (xn_stored, res_stored, xt_stored):
                        sp.wait_ge(q[s], 16 * NT // SL)

            @block.gpsimd
            def _(pool):
                p = nc.gpsimd

                def index(it):
                    if it.again_lane:
                        pool.wait_ge(gathered[it.lane], it.turn * 32)
                        Carrier.carry(pool)
                    for k in range(2):
                        p.tensor_copy(at[k][it.lane][:], picks[k].read[:, bass.ds(it.g, 1)]).then_inc(indexed.sem, 1)

                def gather(it):
                    pool.wait_ge(indexed.sem, indexed.at(it.g))
                    Carrier.carry(pool)
                    pool.wait_ge(summed.sem, summed.at(it.g - SL))
                    Carrier.carry(pool)
                    for k in range(2):
                        pool.indirect_dma_start(got[k][it.lane][:], None, out0[:, :],
                                                bass.IndirectOffsetOnAxis(ap=at[k][it.lane][:, 0:1], axis=0)).then_inc(gathered[it.lane], 16)

                def rstd_x(it):
                    pool.wait_ge(norm.sem, norm.at(it.g))
                    pool.wait_ge(center_s.sem, center_s.at(it.g - SL))
                    p.tensor_tensor(rstd[it.lane][:], var[it.lane][:], env.neg_half[:, 0:1], ALU.pow).then_inc(root.sem, 1)

                for stage in (indexed, root):
                    stage.open(pool)
                pipelined(pool, 8, NT, SL, (0, index), (1, gather), (3, rstd_x))

            @block.vector
            def _(dve):
                v = nc.vector
                dve.wait_ge(w_loaded, 16)
                v.tensor_copy(w[0][:], w_raw[:]).then_inc(w_split, 1)
                dve.wait_ge(w_split, 1)
                v.tensor_tensor(w[1][:], w_raw[:], w[0][:].bitcast(F32), ALU.subtract).then_inc(w_split, 1)

                def weight(it, k):
                    return picks[k].weight[:, bass.ds(it.g, 1)]

                def add_first(it):
                    dve.wait_ge(loaded[it.lane], it.turn * 16 + 16)
                    dve.wait_ge(gathered[it.lane], it.turn * 32 + 32)
                    dve.wait_ge(summed.sem, summed.at(it.g - SL))
                    v.scalar_tensor_tensor(out=part[it.lane][:], in0=got[0][it.lane][:], scalar=weight(it, 0), in1=res_in[it.lane][:],
                                           op0=ALU.mult, op1=ALU.add).then_inc(first.sem, 1)

                def add_second(it):
                    dve.wait_ge(first.sem, first.at(it.g))
                    dve.wait_ge(both.sem, both.at(it.g - SL))
                    v.scalar_tensor_tensor(out=x1[it.lane][:], in0=got[1][it.lane][:], scalar=weight(it, 1), in1=part[it.lane][:],
                                           op0=ALU.mult, op1=ALU.add).then_inc(summed.sem, 1)

                def measure(it):
                    dve.wait_ge(summed.sem, summed.at(it.g))
                    v.bn_stats(stats[it.lane][:], x1[it.lane][:]).then_inc(norm.sem, 1)

                def aggregate(it):
                    dve.wait_ge(norm.sem, norm.at(it.g, 1))
                    dve.wait_ge(center_s.sem, center_s.at(it.g - SL))
                    Carrier.carry(dve)
                    v.bn_aggr(mv[it.lane][:], stats[it.lane][:]).then_inc(norm.sem, 1)
                    dve.wait_ge(norm.sem, norm.at(it.g, 2))
                    dve.wait_ge(root.sem, root.at(it.g - SL))
                    v.tensor_scalar(var[it.lane][:], mv[it.lane][:, 1:2], EPS, None, ALU.add).then_inc(norm.sem, 1)

                def center(it):
                    dve.wait_ge(root.sem, root.at(it.g))
                    dve.wait_ge(turned.sem, turned.at(it.g - SL))
                    dve.wait_ge(both.sem, both.at(it.g - SL))
                    if it.again_lane:
                        dve.wait_ge(xn_stored[it.lane], it.turn * 16)
                    v.tensor_scalar(xn[it.lane][:], x1[it.lane][:], mv[it.lane][:, 0:1], rstd[it.lane][:], ALU.subtract, ALU.mult).then_inc(center_s.sem, 1)

                def add_both(it):
                    dve.wait_ge(center_s.sem, center_s.at(it.g))
                    if it.again_lane:
                        dve.wait_ge(res_stored[it.lane], it.turn * 16)
                    v.tensor_tensor(res[it.lane][:], x1[it.lane][:], xn[it.lane][:], ALU.add).then_inc(both.sem, 1)

                def low_part(it):
                    dve.wait_ge(high.sem, high.at(it.g))
                    dve.wait_ge(heads.sem, heads.at(it.g - SL))
                    if it.again_lane:
                        dve.wait_ge(xt_stored[it.lane], it.turn * 16)
                    v.tensor_tensor(xt[it.lane][:, 1], pT[it.lane][:], xt[it.lane][:, 0].bitcast(F32), ALU.subtract).then_inc(low.sem, 1)

                def keep(it):
                    dve.wait_ge(heads.sem, heads.at(it.g))
                    v.tensor_copy(logits1[:, bass.ds(it.g, 1), :], pH[it.s][:, 0:NE].unsqueeze(1))
                    v.tensor_copy(dt_raw[:, bass.ds(it.g, 1), :], pH[it.s][:, NE:NO].unsqueeze(1)).then_inc(kept.sem, 1)

                for stage in (first, summed, norm, center_s, both, low, kept):
                    stage.open(dve)
                pipelined(dve, 8, NT, SL, (2, add_first), (4, center), (5, add_both), (2, add_second), (6, low_part), (2, measure), (7, keep), (2, aggregate))

            @block.scalar
            def _(act):
                def high_part(it):
                    act.wait_ge(turned.sem, turned.at(it.g))
                    act.wait_ge(heads.sem, heads.at(it.g - SL))
                    if it.again_lane:
                        act.wait_ge(xt_stored[it.lane], it.turn * 16)
                    nc.scalar.activation(xt[it.lane][:, 0], pT[it.lane][:], ACT.Copy).then_inc(high.sem, 1)

                high.open(act)
                pipelined(act, 8, NT, SL, (5, high_part))

            @block.tensor
            def _(pe):
                t_ = nc.tensor
                pe.wait_ge(w_split, 2)

                def turn(it):
                    pe.wait_ge(center_s.sem, center_s.at(it.g))
                    pe.wait_ge(low.sem, low.at(it.g - SL))
                    for k in range(KD):
                        i = t_.transpose(pT[it.lane][:, k, :], xn[it.lane][:, k * P:(k + 1) * P], env.ident[:])
                    i.then_inc(turned.sem, 1)

                def project(it):
                    pe.wait_ge(low.sem, low.at(it.g))
                    pe.wait_ge(kept.sem, kept.at(it.g - 2))
                    n = 0
                    for k in range(KD):
                        for a, b in PARTS:
                            i = t_.matmul(pH[it.s][:], xt[it.lane][:, a, k, :], w[b][:, k, :], start=(n == 0), stop=(n == 5))
                            n += 1
                    i.then_inc(heads.sem, 1)

                for stage in (turned, heads):
                    stage.open(pe)
                pipelined(pe, 8, NT, SL, (5, turn), (7, project))


T, P, D, KD = 8192, 128, 256, 2
PARTS = ((0, 0), (0, 1), (1, 0))
E1, CAP1 = 32, 320
SUBS = [(n * P, min(P, CAP1 - n * P)) for n in range((CAP1 + P - 1) // P)]


def experts_l1(nc, env, tokens, buf, out_buf, weights):
    with ExitStack() as ctx:
        scatter = Scatter(nc, env, ctx, "s1", tokens[0], buf, tokens[1], T // P)
        sb = lambda n, s, d=F32: ctx.enter_context(nc.sbuf_tensor("m1_" + n, s, d))
        ps = lambda n, s, d=F32: ctx.enter_context(nc.psum_tensor("m1_" + n, s, d))
        sem = lambda n: env.sem("m1_" + n)
        two = lambda n, s, d=F32: [sb(f"{n}{i}", s, d) for i in range(2)]
        NS = len(SUBS)
        raw = two("raw", [P, 3, KD, D])
        four = lambda n, s, d: [sb(f"{n}{i}", s, d) for i in range(4)]
        w = [four("w_hi", [P, 3, KD, D], F32R), four("w_lo", [P, 3, KD, D], F32R)]
        x_in = two("x_in", [P, NS, D])
        xt = [two("xt_hi", [P, KD, CAP1], F32R), two("xt_lo", [P, KD, CAP1], F32R)]
        gate = two("gate", [P, KD, CAP1]); h = two("h", [P, KD, CAP1])
        ht = [two("ht_hi", [P, KD, CAP1], F32R), two("ht_lo", [P, KD, CAP1], F32R)]
        out = two("out", [P, NS, D])
        pA = [ps(f"pA{k}", [P, CAP1]) for k in range(KD)]
        pG = [ps(f"pG{k}", [P, CAP1]) for k in range(KD)]; pU = [ps(f"pU{k}", [P, CAP1]) for k in range(KD)]
        pO = [ps("pO0", [P, 2, D]), ps("pO1", [P, 1, D])]
        w_loaded = [sem(f"w_loaded{i}") for i in range(2)]; x_loaded = [sem(f"x_loaded{i}") for i in range(2)]
        stored = [sem(f"stored{i}") for i in range(2)]
        w_high = Steps(sem("w_high"), 1); w_low = Steps(sem("w_low"), 1)
        turned = Steps(sem("turned"), 2); x_high = Steps(sem("x_high"), 2); x_low = Steps(sem("x_low"), 2)
        up = Steps(sem("up"), 2); silu = Steps(sem("silu"), 2); mul = Steps(sem("mul"), 2)
        h_high = Steps(sem("h_high"), 2); h_low = Steps(sem("h_low"), 2)
        down = Steps(sem("down"), 2); kept = Steps(sem("kept"), 2)
        with nc.Block() as block:
            @block.sync
            def _(sp):
                def load(it):
                    e = it.g if isinstance(it.g, int) else sp.snap(it.g)
                    row = at_row(sp, it, CAP1)
                    sp.wait_ge(w_low.sem, w_low.at(it.g - 2))
                    Carrier.carry(sp)
                    sp.dma_start(raw[it.s][:], weights[bass.ds(e, 1)].rearrange("o w (k p) f -> p (o w) k f", p=P)).then_inc(w_loaded[it.s], 16)
                    sp.wait_ge(turned.sem, turned.at(it.g - 2))
                    Carrier.carry(sp)
                    for n, (at, m) in enumerate(SUBS):
                        sp.dma_start(x_in[it.s][0:m, n, :], buf[bass.ds(row + at, m), :]).then_inc(x_loaded[it.s], 16)

                def store(it):
                    row = at_row(sp, it, CAP1)
                    sp.wait_ge(kept.sem, kept.at(it.g))
                    Carrier.carry(sp)
                    for n, (at, m) in enumerate(SUBS):
                        sp.dma_start(out_buf[bass.ds(row + at, m), :], out[it.s][0:m, n, :]).then_inc(stored[it.s], 16)

                scatter.load(sp)
                scatter.finish(sp)
                pipelined(sp, 4, E1, 4, (3, store), (0, load))
                for s in range(2):
                    sp.wait_ge(stored[s], 16 * NS * E1 // 2)

            @block.vector
            def _(dve):
                v = nc.vector

                def weights_high(it):
                    dve.wait_ge(w_loaded[it.s], it.q * 16 + 16)
                    dve.wait_ge(down.sem, down.at(it.g - 4))
                    v.tensor_copy(w[0][it.lane][:], raw[it.s][:]).then_inc(w_high.sem, 1)

                def lows(it):
                    for k in range(KD):
                        dve.wait_ge(x_high.sem, x_high.at(it.g, k + 1))
                        dve.wait_ge(up.sem, up.at(it.g - 2))
                        v.tensor_tensor(xt[1][it.s][:, k, :], pA[k][:], xt[0][it.s][:, k, :].bitcast(F32), ALU.subtract).then_inc(x_low.sem, 1)

                def hidden(it):
                    dve.wait_ge(h_low.sem, h_low.at(it.g - 2))
                    for k in range(KD):
                        dve.wait_ge(silu.sem, silu.at(it.g, k + 1))
                        v.tensor_tensor(h[it.s][:, k, :], pU[k][:], gate[it.s][:, k, :], ALU.mult).then_inc(mul.sem, 1)
                    dve.wait_ge(down.sem, down.at(it.g - 2))
                    for k in range(KD):
                        dve.wait_ge(mul.sem, mul.at(it.g, k + 1))
                        v.tensor_copy(ht[0][it.s][:, k, :], h[it.s][:, k, :]).then_inc(h_high.sem, 1)

                for stage in (w_high, x_low, mul, h_high):
                    stage.open(dve)
                pipelined(dve, 4, E1, 4, (1, weights_high), (2, hidden), (1, lows))

            @block.gpsimd
            def _(pool):
                p = nc.gpsimd

                def split(it):
                    pool.wait_ge(w_high.sem, w_high.at(it.g))
                    p.tensor_tensor(w[1][it.lane][:], raw[it.s][:], w[0][it.lane][:].bitcast(F32), ALU.subtract).then_inc(w_low.sem, 1)

                def hidden(it):
                    for k in range(KD):
                        pool.wait_ge(h_high.sem, h_high.at(it.g, k + 1))
                        p.tensor_tensor(ht[1][it.s][:, k, :], h[it.s][:, k, :], ht[0][it.s][:, k, :].bitcast(F32), ALU.subtract).then_inc(h_low.sem, 1)

                scatter.send(pool)
                for stage in (w_low, h_low):
                    stage.open(pool)
                pipelined(pool, 4, E1, 4, (1, split), (2, hidden))

            @block.scalar
            def _(act):
                a = nc.scalar

                def high_part(it):
                    for k in range(KD):
                        act.wait_ge(turned.sem, turned.at(it.g, k + 1))
                        act.wait_ge(up.sem, up.at(it.g - 2))
                        a.activation(xt[0][it.s][:, k, :], pA[k][:], ACT.Copy).then_inc(x_high.sem, 1)

                def gates(it):
                    act.wait_ge(mul.sem, mul.at(it.g - 2))
                    for k in range(KD):
                        act.wait_ge(up.sem, up.at(it.g, k + 1))
                        a.activation(gate[it.s][:, k, :], pG[k][:], ACT.Silu).then_inc(silu.sem, 1)

                def keep(it):
                    if it.again:
                        act.wait_ge(stored[it.s], it.q * (16 * NS))
                    act.wait_ge(down.sem, down.at(it.g, 1))
                    a.activation(out[it.s][:, 0:2, :], pO[0][:], ACT.Copy).then_inc(kept.sem, 1)
                    act.wait_ge(down.sem, down.at(it.g, 2))
                    m = SUBS[-1][1]
                    a.activation(out[it.s][0:m, 2, :], pO[1][0:m, 0, :], ACT.Copy).then_inc(kept.sem, 1)

                for stage in (x_high, silu, kept):
                    stage.open(act)
                pipelined(act, 4, E1, 4, (2, gates), (3, keep), (1, high_part))

            @block.tensor
            def _(pe):
                t_ = nc.tensor

                def turn(it):
                    pe.wait_ge(x_loaded[it.s], (it.q + 1) * (16 * NS))
                    for k in range(KD):
                        pe.wait_ge(x_low.sem, x_low.at(it.g - 1, k + 1))
                        for n, (at, m) in enumerate(SUBS):
                            i = t_.transpose(pA[k][:, at:at + m], x_in[it.s][0:m, n, k * P:(k + 1) * P], env.ident[0:m, 0:m])
                        i.then_inc(turned.sem, 1)

                def up_products(it):
                    pe.wait_ge(w_low.sem, w_low.at(it.g))
                    pe.wait_ge(x_low.sem, x_low.at(it.g))
                    for f in range(KD):
                        pe.wait_ge(mul.sem, mul.at(it.g - 1, f + 1))
                        for n_w, bank in ((0, pG), (1, pU)):
                            n = 0
                            for k in range(KD):
                                for i, j in PARTS:
                                    last = t_.matmul(bank[f][:], w[i][it.lane][:, n_w, k, f * P:(f + 1) * P], xt[j][it.s][:, k, :],
                                                     start=(n == 0), stop=(n == 5))
                                    n += 1
                        last.then_inc(up.sem, 1)

                def down_products(it):
                    pe.wait_ge(h_low.sem, h_low.at(it.g))
                    for s_, (at, m) in enumerate(SUBS):
                        if s_ == 0:
                            pe.wait_ge(kept.sem, kept.at(it.g - 1, 1))
                        if s_ == 2:
                            pe.wait_ge(kept.sem, kept.at(it.g - 1, 2))
                        n = 0
                        for k in range(KD):
                            for i, j in PARTS:
                                last = t_.matmul(pO[s_ // 2][0:m, s_ % 2, :], ht[i][it.s][:, k, at:at + m], w[j][it.lane][:, 2, k, :],
                                                 start=(n == 0), stop=(n == 5))
                                n += 1
                        if s_:
                            last.then_inc(down.sem, 1)

                for stage in (turned, up, down):
                    stage.open(pe)
                pipelined(pe, 4, E1, 4, (2, up_products), (3, down_products), (1, turn))


P, D, KD = 128, 256, 2
PARTS = ((0, 0), (0, 1), (1, 0))
EPS = 1e-5
DI, NS, NH, HD = 512, 64, 8, 64
CC = DI // P
CX = CC + 1
TAPS = 4
HALO = TAPS - 1
BATCH, SEQ = 4, 2048
TB = SEQ // P
NT = BATCH * TB
W = P + HALO


def mixer(nc, env, tag, backward, in_w, conv_cols, out_w, norm_cols, head_rows, dt_raw, dt_col, xt1, res_in_d, res_out_d, expert_rows=None, pick=None):
    with ExitStack() as ctx:
        sb = lambda n, s, d=F32: ctx.enter_context(nc.sbuf_tensor(f"{tag}_{n}", s, d))
        ps = lambda n, s, d=F32: ctx.enter_context(nc.psum_tensor(f"{tag}_{n}", s, d))
        sem = lambda n: env.sem(f"{tag}_{n}")
        two = lambda n, s, d=F32: [sb(f"{n}{i}", s, d) for i in range(2)]
        NO = DI + CX * P
        w_raw = sb("w_raw", [P, KD, NO]); w = [sb("w_hi", [P, KD, NO], F32R), sb("w_lo", [P, KD, NO], F32R)]
        conv = sb("conv", [P, CX, TAPS + 1]); norm_c = sb("norm_c", [P, CC])
        ow_raw = sb("ow_raw", [P, CC, D]); ow = sb("ow", [P, CC, D])
        rows = sb("rows", [P, 3, NH])
        dt = sb("dt", [P, NT, NH]); da = sb("da", [P, NT, NH])
        da_hi = sb("da_hi", [P, NT, NH], F32R); da_lo = sb("da_lo", [P, NT, NH])
        grow = sb("grow", [P, NT, NH]); fade = sb("fade", [P, NT, NH]); whole = sb("whole", [P, NT, NH])
        t1 = sb("t1", [P, NT, NH]); t2 = sb("t2", [P, NT, NH])
        upto = sb("upto", [P, P]); past = sb("past", [P, P]); past_r = sb("past_r", [P, P], F32R); ones = sb("ones", [P, P])
        state = sb("state", [NS, BATCH, DI]); faded = [sb(f"faded{i}", [NS, DI]) for i in range(2)]
        u = sb("u", [P, BATCH, CX, W])

        xt = two("xt", [P, 2, KD, P], F32R)
        gate = [sb(f"gate{i}", [P, DI]) for i in range(4)]
        cv = two("cv", [P, CX, P]); xc = two("xc", [P, CC, P]); bt = two("bt", [NS, P]); ct = two("ct", [NS, P])
        seg = [two("seg_hi", [P, NH, P], F32R), two("seg_lo", [P, NH, P], F32R)]
        decay = sb("decay", [P, NH, P]); gm = sb("gm", [P, P]); mix = two("mix", [P, NH, P])
        b_tok = two("b_tok", [P, NS]); x_tok = two("x_tok", [P, DI]); xdt = two("xdt", [P, DI])
        xw = two("xw", [P, DI]); skip = two("skip", [P, DI])
        y1 = sb("y1", [P, DI]); y2 = sb("y2", [P, DI]); y3 = sb("y3", [P, DI]); yz = two("yz", [P, DI])
        sq = sb("sq", [P, DI]); ss = two("ss", [P, 1]); ms = two("ms", [P, 1]); rstd = two("rstd", [P, 1])
        yt = two("yt", [P, CC, P])
        res = two("res", [P, D]); out = two("out", [P, D])
        at = two("at", [P, 1], U32); got = two("got", [P, D]); sum_e = two("sum_e", [P, D])

        bank = [ps(f"bank{i}", [P, 512]) for i in range(8)]
        pB0 = bank[0][:].rearrange("p (c t) -> p c t", c=CC); pB1 = bank[1][:, 0:P]
        pYT = bank[0][:].rearrange("p (c t) -> p c t", c=CC); pS = bank[1][0:NS, :]
        pZ = bank[2][:]; pI = bank[2][:]
        pX = bank[3][:]
        pBT = bank[4][:, 0:NS]; pG = bank[4][:, P:2 * P]; pO = bank[4][:, 2 * P:2 * P + D]
        pD = [bank[5][:].rearrange("p (h t) -> p h t", h=4), bank[6][:].rearrange("p (h t) -> p h t", h=4)]
        pY = bank[7][:]

        loaded, made, prep, prep_pe, prep_act = sem("loaded"), sem("made"), sem("prep"), sem("prep_pe"), sem("prep_act")
        x_loaded = [sem(f"x_loaded{i}") for i in range(2)]; r_loaded = [sem(f"r_loaded{i}") for i in range(2)]
        stored = [sem(f"stored{i}") for i in range(2)]
        proj = Steps(sem("proj"), 2)
        u_kept = Steps(sem("u_kept"), 1)
        halo = Steps(sem("halo"), 1)
        tapped = Steps(sem("tapped"), 1)
        conved = Steps(sem("conved"), TAPS - 1)
        silu_z = Steps(sem("silu_z"), 1)
        silu = Steps(sem("silu"), 3)
        seg_p = Steps(sem("seg"), 1)
        turn = Steps(sem("turn"), 3)
        tok = Steps(sem("tok"), 4)
        tok_act = Steps(sem("tok_act"), 2)
        tok_pool = Steps(sem("tok_pool"), 2)
        scan = Steps(sem("scan"), 3)
        st_pool = Steps(sem("st_pool"), 1)
        y_dve = Steps(sem("y_dve"), 4)
        added = Steps(sem("added"), 1)
        y_act = Steps(sem("y_act"), 1)
        ms_dve = Steps(sem("ms_dve"), 1); ms_pool = Steps(sem("ms_pool"), 1)
        yturn = Steps(sem("yturn"), 1); y_kept = Steps(sem("y_kept"), 1)
        gathered = [sem(f"gathered{i}") for i in range(2)]
        indexed, expert = Steps(sem("indexed"), 1), Steps(sem("expert"), 1)
        outp = Steps(sem("outp"), 1); summed = Steps(sem("summed"), 1)
        main = slice(0, P) if backward else slice(HALO, W)

        def tile(it):
            return it.turn * (-1 if backward else 1) + (it.lane * TB + (TB - 1 if backward else 0))

        def bc(ap, n):
            return ap.unsqueeze(2).to_broadcast([ap.shape[0], ap.shape[1], n])

        def heads(ap):
            return ap.rearrange("p (h d) -> p h d", h=NH)

        with nc.Block() as block:
            @block.sync
            def _(sp):
                sp.dma_start(w_raw[:], in_w.rearrange("(k p) e -> p k e", p=P)).then_inc(loaded, 16)
                sp.dma_start(conv[:], conv_cols.rearrange("p (c w) -> p c w", c=CX)).then_inc(loaded, 16)
                sp.dma_start(ow_raw[:], out_w.rearrange("(k p) e -> p k e", p=P)).then_inc(loaded, 16)
                sp.dma_start(norm_c[:], norm_cols).then_inc(loaded, 16)
                sp.dma_start(rows[:], head_rows.rearrange("p (v h) -> p v h", h=NH)).then_inc(loaded, 16)

            @block.gpsimd
            def _(pool):
                p = nc.gpsimd
                p.memset(upto[:], 1.0).then_inc(made, 1)
                p.memset(past[:], 1.0).then_inc(made, 1)
                p.memset(ones[:], 1.0).then_inc(made, 1)
                p.memset(state[:], 0.0).then_inc(made, 1)
                p.memset(u[:], 0.0).then_inc(made, 1)
                pool.wait_ge(made, 5)
                d = -1 if backward else 1
                p.affine_select(out=upto[:], in_=upto[:], compare_op=ALU.is_ge, fill=0.0, base=0,
                                pattern=[[d, P]], channel_multiplier=-d).then_inc(made, 1)
                p.affine_select(out=past[:], in_=past[:], compare_op=ALU.is_gt, fill=0.0, base=0,
                                pattern=[[-d, P]], channel_multiplier=d).then_inc(made, 1)

            @block.vector
            def _(dve):
                v = nc.vector
                n = [0]

                def done(i):
                    n[0] += 1
                    i.then_inc(prep, 1)
                    dve.wait_ge(prep, n[0])

                dve.wait_ge(loaded, 80)
                done(v.tensor_copy(w[0][:], w_raw[:]))
                done(v.tensor_tensor(w[1][:], w_raw[:], w[0][:].bitcast(F32), ALU.subtract))
                for c in range(CC):
                    done(v.tensor_scalar(ow[:, c, :], ow_raw[:, c, :], norm_c[:, c:c + 1], None, ALU.mult))
                row = lambda k: rows[:, k, :].unsqueeze(1).to_broadcast([P, NT, NH])
                done(v.tensor_tensor(t1[:], dt_raw[:, :, dt_col:dt_col + NH], row(0), ALU.add))
                assert n[0] == 7
                dve.wait_ge(prep_act, 2)
                done(v.tensor_scalar(grow[:], t2[:], 1.0, None, ALU.add))
                assert n[0] == 8
                done(v.tensor_scalar(dt[:], grow[:], -1.0, None, ALU.add))
                done(v.tensor_tensor(dt[:], dt[:], t2[:], ALU.subtract))
                done(v.reciprocal(fade[:], grow[:]))
                done(v.tensor_tensor(dt[:], dt[:], fade[:], ALU.mult))
                dve.wait_ge(prep_act, 3)
                done(v.tensor_tensor(dt[:], whole[:], dt[:], ALU.subtract))
                done(v.tensor_scalar(t1[:], t1[:], 0.0, None, ALU.max))
                done(v.tensor_tensor(dt[:], dt[:], t1[:], ALU.add))
                done(v.tensor_tensor(da[:], dt[:], row(1), ALU.mult))
                done(v.tensor_scalar(da[:], da[:], -1.0, None, ALU.mult))
                assert n[0] == 17
                dve.wait_ge(made, 7)
                done(v.tensor_copy(past_r[:], past[:]))
                done(v.tensor_copy(da_hi[:], da[:]))
                done(v.tensor_tensor(da_lo[:], da[:], da_hi[:].bitcast(F32), ALU.subtract))

            @block.scalar
            def _(act):
                a = nc.scalar
                act.wait_ge(prep, 7)
                a.activation(t2[:], t1[:], ACT.Abs).then_inc(prep_act, 1)
                act.wait_ge(prep_act, 1)
                a.activation(t2[:], t2[:], ACT.Exp, scale=-1.0)
                a.activation(rows[:, 1, :], rows[:, 1, :], ACT.Exp).then_inc(prep_act, 1)
                act.wait_ge(prep, 8)
                a.activation(whole[:], grow[:], ACT.Ln).then_inc(prep_act, 1)
                act.wait_ge(prep_pe, 1)
                for n, to in enumerate((grow, fade, whole)):
                    a.activation(to[:].rearrange("p t h -> p (t h)"), bank[n][:, 0:NT * NH], ACT.Exp).then_inc(prep_act, 1)

            @block.tensor
            def _(pe):
                pe.wait_ge(made, 7)
                pe.wait_ge(prep, 17)
                for n, m in enumerate((upto, past, ones)):
                    i = nc.tensor.matmul(bank[n][:, 0:NT * NH], m[:], da[:].rearrange("p t h -> p (t h)"), start=True, stop=True)
                i.then_inc(prep_pe, 1)

        with nc.Block() as block:
            @block.sync
            def _(sp):
                def load(it):
                    row = tile(it) * P if isinstance(it.g, int) else sp.snap(tile(it) * P)
                    sp.wait_ge(proj.sem, proj.at(it.g - 2))
                    Carrier.carry(sp)
                    sp.dma_start(xt[it.s][:].bitcast(F32), xt1[bass.ds(row, P)]).then_inc(x_loaded[it.s], 16)

                def reload(it):
                    row = tile(it) * P if isinstance(it.g, int) else sp.snap(tile(it) * P)
                    sp.wait_ge(summed.sem, summed.at(it.g - 2))
                    Carrier.carry(sp)
                    if pick:
                        sp.wait_ge(expert.sem, expert.at(it.g - 2))
                        Carrier.carry(sp)
                    sp.dma_start(res[it.s][:], res_in_d[bass.ds(row, P), :]).then_inc(r_loaded[it.s], 16)

                def store(it):
                    row = tile(it) * P if isinstance(it.g, int) else sp.snap(tile(it) * P)
                    sp.wait_ge(summed.sem, summed.at(it.g))
                    Carrier.carry(sp)
                    sp.dma_start(res_out_d[bass.ds(row, P), :], out[it.s][:]).then_inc(stored[it.s], 16)

                pipelined(sp, 7, NT, 4, (6, store), (5, reload), (0, load))
                for s in range(2):
                    sp.wait_ge(stored[s], 16 * NT // 2)

            @block.gpsimd
            def _(pool):
                p = nc.gpsimd

                def segments(it):
                    T = tile(it)
                    pool.wait_ge(turn.sem, turn.at(it.g - 2))
                    Carrier.carry(pool)
                    for part, source in ((0, da_hi[:].bitcast(F32)), (1, da_lo[:])):
                        i = p.tensor_tensor(seg[part][it.s][:], source[:, bass.ds(T, 1), :].rearrange("p o h -> p (o h)").unsqueeze(2).to_broadcast([P, NH, P]),
                                            upto[:].unsqueeze(1).to_broadcast([P, NH, P]), ALU.mult)
                    i.then_inc(seg_p.sem, 1)

                def weigh(it):
                    T = tile(it)
                    pool.wait_ge(tok.sem, tok.at(it.g, 1))
                    Carrier.carry(pool)
                    pool.wait_ge(scan.sem, scan.at(it.g - 2))
                    Carrier.carry(pool)
                    p.tensor_tensor(heads(xw[it.s][:]), heads(xdt[it.s][:]),
                                                  fade[:, bass.ds(T, 1), :].rearrange("p o h -> p (o h)").unsqueeze(2).to_broadcast([P, NH, HD]), ALU.mult).then_inc(tok_pool.sem, 1)

                def skips(it):
                    pool.wait_ge(tok_act.sem, tok_act.at(it.g, 1))
                    pool.wait_ge(added.sem, added.at(it.g - 2))
                    p.tensor_tensor(heads(skip[it.s][:]), heads(x_tok[it.s][:]), bc(rows[:, 2, :], HD), ALU.mult).then_inc(tok_pool.sem, 1)

                def add_skip(it):
                    pool.wait_ge(y_dve.sem, y_dve.at(it.g, 2))
                    pool.wait_ge(tok_pool.sem, tok_pool.at(it.g))
                    pool.wait_ge(y_dve.sem, y_dve.at(it.g - 1))
                    p.tensor_tensor(y3[:], y2[:], skip[it.s][:], ALU.add).then_inc(added.sem, 1)

                def fade_state(it):
                    T = tile(it)
                    pool.wait_ge(y_dve.sem, y_dve.at(it.g - 2))
                    Carrier.carry(pool)
                    pool.wait_ge(y_dve.sem, y_dve.at(it.g - BATCH, 3))
                    Carrier.carry(pool)
                    p.tensor_tensor(heads(faded[it.s][:]), heads(state[:, it.lane, :]),
                                                 whole[0:NS, bass.ds(T, 1), :].rearrange("p o h -> p (o h)").unsqueeze(2).to_broadcast([NS, NH, HD]), ALU.mult).then_inc(st_pool.sem, 1)

                def root(it):
                    pool.wait_ge(ms_dve.sem, ms_dve.at(it.g))
                    pool.wait_ge(summed.sem, summed.at(it.g - 2))
                    p.tensor_tensor(rstd[it.s][:], ms[it.s][:], env.neg_half[:, 0:1], ALU.pow).then_inc(ms_pool.sem, 1)

                def index(it):
                    T = tile(it)
                    if it.again:
                        pool.wait_ge(gathered[it.s], it.q * 16)
                        Carrier.carry(pool)
                    p.tensor_copy(at[it.s][:], pick.read[:, bass.ds(T, 1)]).then_inc(indexed.sem, 1)

                def gather(it):
                    pool.wait_ge(indexed.sem, indexed.at(it.g))
                    Carrier.carry(pool)
                    pool.wait_ge(expert.sem, expert.at(it.g - 2))
                    Carrier.carry(pool)
                    pool.indirect_dma_start(got[it.s][:], None, expert_rows[:, :],
                                            bass.IndirectOffsetOnAxis(ap=at[it.s][:, 0:1], axis=0)).then_inc(gathered[it.s], 16)

                experts = [(3, index), (4, gather)] if pick else []
                for stage in (seg_p, tok_pool, added, st_pool, ms_pool, indexed):
                    stage.open(pool)
                pipelined(pool, 7, NT, 4, *experts, (4, fade_state), (4, add_skip), (5, root), (3, weigh), (2, segments), (3, skips))

            @block.vector
            def _(dve):
                v = nc.vector

                def convolve(it):
                    T_u = u[:, it.lane]
                    dve.wait_ge(tapped.sem, tapped.at(it.g))
                    for k in range(1, TAPS):
                        off = HALO - k if backward else k
                        for c in range(CX):
                            i = v.scalar_tensor_tensor(out=cv[it.s][:, c, :], in0=T_u[:, c, off:off + P], scalar=conv[:, c, k:k + 1],
                                                       in1=cv[it.s][:, c, :], op0=ALU.mult, op1=ALU.add)
                        i.then_inc(conved.sem, 1)
                        if k < TAPS - 1:
                            dve.wait_ge(conved.sem, conved.at(it.g, k))

                def steps(it):
                    T = tile(it)
                    dve.wait_ge(tok_act.sem, tok_act.at(it.g, 1))
                    dve.wait_ge(tok_pool.sem, tok_pool.at(it.g - 2))
                    dve.wait_ge(scan.sem, scan.at(it.g - 2))
                    v.tensor_tensor(heads(xdt[it.s][:]), heads(x_tok[it.s][:]), dt[:, bass.ds(T, 1), :].rearrange("p o h -> p (o h)").unsqueeze(2).to_broadcast([P, NH, HD]), ALU.mult).then_inc(tok.sem, 1)

                def mixes(it):
                    dve.wait_ge(turn.sem, turn.at(it.g, 3))
                    dve.wait_ge(scan.sem, scan.at(it.g - 2))
                    v.tensor_copy(b_tok[it.s][:], pBT).then_inc(tok.sem, 1)
                    v.tensor_tensor(gm[:], pG, upto[:], ALU.mult).then_inc(tok.sem, 1)
                    dve.wait_ge(tok.sem, tok.at(it.g, 3))
                    dve.wait_ge(tok_act.sem, tok_act.at(it.g, 2))
                    v.tensor_tensor(mix[it.s][:], decay[:], gm[:].unsqueeze(1).to_broadcast([P, NH, P]), ALU.mult).then_inc(tok.sem, 1)

                def outputs(it):
                    T = tile(it)
                    dve.wait_ge(scan.sem, scan.at(it.g, 1))
                    v.tensor_tensor(heads(y1[:]), heads(pI), grow[:, bass.ds(T, 1), :].rearrange("p o h -> p (o h)").unsqueeze(2).to_broadcast([P, NH, HD]), ALU.mult).then_inc(y_dve.sem, 1)
                    dve.wait_ge(y_dve.sem, y_dve.at(it.g, 1))
                    dve.wait_ge(scan.sem, scan.at(it.g, 2))
                    dve.wait_ge(added.sem, added.at(it.g - 1))
                    v.tensor_tensor(y2[:], pY, y1[:], ALU.add).then_inc(y_dve.sem, 1)

                def new_state(it):
                    dve.wait_ge(scan.sem, scan.at(it.g, 3))
                    dve.wait_ge(st_pool.sem, st_pool.at(it.g))
                    v.tensor_tensor(state[:, it.lane, :], pS, faded[it.s][:], ALU.add).then_inc(y_dve.sem, 1)

                def gated(it):
                    dve.wait_ge(added.sem, added.at(it.g))
                    dve.wait_ge(yturn.sem, yturn.at(it.g - 2))
                    dve.wait_ge(y_act.sem, y_act.at(it.g - 2))
                    v.tensor_tensor(yz[it.s][:], y3[:], gate[it.lane][:], ALU.mult).then_inc(y_dve.sem, 1)

                def mean_square(it):
                    dve.wait_ge(y_act.sem, y_act.at(it.g))
                    dve.wait_ge(ms_pool.sem, ms_pool.at(it.g - 2))
                    v.tensor_scalar(ms[it.s][:], ss[it.s][:], 1.0 / DI, EPS, ALU.mult, ALU.add).then_inc(ms_dve.sem, 1)

                def add_expert(it):
                    T = tile(it)
                    dve.wait_ge(gathered[it.s], it.q * 16 + 16)
                    dve.wait_ge(r_loaded[it.s], it.q * 16 + 16)
                    dve.wait_ge(summed.sem, summed.at(it.g - 2))
                    v.scalar_tensor_tensor(out=sum_e[it.s][:], in0=got[it.s][:], scalar=pick.weight[:, bass.ds(T, 1)],
                                           in1=res[it.s][:], op0=ALU.mult, op1=ALU.add).then_inc(expert.sem, 1)

                def add_out(it):
                    dve.wait_ge(outp.sem, outp.at(it.g))
                    dve.wait_ge(ms_pool.sem, ms_pool.at(it.g))
                    if pick:
                        dve.wait_ge(expert.sem, expert.at(it.g))
                    else:
                        dve.wait_ge(r_loaded[it.s], it.q * 16 + 16)
                    if it.again:
                        dve.wait_ge(stored[it.s], it.q * 16)
                    v.scalar_tensor_tensor(out=out[it.s][:], in0=pO, scalar=rstd[it.s][:], in1=sum_e[it.s][:] if pick else res[it.s][:], op0=ALU.mult, op1=ALU.add).then_inc(summed.sem, 1)

                experts = [(6, add_expert)] if pick else []
                for stage in (conved, tok, y_dve, ms_dve, summed, expert):
                    stage.open(dve)
                pipelined(dve, 7, NT, 4, *experts, (6, add_out), (5, mean_square), (4, outputs), (4, new_state), (4, gated),
                          (3, steps), (3, mixes), (2, convolve))

            @block.scalar
            def _(act):
                a = nc.scalar

                def keep(it):
                    T_u = u[:, it.lane]
                    act.wait_ge(conved.sem, conved.at(it.g - BATCH))
                    act.wait_ge(tapped.sem, tapped.at(it.g - BATCH))
                    frm, to = (slice(0, HALO), slice(P, W)) if backward else (slice(P, W), slice(0, HALO))
                    a.activation(T_u[:, :, to], T_u[:, :, frm], ACT.Copy).then_inc(halo.sem, 1)
                    act.wait_ge(halo.sem, halo.at(it.g, 1))
                    act.wait_ge(proj.sem, proj.at(it.g, 1))
                    a.activation(T_u[:, 0:CC, main], pB0, ACT.Copy)
                    a.activation(T_u[:, CC, main], pB1, ACT.Copy).then_inc(u_kept.sem, 1)

                def tap(it):
                    T_u = u[:, it.lane]
                    off = HALO if backward else 0
                    act.wait_ge(u_kept.sem, u_kept.at(it.g))
                    act.wait_ge(silu.sem, silu.at(it.g - 2))
                    for c in range(CX):
                        i = a.activation(cv[it.s][:, c, :], T_u[:, c, off:off + P], ACT.Identity, bias=conv[:, c, TAPS:TAPS + 1], scale=conv[:, c, 0:1])
                    i.then_inc(tapped.sem, 1)

                def gates(it):
                    act.wait_ge(proj.sem, proj.at(it.g, 2))
                    act.wait_ge(y_dve.sem, y_dve.at(it.g - 4))
                    a.activation(gate[it.lane][:], pZ, ACT.Silu).then_inc(silu_z.sem, 1)

                def activate(it):
                    act.wait_ge(conved.sem, conved.at(it.g))
                    act.wait_ge(turn.sem, turn.at(it.g - 2))
                    act.wait_ge(scan.sem, scan.at(it.g - 2))
                    a.activation(xc[it.s][:], cv[it.s][:, 0:CC, :], ACT.Silu).then_inc(silu.sem, 1)
                    a.activation(bt[it.s][:], cv[it.s][0:NS, CC, :], ACT.Silu).then_inc(silu.sem, 1)
                    a.activation(ct[it.s][:], cv[it.s][NS:P, CC, :], ACT.Silu).then_inc(silu.sem, 1)

                def keep_x(it):
                    act.wait_ge(turn.sem, turn.at(it.g, 2))
                    act.wait_ge(tok_pool.sem, tok_pool.at(it.g - 2))
                    act.wait_ge(tok.sem, tok.at(it.g - 2))
                    a.activation(x_tok[it.s][:], pX, ACT.Copy).then_inc(tok_act.sem, 1)

                def decays(it):
                    act.wait_ge(turn.sem, turn.at(it.g, 1))
                    act.wait_ge(tok.sem, tok.at(it.g - 1))
                    for half in range(2):
                        i = a.activation(decay[:, half * 4:half * 4 + 4, :], pD[half], ACT.Exp)
                    i.then_inc(tok_act.sem, 1)

                def square(it):
                    act.wait_ge(y_dve.sem, y_dve.at(it.g))
                    act.wait_ge(ms_dve.sem, ms_dve.at(it.g - 2))
                    a.activation(sq[:], yz[it.s][:], ACT.Square, accum_out=ss[it.s][:]).then_inc(y_act.sem, 1)

                def keep_turned(it):
                    act.wait_ge(yturn.sem, yturn.at(it.g))
                    act.wait_ge(outp.sem, outp.at(it.g - 2))
                    a.activation(yt[it.s][:], pYT, ACT.Copy).then_inc(y_kept.sem, 1)

                for stage in (u_kept, halo, tapped, silu_z, silu, tok_act, y_act, y_kept):
                    stage.open(act)
                pipelined(act, 7, NT, 4, (5, keep_turned), (3, keep_x), (3, decays), (1, keep), (1, gates), (4, square),
                          (1, tap), (2, activate))

            @block.tensor
            def _(pe):
                t_ = nc.tensor

                def cap(g):
                    return min(g, NT - 1) if isinstance(g, int) else g

                def project_x(it):
                    pe.wait_ge(x_loaded[it.s], it.q * 16 + 16)
                    pe.wait_ge(y_kept.sem, y_kept.at(it.g - 4))
                    pe.wait_ge(y_dve.sem, y_dve.at(it.g - 3, 3))
                    pe.wait_ge(u_kept.sem, u_kept.at(it.g - 1))
                    for c in range(CX):
                        n = 0
                        for k in range(KD):
                            for i, j in PARTS:
                                last = t_.matmul(pB0[:, c, :] if c < CC else pB1, w[i][:, k, DI + c * P:DI + (c + 1) * P],
                                                 xt[it.s][:, j, k, :], start=(n == 0), stop=(n == 5))
                                n += 1
                    last.then_inc(proj.sem, 1)

                def project_z(it):
                    pe.wait_ge(silu_z.sem, silu_z.at(it.g - 1))
                    n = 0
                    for k in range(KD):
                        for i, j in PARTS:
                            last = t_.matmul(pZ, xt[it.s][:, i, k, :], w[j][:, k, 0:DI], start=(n == 0), stop=(n == 5))
                            n += 1
                    last.then_inc(proj.sem, 1)

                def sums(it):
                    pe.wait_ge(seg_p.sem, seg_p.at(it.g))
                    pe.wait_ge(tok_act.sem, tok_act.at(it.g - 1))
                    for half in range(2):
                        for part in range(2):
                            i = t_.matmul(pD[half], past_r[:], seg[part][it.s][:, half * 4:half * 4 + 4, :], start=(part == 0), stop=(part == 1))
                    i.then_inc(turn.sem, 1)

                def turn_tokens(it):
                    pe.wait_ge(silu.sem, silu.at(it.g))
                    pe.wait_ge(tok_act.sem, tok_act.at(it.g - 1))
                    for c in range(CC):
                        i = t_.transpose(pX[:, c * P:(c + 1) * P], xc[it.s][:, c, :], env.ident[:])
                    i.then_inc(turn.sem, 1)
                    pe.wait_ge(summed.sem, summed.at(it.g - 3))
                    pe.wait_ge(tok.sem, tok.at(it.g - 1, 3))
                    t_.matmul(pG, bt[it.s][:], ct[it.s][:], start=True, stop=True)
                    t_.transpose(pBT, bt[it.s][:], env.ident[0:NS, 0:NS]).then_inc(turn.sem, 1)

                def scan_state(it):
                    pe.wait_ge(y_dve.sem, y_dve.at(it.g - BATCH, 3))
                    pe.wait_ge(silu_z.sem, silu_z.at(cap(it.g + 2)))
                    t_.matmul(pI, ct[it.s][:], state[:, it.lane, :], start=True, stop=True).then_inc(scan.sem, 1)

                def scan_tile(it):
                    pe.wait_ge(tok.sem, tok.at(it.g))
                    pe.wait_ge(y_dve.sem, y_dve.at(it.g - 1, 2))
                    for h in range(NH):
                        i = t_.matmul(pY[:, h * HD:(h + 1) * HD], mix[it.s][:, h, :], xdt[it.s][:, h * HD:(h + 1) * HD], start=True, stop=True)
                    i.then_inc(scan.sem, 1)

                def add_tile(it):
                    pe.wait_ge(tok_pool.sem, tok_pool.at(it.g, 1))
                    pe.wait_ge(u_kept.sem, u_kept.at(cap(it.g + 2)))
                    t_.matmul(pS, b_tok[it.s][:], xw[it.s][:], start=True, stop=True).then_inc(scan.sem, 1)

                def turn_y(it):
                    pe.wait_ge(y_dve.sem, y_dve.at(it.g))
                    pe.wait_ge(u_kept.sem, u_kept.at(cap(it.g + 3)))
                    for c in range(CC):
                        i = t_.transpose(pYT[:, c, :], yz[it.s][:, c * P:(c + 1) * P], env.ident[:])
                    i.then_inc(yturn.sem, 1)

                def project_out(it):
                    pe.wait_ge(y_kept.sem, y_kept.at(it.g))
                    pe.wait_ge(summed.sem, summed.at(it.g - 1))
                    pe.wait_ge(tok.sem, tok.at(cap(it.g + 2), 3))
                    for c in range(CC):
                        i = t_.matmul(pO, yt[it.s][:, c, :], ow[:, c, :], start=(c == 0), stop=(c == CC - 1))
                    i.then_inc(outp.sem, 1)

                for stage in (proj, turn, scan, yturn, outp):
                    stage.open(pe)
                pipelined(pe, 7, NT, 4, (6, project_out), (5, turn_y), (4, scan_state), (4, scan_tile), (4, add_tile),
                          (3, sums), (3, turn_tokens), (1, project_x), (1, project_z))


def program(nc, x, attn_w, router_w, cols0, bo_rows, rb_rows, w_fc, w_gate, w_proj, e_cols, e_rows, head_w,
            f_in, f_conv, f_out, f_norm, f_heads, b_in, b_conv, b_out, b_norm, b_heads, w_experts, final):
    NT = T // P
    rows_l0, rows_l1 = E0 * ROWS0, E1 * CAP1

    def dram(name, shape):
        return nc.dram_tensor("dram_" + name, shape, F32, kind="Internal").ap()

    xn0, res0, res1, res2, xn1 = (dram(n, [T, D]) for n in ("xn0", "res0", "res1", "res2", "xn1"))
    xt1 = dram("xt1", [T, 2, KD, P])
    buf0, buf1 = dram("buf0", [rows_l0 + 2 * T, D]), dram("buf1", [rows_l1 + T, D])
    out0, out1 = dram("out0", [rows_l0, D]), dram("out1", [rows_l1, D])

    env = Env(nc)
    with ExitStack() as outer:
        keep = lambda n, s, d=F32: outer.enter_context(nc.sbuf_tensor(n, s, d))
        Carrier.sem = nc.alloc_semaphore("carrier")
        env.ident, env.neg_half = keep("ident", [P, P]), keep("neg_half", [P, 4])
        env.logits = keep("logits0", [P, NT, 8])
        logits1, dt_raw = keep("logits1", [P, NT, E1]), keep("dt_raw", [P, NT, 2 * NH])
        picks0 = [Pick(keep, f"pick0_{k}", NT) for k in range(2)]
        picks1 = [Pick(keep, "pick1", NT)]
        with env.phase(), ExitStack() as ctx:
            setup_l0(nc, env, ctx, attn_w, router_w, cols0, bo_rows, rb_rows)
            tokens_l0(nc, env, x, xn0, res0, ((buf0, rows_l0), (buf1, rows_l1)))
        with env.phase():
            route(nc, env, "r0", env.logits, E0, 2, BATCH, CAP0, ROWS0, rows_l0, picks0)
        with env.phase():
            experts_l0(nc, env, (xn0, picks0), buf0, out0, w_fc, w_gate, w_proj, e_cols, e_rows)
        with env.phase():
            combine_l0(nc, env, out0, picks0, res0, res1, xn1, xt1, head_w, logits1, dt_raw, NT)
        with env.phase():
            route(nc, env, "r1", logits1, E1, 1, 1, CAP1, CAP1, rows_l1, picks1)
        with env.phase():
            experts_l1(nc, env, (xn1, picks1), buf1, out1, w_experts)
        with env.phase():
            mixer(nc, env, "mf", False, f_in, f_conv, f_out, f_norm, f_heads, dt_raw, 0, xt1, res1, res2)
        with env.phase():
            mixer(nc, env, "mb", True, b_in, b_conv, b_out, b_norm, b_heads, dt_raw, NH, xt1, res2, final, out1, picks1[0])


class Env:

    def __init__(self, nc):
        self.nc = nc

    def phase(self):
        return self.nc.cleanup_on_exit()

    def sem(self, name):
        return self.nc.alloc_semaphore(name)



def _laid_out(i):
    import numpy as np

    p0, p1 = "L0_attn_", "L0_ffn_"

    def columns(a):
        return a.reshape(-1, P).T

    out = {
        "x": i[p0 + "x"].reshape(T, D),
        "attn_w": np.stack([i[p0 + n].T for n in ("Wk", "Wq", "Wv", "Wkp", "Wqp", "Wo")]),
        "router_w": i[p1 + "router_w"],
        "cols0": np.concatenate([columns(i[p0 + n]) for n in ("bk", "bq", "bv", "bkp", "bqp", "phase_scale", "ln_g", "ln_b")], 1),
        "bo_rows": np.tile(i[p0 + "bo"], (P, 1)),
        "rb_rows": np.tile(i[p1 + "router_b"], (P, 1)),
        "w_fc": i[p1 + "w_c_fc"], "w_gate": i[p1 + "w_gate"], "w_proj": i[p1 + "w_c_proj"],
        "e_cols": np.concatenate([columns(i[p1 + "b_c_fc"]), columns(i[p1 + "b_gate"])], 1),
        "e_rows": np.tile(i[p1 + "b_c_proj"].reshape(1, -1), (P, 1)),
        "head_w": np.concatenate([i["L1_ffn_w_router"]] + [i[f"L1_attn_{d}_in_w"][-NH:].T for d in "fb"], 1),
    }
    for d in "fb":
        q = f"L1_attn_{d}_"
        conv = np.concatenate([i[q + "conv_w"], i[q + "conv_b"][:, None]], 1)
        out[d + "_in"] = i[q + "in_w"][:-NH].T
        out[d + "_conv"] = conv.reshape(CX, P, TAPS + 1).transpose(1, 0, 2).reshape(P, -1)
        out[d + "_out"] = i[q + "out_w"].T
        out[d + "_norm"] = columns(i[q + "norm_w"])
        out[d + "_heads"] = np.tile(np.concatenate([i[q + n] for n in ("dt_bias", "A_log", "Dp")]), (P, 1))
    out["w_experts"] = np.stack([i["L1_ffn_" + n] for n in ("w_gate", "w_up", "w_down")], 1)
    return {n: np.ascontiguousarray(a) for n, a in out.items()}


def kernel(**inputs):
    import numpy as _np
    import concourse.bacc as _bacc
    from concourse.bass_utils import run_bass_kernel_spmd as _run

    nc = _bacc.Bacc("TRN2", target_bir_lowering=False, num_devices=1)
    laid = _laid_out({n: _np.asarray(a) for n, a in inputs.items()})
    arrays, args = {}, []
    for name, a in laid.items():
        arrays[f"in_{name}"] = a
        args.append(nc.dram_tensor(f"in_{name}", a.shape, mybir.dt.from_np(a.dtype), kind="ExternalInput").ap())
    args.append(nc.dram_tensor("final", (T, D), F32, kind="ExternalOutput").ap())
    program(nc, *args)
    r = _run(nc, [arrays], core_ids=[0])
    return r.results[0]["final"].reshape(BATCH, SEQ, D)
```
